# Optimizing a Trainium2 kernel written in Bass

```python
import numpy as np
import jax
import jax.numpy as jnp

def _softmax(x, axis=-1):
    return jax.nn.softmax(x, axis=axis)

def _gelu(x):
    return jax.nn.gelu(x, approximate=True)

def _silu(x):
    return jax.nn.silu(x)

def _sigmoid(x):
    return jax.nn.sigmoid(x)

def _layernorm(x, axis=-1, eps=1e-05):
    m = jnp.mean(x, axis=axis, keepdims=True)
    v = jnp.var(x, axis=axis, keepdims=True)
    return (x - m) / jnp.sqrt(v + eps)

def _scatter_add(tgt, idx, src, axis=0):
    return tgt.at[idx].add(src)

def _segment_sum(src, seg, n):
    return jax.ops.segment_sum(src, seg, n)
kernel_name = 'mk_gnn_resnorm_d2_gnn_r32_c5f608'

def setup_inputs(seed: int=0):
    np.random.seed(seed)
    _w = jnp.asarray

    def _rec_inputs():
        import jax
        import jax.numpy as jnp
        _gk = jax.random.key(seed)
        x = -0.0002117 + 1 * jax.random.normal(jax.random.fold_in(_gk, 1), (10000, 512), jnp.float32)
        src = jax.random.randint(jax.random.fold_in(_gk, 2), (5000,), 0, 10000, jnp.int32)
        dst = jnp.minimum((10000 * jax.random.uniform(jax.random.fold_in(_gk, 3), (5000,)) ** 2.0).astype(jnp.int32), 9999)
        _o = jnp.argsort(dst, stable=True)
        src = src[_o]
        dst = dst[_o]
        edge_attr_512 = -8.16379e-05 + 0.999858 * jax.random.normal(jax.random.fold_in(_gk, 12), (5000, 512), jnp.float32)
        return (x, src, dst, edge_attr_512)
    x, src, dst, edge_attr_512 = _rec_inputs()

    def _L0_gnn_setup():
        import jax, jax.numpy as jnp
        import numpy as np
        N_NODES = 50000
        EMBED_DIM = 512
        N_EDGES = 25000
        NEG_SLOPE = 0.01
        key = jax.random.key(seed)
        k1, k2, k3 = jax.random.split(key, 3)
        X = jax.random.normal(k1, (N_NODES, EMBED_DIM), dtype=jnp.float32)
        W = jax.random.normal(k2, (EMBED_DIM, EMBED_DIM), dtype=jnp.float32) / np.sqrt(EMBED_DIM)
        b = jnp.zeros((EMBED_DIM,), dtype=jnp.float32)
        edge_index = jax.random.randint(k3, (2, N_EDGES), 0, N_NODES, dtype=jnp.int32)
        return {'X': X, 'W': W, 'b': b, 'edge_index': edge_index}
    _L0_gnn_all = _L0_gnn_setup()
    _L0_gnn_in = {k: v for k, v in _L0_gnn_all.items() if k in ('W', 'b')}
    del _L0_gnn_all

    def _L1_gnn_setup():
        import jax, jax.numpy as jnp
        import numpy as np
        N = 50000
        E = 6250
        IN = 512
        H = 8
        D = 64
        EPS = 1e-05

        def _xavier(k, out_f, in_f):
            std = float(np.sqrt(2.0 / (in_f + out_f)))
            return jax.random.normal(k, (out_f, in_f), dtype=jnp.float32) * std
        key = jax.random.key(seed)
        ks = jax.random.split(key, 10)
        z = jnp.zeros((H * D,), jnp.float32)
        return {'node_feat': jax.random.normal(ks[0], (N, IN), dtype=jnp.float32), 'edge_feat': jax.random.normal(ks[1], (E, IN), dtype=jnp.float32), 'src': jax.random.randint(ks[2], (E,), 0, N), 'dst': jax.random.randint(ks[3], (E,), 0, N), 'Wq': _xavier(ks[4], H * D, IN), 'bq': z, 'Wr': _xavier(ks[5], H * D, 3 * IN), 'br': z, 'Wk': _xavier(ks[6], H * D, H * D), 'bk': z, 'Wv': _xavier(ks[7], H * D, H * D), 'bv': z, 'Wo': _xavier(ks[8], H * D, H * D), 'bo': z, 'gamma': jnp.ones((IN,), jnp.float32), 'beta': jnp.zeros((IN,), jnp.float32)}
    _L1_gnn_all = _L1_gnn_setup()
    _L1_gnn_in = {k: v for k, v in _L1_gnn_all.items() if k in ('Wq', 'bq', 'Wr', 'br', 'Wk', 'bk', 'Wv', 'bv', 'Wo', 'bo', 'gamma', 'beta')}
    del _L1_gnn_all
    return {'x': x, 'src': src, 'dst': dst, 'edge_attr_512': edge_attr_512, 'L0_gnn_W': _L0_gnn_in['W'], 'L0_gnn_b': _L0_gnn_in['b'], 'L1_gnn_Wq': _L1_gnn_in['Wq'], 'L1_gnn_bq': _L1_gnn_in['bq'], 'L1_gnn_Wr': _L1_gnn_in['Wr'], 'L1_gnn_br': _L1_gnn_in['br'], 'L1_gnn_Wk': _L1_gnn_in['Wk'], 'L1_gnn_bk': _L1_gnn_in['bk'], 'L1_gnn_Wv': _L1_gnn_in['Wv'], 'L1_gnn_bv': _L1_gnn_in['bv'], 'L1_gnn_Wo': _L1_gnn_in['Wo'], 'L1_gnn_bo': _L1_gnn_in['bo'], 'L1_gnn_gamma': _L1_gnn_in['gamma'], 'L1_gnn_beta': _L1_gnn_in['beta']}

def reference(x, src, dst, edge_attr_512, L0_gnn_W, L0_gnn_b, L1_gnn_Wq, L1_gnn_bq, L1_gnn_Wr, L1_gnn_br, L1_gnn_Wk, L1_gnn_bk, L1_gnn_Wv, L1_gnn_bv, L1_gnn_Wo, L1_gnn_bo, L1_gnn_gamma, L1_gnn_beta):
    import jax
    import jax.numpy as jnp

    def _L0_gnn_ref(X, W, b, edge_index):
        import jax, jax.numpy as jnp
        import numpy as np
        N_NODES = 50000
        EMBED_DIM = 512
        N_EDGES = 25000
        NEG_SLOPE = 0.01
        N = X.shape[0]
        loop = jnp.arange(N, dtype=edge_index.dtype)
        src = jnp.concatenate([edge_index[0], loop])
        dst = jnp.concatenate([edge_index[1], loop])
        deg = jax.ops.segment_sum(jnp.ones_like(dst, dtype=X.dtype), dst, num_segments=N)
        dinv = jnp.where(deg > 0, jax.lax.rsqrt(deg), 0.0)
        norm = dinv[src] * dinv[dst]
        H = X @ W
        msgs = H[src] * norm[:, None]
        out = jax.ops.segment_sum(msgs, dst, num_segments=N) + b
        return jnp.where(out >= 0, out, NEG_SLOPE * out)

    def _L1_gnn_ref(node_feat, edge_feat, src, dst, Wq, bq, Wr, br, Wk, bk, Wv, bv, Wo, bo, gamma, beta):
        import jax, jax.numpy as jnp
        import numpy as np
        N = 50000
        E = 6250
        IN = 512
        H = 8
        D = 64
        EPS = 1e-05

        def _xavier(k, out_f, in_f):
            std = float(np.sqrt(2.0 / (in_f + out_f)))
            return jax.random.normal(k, (out_f, in_f), dtype=jnp.float32) * std
        n = node_feat.shape[0]
        e = edge_feat.shape[0]
        scaler = 1.0 / np.sqrt(D)
        x_cat = jnp.concatenate([node_feat[src], node_feat[dst], edge_feat], axis=-1)
        r = x_cat @ Wr.T + br
        q = (node_feat @ Wq.T + bq).reshape(n, H, D)
        k = (r @ Wk.T + bk).reshape(e, H, D)
        v = (r @ Wv.T + bv).reshape(e, H, D)
        a = jnp.einsum('ehd,ehd->eh', q[dst], k) * scaler
        amax = jax.ops.segment_max(a, dst, num_segments=n)
        ae = jnp.exp(a - amax[dst])
        asum = jax.ops.segment_sum(ae, dst, num_segments=n)
        attn = ae / asum[dst]
        m = v * attn[..., None]
        out = jax.ops.segment_sum(m, dst, num_segments=n).reshape(n, H * D)
        out = out @ Wo.T + bo
        out = node_feat + out
        mean = out.mean(axis=0)
        var = jnp.mean(jnp.square(out - mean), axis=0)
        out = (out - mean) * jax.lax.rsqrt(var + EPS) * gamma + beta
        return out
    edge_index = jnp.stack([src, dst])
    x = _layernorm(x + _L0_gnn_ref(x, L0_gnn_W, L0_gnn_b, edge_index), axis=-1)
    x = _layernorm(x + _L1_gnn_ref(x, edge_attr_512, src, dst, L1_gnn_Wq, L1_gnn_bq, L1_gnn_Wr, L1_gnn_br, L1_gnn_Wk, L1_gnn_bk, L1_gnn_Wv, L1_gnn_bv, L1_gnn_Wo, L1_gnn_bo, L1_gnn_gamma, L1_gnn_beta), axis=-1)
    return x

_drawn_inputs = setup_inputs


def setup_inputs(seed=0):
    import zlib

    import numpy as np

    out = dict(_drawn_inputs(seed))
    spreads = {'L0_gnn_b': (0.0, 0.1),
     'L1_gnn_bq': (0.0, 0.8),
     'L1_gnn_br': (0.0, 0.415),
     'L1_gnn_bk': (0.0, 0.8),
     'L1_gnn_bv': (0.0, 0.412),
     'L1_gnn_bo': (0.0, 0.8),
     'L1_gnn_gamma': (1.0, 0.2),
     'L1_gnn_beta': (0.0, 0.1)}
    factors = {}
    for name, (base, spread) in spreads.items():
        noise = np.random.default_rng([zlib.crc32(name.encode()), seed]).standard_normal(out[name].shape)
        drawn = base * np.exp(spread * noise) if base else spread * noise
        out[name] = jnp.asarray(drawn.astype(out[name].dtype))
    for name, factor in factors.items():
        out[name] = (out[name] * factor).astype(out[name].dtype)
    return out
```

```python
from contextlib import ExitStack

import concourse.bass as bass
from concourse import mybir

F32 = mybir.dt.float32
F32R = mybir.dt.float32r
BF16 = mybir.dt.bfloat16
I32 = mybir.dt.int32
ALU = mybir.AluOpType
ACT = mybir.ActivationFunctionType
AX = mybir.AxisListType

P = 128
N = 10000
E = 5000
D = 512
H = 8
K = D // P
NT = -(-N // P)
NP = NT * P
ET = -(-E // P)
EP = ET * P
BE = 2 * P
NB = EP // BE
LAST = N - (NT - 1) * P
BITS = 7
EPS = 1e-5
NEG_SLOPE = 0.01
START = -1e30
W0, WR_EDGE, WR_SRC, WR_DST, WQ, WK, WV, WO = range(8)
NW = 8


def wait(eng, sem, count):
    if isinstance(count, int) and count <= 0:
        return
    eng.wait_ge(sem, count)


def wait_alone(eng, sem, count, passed):
    eng.wait_ge(sem, count)
    eng.sem_inc(passed, 1)


def sweep(eng, n, lag, unroll, head, step):
    rounds = (n - head) // unroll
    for j in range(head):
        step(j, j % unroll, lambda k, j=j: 0 <= j - k < n)
    with eng.Fori(0, rounds) as i:
        for s in range(unroll):
            step(i * unroll + (head + s), s, lambda k: True)
    for j in range(head + rounds * unroll, n + lag):
        step(j, j % unroll, lambda k, j=j: 0 <= j - k < n)


class Shared:
    pass


def gnn_kernel(nc, x, dst_in, src_in, eid_in, ea, weights, br, bv, rows, out):

    g = Shared()
    g.x, g.dst_in, g.src_in, g.eid_in, g.ea, g.weights = x, dst_in, src_in, eid_in, ea, weights
    g.br, g.bv, g.rows, g.out = br, bv, rows, out

    def dram(name, shape, dt):
        return nc.dram_tensor(name, shape, dt, kind="Internal").ap()

    g.sdst = dram("sorted_dst", [EP + P, 1], I32)
    g.ssrc = dram("sorted_src", [EP + P, 1], I32)
    g.seid = dram("sorted_edge", [EP + P, 1], I32)
    g.dinv_table = dram("dinv_table", [NP, 1], F32)
    g.goes_row = dram("goes_row", [1, EP], BF16)
    g.edge_part = dram("edge_part", [NB, P, K * BE], F32)
    g.sum_table = dram("sum_table", [EP + P, D], F32)
    g.x1_table = dram("x1_table", [NP, D], F32)
    g.coef_table = dram("coef_table", [NB, H, 2 * BE], F32)
    g.msg_table = dram("msg_table", [EP + P, D], F32)

    with ExitStack() as whole:

        def sem(name, ctx=whole):
            return ctx.enter_context(nc.semaphore(name))

        def sb(ctx, name, shape, dt=F32):
            return ctx.enter_context(nc.sbuf_tensor(name, shape, dt))

        def banks(ctx, name, n=8):
            return [ctx.enter_context(nc.psum_tensor(f"{name}{i}", [P, 512], F32)) for i in range(n)]

        g.passed = sem("wait_passed")
        g.w_hi = sb(whole, "w_hi", [P, NW, K * D], F32R)
        g.w_lo = sb(whole, "w_lo", [P, NW, K * D], F32R)
        g.ident = sb(whole, "ident", [P, P])
        g.ones = sb(whole, "ones", [P, P])
        g.eps = sb(whole, "eps", [P, 1])
        g.dinv = sb(whole, "dinv", [P, NT])
        g.last_edge = sb(whole, "last_edge", [P, NT], I32)
        g.edge_idx = sb(whole, "edge_idx", [P, ET, 4], I32)
        g.is_last = sb(whole, "is_last", [P, ET])
        g.br_col = sb(whole, "br_col", [P, K])
        g.bv_col = sb(whole, "bv_col", [P, K])
        g.acc_x = sb(whole, "acc_x", [P, D])
        g.acc_xx = sb(whole, "acc_xx", [P, D])
        g.sum_y = sb(whole, "sum_y", [P, D])
        g.sum_yy = sb(whole, "sum_yy", [P, D])

        def w(half, slot, k, lo=0, n=D):
            return half[:, slot, k * D + lo:k * D + lo + n]

        def product(pe, to, left, right, first, last):
            pe.matmul(to, left[0], right[1], start=first, stop=False)
            pe.matmul(to, left[1], right[0], start=False, stop=False)
            return pe.matmul(to, left[0], right[0], start=False, stop=last)

        with ExitStack() as early:
            g.goes_on = sb(early, "goes_on", [P, EP], BF16)
            g.sb, g.sem, g.banks, g.w, g.product = sb, sem, banks, w, product
            index_stage(nc, g)
            aggregate_stage(nc, g)
        node_stage(nc, g)
        edge_stage(nc, g)
        finish_stage(nc, g)


def index_stage(nc, g):
    sb, sem = g.sb, g.sem
    with ExitStack() as ctx:
        flat = sb(ctx, "flat_check", [ET, 2, P], I32)
        worse = sb(ctx, "worse", [ET, P])
        worse_row = sb(ctx, "worse_row", [ET, 1])
        unsorted_i = sb(ctx, "unsorted", [1, 1], I32)
        w_stage = sb(ctx, "w_stage", [P, 2, K * D // 2])
        dst_row = sb(ctx, "dst_row", [P, 1 + EP], I32)
        iota_row = sb(ctx, "iota_row", [P, P], I32)
        upper = sb(ctx, "upper", [P, P])
        none_at = sb(ctx, "none_at", [P, NT])
        zero = sb(ctx, "zero_rows", [P, D])
        counting = ctx.enter_context(ExitStack())
        place_row = sb(counting, "place_row", [P, EP], mybir.dt.int16)
        one_row = g.goes_on
        cols = sb(counting, "cols", [P, 3, ET], I32)
        cols_f = sb(counting, "cols_f", [P, 3, ET])
        less = sb(counting, "less", [P, 2, ET])
        rank = sb(counting, "rank", [P, ET], I32)
        put = sb(counting, "put", [P, 4], I32)
        counting.close()
        flat_s = sb(ctx, "flat_sorted", [ET, 4, P], I32)
        flat_f = sb(ctx, "flat_float", [ET, 4, P])
        cols_s = sb(ctx, "cols_sorted", [P, 4, ET], I32)
        low = sb(ctx, "node_low", [P, 2, ET], I32)
        high = sb(ctx, "node_high", [P, 2, ET], I32)
        hot_low = sb(ctx, "hot_low", [P, ET, P], BF16)
        hot_high = sb(ctx, "hot_high", [P, ET, NT], BF16)
        cnt = sb(ctx, "cnt", [P, NT])
        small = sb(ctx, "small", [P, 8, NT])
        differs = sb(ctx, "differs", [P, ET])
        ps = g.banks(ctx, "psi")

        copied, checked_in = sem("tables_copied"), sem("check_loaded")
        worse_ok, flag_ps, flag_ok = sem("worse_summed"), sem("flag_in_psum"), sem("flag_ready")
        count_in, counted, rank_ok, put_ok, put_out = (sem(n) for n in ("count_loaded", "counted", "rank_ready", "put_staged", "put_written"))
        ordered, flat_in, row_in = sem("edges_ordered"), sem("flat_loaded"), sem("row_loaded")
        const_ok, const_in = sem("constants_made"), sem("constants_loaded")
        flat_ok, cols_ok, hot_ok = sem("flat_as_float"), sem("columns_in_psum"), sem("one_hots_ready")
        hist_ok, cnt_ok, cum_ok, root_ok = (sem(n) for n in ("histogram_in_psum", "count_ready", "prefix_in_psum", "root_ready"))
        dinv_ok, start_ok, stored = sem("dinv_ready"), sem("start_ready"), sem("index_stored")
        w_in = [sem(f"weights_loaded{s}") for s in range(2)]
        w_hi_ok, w_lo_ok = sem("weights_high"), sem("weights_low")
        step_v, step_p = sem("vector_step"), sem("pool_step")
        zero_ok = sem("zero_rows_made")

        def w_half(to, i):
            return to[:, i // 2, (i % 2) * K * D // 2:(i % 2 + 1) * K * D // 2]

        with nc.Block() as block:

            @block.sync
            def _(sp):
                for i in range(2):
                    sp.dma_start(flat[:, i, :], g.dst_in[i:i + EP, :].rearrange("(t p) c -> t (p c)", p=P)).then_inc(checked_in, 16)
                for to, of in ((g.sdst, g.dst_in), (g.ssrc, g.src_in), (g.seid, g.eid_in)):
                    sp.dma_start(to.rearrange("(a b) c -> a (b c)", a=16), of.rearrange("(a b) c -> a (b c)", a=16)).then_inc(copied, 16)
                sp.dma_start(g.br_col[:], g.br.rearrange("(k p) -> p k", p=P), allow_slow_non_contiguous=True).then_inc(const_in, 16)
                sp.dma_start(g.bv_col[:], g.bv.rearrange("(k p) -> p k", p=P), allow_slow_non_contiguous=True).then_inc(const_in, 16)
                sp.wait_ge(zero_ok, 1)
                sp.dma_start(g.sum_table[EP:EP + P, :], zero[:]).then_inc(stored, 16)
                sp.dma_start(g.msg_table[EP:EP + P, :], zero[:]).then_inc(stored, 16)
                sp.wait_ge(copied, 48)
                sp.wait_ge(ordered, 1)
                for i, (of, o) in enumerate(((g.sdst, 0), (g.ssrc, 0), (g.seid, 0), (g.sdst, 1))):
                    sp.dma_start(flat_s[:, i, :], of[o:o + EP, :].rearrange("(t p) c -> t (p c)", p=P)).then_inc(flat_in, 16)
                sp.dma_start(dst_row[:, 1:], g.sdst[0:EP, :].rearrange("e c -> (e c)").unsqueeze(0).to_broadcast([P, EP])).then_inc(row_in, 16)
                sp.wait_ge(dinv_ok, 1)
                sp.dma_start(g.dinv_table.rearrange("(p j) c -> p (j c)", p=P), g.dinv[:]).then_inc(stored, 16)
                sp.wait_ge(start_ok, 1)
                sp.dma_start(g.goes_row, g.goes_on[0:1, :]).then_inc(stored, 16)
                sp.wait_ge(const_in, 32)
                sp.wait_ge(stored, 64)

            @block.scalar
            def _(act):
                def load(i, s):
                    rows = g.weights[bass.ds(i * (D // 2), D // 2), :]
                    act.dma_start(w_stage[:, s, :].rearrange("p (k n) -> p k n", k=K // 2), rows.rearrange("(k p) n -> p k n", p=P)).then_inc(w_in[s], 16)

                load(0, 0)
                load(1, 1)
                for i in range(2 * NW):
                    s = i % 2
                    act.wait_ge(w_in[s], 16 * (i // 2 + 1))
                    nc.scalar.copy(w_half(g.w_hi, i), w_stage[:, s, :]).then_inc(w_hi_ok, 1)
                    if i + 2 < 2 * NW:
                        act.wait_ge(w_lo_ok, i + 1)
                        load(i + 2, s)
                    if i == 4:
                        act.wait_ge(cnt_ok, 1)
                        act.wait_ge(const_ok, 2)
                        nc.scalar.activation(small[:, 0, :], cnt[:], ACT.Sqrt, bias=g.ones[:, 0:1]).then_inc(root_ok, 1)

            @block.gpsimd
            def _(pool):
                steps = [0]

                def then(ins):
                    steps[0] += 1
                    ins.then_inc(step_p, 1)
                    pool.wait_ge(step_p, steps[0])

                then(nc.gpsimd.memset(g.ones[:], 1.0))
                nc.gpsimd.memset(g.eps[:], EPS).then_inc(const_ok, 1)
                nc.gpsimd.affine_select(out=g.ident[:], in_=g.ones[:], compare_op=ALU.is_equal, fill=0.0, base=0, pattern=[[-1, P]], channel_multiplier=1).then_inc(const_ok, 1)
                nc.gpsimd.affine_select(out=upper[:], in_=g.ones[:], compare_op=ALU.is_ge, fill=0.0, base=0, pattern=[[1, P]], channel_multiplier=-1).then_inc(const_ok, 1)
                nc.gpsimd.iota(iota_row[:], [[1, P]], base=0, channel_multiplier=0).then_inc(const_ok, 1)
                nc.gpsimd.iota(none_at[:], [[0, NT]], base=EP, channel_multiplier=1, allow_small_or_imprecise_dtypes=True).then_inc(const_ok, 1)
                nc.gpsimd.memset(zero[:], 0.0).then_inc(zero_ok, 1)
                nc.gpsimd.memset(g.acc_x[:], 0.0).then_inc(const_ok, 1)
                nc.gpsimd.memset(g.acc_xx[:], 0.0).then_inc(const_ok, 1)
                nc.gpsimd.memset(g.sum_y[:], 0.0).then_inc(const_ok, 1)
                nc.gpsimd.memset(g.sum_yy[:], 0.0).then_inc(const_ok, 1)
                pool.wait_ge(flag_ok, 1)
                flag = pool.value_load(unsorted_i[0:1, 0:1], min_val=0, max_val=EP)
                with pool.If(flag > 0):
                    pool.wait_ge(copied, 48)
                    nc.gpsimd.dma_start(dst_row[:, 1:], g.dst_in[0:EP, :].rearrange("e c -> (e c)").unsqueeze(0).to_broadcast([P, EP])).then_inc(count_in, 16)
                    for i, of in enumerate((g.dst_in, g.src_in, g.eid_in)):
                        nc.gpsimd.dma_start(cols[:, i, :], of[0:EP, :].rearrange("(t p) c -> p (t c)", p=P), allow_slow_non_contiguous=True).then_inc(count_in, 16)
                    nc.gpsimd.iota(place_row[:], [[1, EP]], base=0, channel_multiplier=0, allow_small_or_imprecise_dtypes=True).then_inc(counted, 1)
                    pool.wait_ge(rank_ok, 1)
                    with pool.Fori(0, ET) as t:
                        nc.gpsimd.tensor_copy(put[:, 0:3], cols[:, :, bass.ds(t, 1)].rearrange("p c t -> p (c t)")).then_inc(put_ok, 1)
                        nc.gpsimd.tensor_copy(put[:, 3:4], rank[:, bass.ds(t, 1)]).then_inc(put_ok, 1)
                        wait_alone(pool, put_ok, 2 * t + 2, g.passed)
                        for i, to in enumerate((g.sdst, g.ssrc, g.seid)):
                            nc.gpsimd.indirect_dma_start(out=to, out_offset=bass.IndirectOffsetOnAxis(ap=put[:, 3:4], axis=0), in_=put[:, i:i + 1], in_offset=None).then_inc(put_out, 16)
                        pool.wait_ge(put_out, 48 * t + 48)
                nc.gpsimd.engine_nop().then_inc(ordered, 1)
                for i in range(2 * NW):
                    pool.wait_ge(w_hi_ok, i + 1)
                    nc.gpsimd.tensor_tensor(w_half(g.w_lo, i), w_stage[:, i % 2, :], w_half(g.w_hi, i).bitcast(F32), ALU.subtract).then_inc(w_lo_ok, 1)

            @block.tensor
            def _(pe):
                pe.wait_ge(const_ok, 9)
                pe.wait_ge(worse_ok, 2)
                pe.matmul(ps[0][0:1, 0:1], worse_row[:], g.ones[0:ET, 0:1], start=True, stop=True).then_inc(flag_ps, 1)
                pe.wait_ge(flat_ok, 1)
                for i in range(4):
                    pe.transpose(ps[1][:, i * ET:(i + 1) * ET], flat_f[:, i, :], g.ident[0:ET, 0:ET]).then_inc(cols_ok, 1)
                pe.wait_ge(hot_ok, 2)
                for t in range(ET):
                    mm = pe.matmul(ps[2][:, 0:NT], hot_low[:, t, :], hot_high[:, t, :], start=t == 0, stop=t == ET - 1)
                mm.then_inc(hist_ok, 1)
                pe.wait_ge(cnt_ok, 1)
                pe.matmul(ps[3][:, 0:NT], upper[:], cnt[:], start=True, stop=True).then_inc(cum_ok, 1)
                pe.matmul(ps[4][:, 0:NT], g.ones[:], cnt[:], start=True, stop=True).then_inc(cum_ok, 1)

            @block.vector
            def _(dve):
                steps = [0]

                def then(ins):
                    steps[0] += 1
                    ins.then_inc(step_v, 1)
                    dve.wait_ge(step_v, steps[0])

                v = nc.vector
                dve.wait_ge(checked_in, 32)
                v.tensor_tensor(worse[:], flat[:, 0, :], flat[:, 1, :], ALU.is_gt).then_inc(worse_ok, 1)
                dve.wait_ge(worse_ok, 1)
                v.tensor_reduce(worse_row[:], worse[:], AX.X, ALU.add).then_inc(worse_ok, 1)
                dve.wait_ge(flag_ps, 1)
                v.tensor_copy(unsorted_i[:], ps[0][0:1, 0:1]).then_inc(flag_ok, 1)
                dve.wait_ge(flag_ok, 1)
                flag = dve.value_load(unsorted_i[0:1, 0:1], min_val=0, max_val=EP)
                with dve.If(flag > 0):
                    dve.wait_ge(count_in, 64)
                    dve.wait_ge(counted, 1)
                    v.tensor_copy(cols_f[:], cols[:]).then_inc(counted, 1)
                    dve.wait_ge(counted, 2)
                    with dve.Fori(0, ET) as t:
                        v.tensor_scalar(one_row[:], dst_row[:, 1:], cols_f[:, 0, bass.ds(t, 1)], 0.0, ALU.is_lt, ALU.add,
                                        accum_out=less[:, 0, bass.ds(t, 1)]).then_inc(counted, 1)
                        dve.wait_ge(counted, 3 * t + 3)
                        v.tensor_scalar(one_row[:], dst_row[:, 1:], cols_f[:, 0, bass.ds(t, 1)], None, ALU.is_equal).then_inc(counted, 1)
                        dve.wait_ge(counted, 3 * t + 4)
                        v.scalar_tensor_tensor(one_row[:], place_row[:], cols_f[:, 2, bass.ds(t, 1)], one_row[:], ALU.is_lt, ALU.mult,
                                               accum_out=less[:, 1, bass.ds(t, 1)]).then_inc(counted, 1)
                        dve.wait_ge(counted, 3 * t + 5)
                    v.tensor_tensor(rank[:], less[:, 0, :], less[:, 1, :], ALU.add).then_inc(rank_ok, 1)
                dve.wait_ge(flat_in, 64)
                v.tensor_copy(flat_f[:], flat_s[:]).then_inc(flat_ok, 1)
                dve.wait_ge(cols_ok, 4)
                then(v.tensor_copy(cols_s[:], ps[1][:, 0:4 * ET].rearrange("p (c t) -> p c t", c=4)))
                v.tensor_tensor(differs[:], cols_s[:, 0, :], cols_s[:, 3, :], ALU.not_equal)
                v.tensor_scalar(high[:], cols_s[:, 0:2, :], BITS, None, ALU.logical_shift_right)
                then(v.tensor_scalar(low[:], cols_s[:, 0:2, :], P - 1, None, ALU.bitwise_and))
                dve.wait_ge(const_ok, 9)
                v.tensor_tensor(hot_low[:], iota_row[:].unsqueeze(1).to_broadcast([P, ET, P]),
                                low[:, 0, :].unsqueeze(2).to_broadcast([P, ET, P]), ALU.is_equal).then_inc(hot_ok, 1)
                v.tensor_tensor(hot_high[:], iota_row[:, 0:NT].unsqueeze(1).to_broadcast([P, ET, NT]),
                                high[:, 0, :].unsqueeze(2).to_broadcast([P, ET, NT]), ALU.is_equal).then_inc(hot_ok, 1)
                v.scalar_tensor_tensor(g.is_last[:], cols_s[:, 0, :], float(N), differs[:], ALU.is_lt, ALU.mult)
                v.tensor_copy(g.edge_idx[:, :, 0], cols_s[:, 2, :])
                v.tensor_copy(g.edge_idx[:, :, 1], cols_s[:, 1, :])
                v.scalar_tensor_tensor(g.edge_idx[:, :, 2], low[:, 1, :], float(NT), high[:, 1, :], ALU.mult, ALU.add)
                v.tensor_copy(g.edge_idx[:, :, 3], cols_s[:, 0, :])
                dve.wait_ge(hist_ok, 1)
                v.tensor_copy(cnt[:], ps[2][:, 0:NT]).then_inc(cnt_ok, 1)
                then(v.memset(dst_row[:, 0:1], -1))
                dve.wait_ge(row_in, 16)
                v.tensor_tensor(g.goes_on[:], dst_row[:, 1:], dst_row[:, 0:EP], ALU.is_equal).then_inc(start_ok, 1)
                deg, y, t = small[:, 1, :], small[:, 2, :], small[:, 3, :]
                v.tensor_scalar(deg, cnt[:], 1.0, None, ALU.add)
                dve.wait_ge(root_ok, 1)
                then(v.reciprocal(y, small[:, 0, :]))
                then(v.tensor_tensor(t, y, y, ALU.mult))
                then(v.tensor_tensor(t, t, deg, ALU.mult))
                then(v.tensor_scalar(t, t, -0.5, 1.5, ALU.mult, ALU.add))
                v.tensor_tensor(g.dinv[:], y, t, ALU.mult).then_inc(dinv_ok, 1)
                dve.wait_ge(cum_ok, 2)
                a, b, c, e = (small[:, i, :] for i in range(4, 8))
                then(v.tensor_tensor_scan(a, g.ones[:, 0:NT], ps[4][:, 0:NT], 0.0, ALU.mult, ALU.add))
                then(v.tensor_tensor(b, a, ps[4][:, 0:NT], ALU.subtract))
                then(v.scalar_tensor_tensor(c, ps[3][:, 0:NT], -1.0, b, ALU.add, ALU.add))
                then(v.tensor_tensor(e, none_at[:], c, ALU.subtract))
                then(v.scalar_tensor_tensor(e, cnt[:], 0.0, e, ALU.is_equal, ALU.mult))
                then(v.tensor_tensor(g.last_edge[:], c, e, ALU.add))


def aggregate_stage(nc, g):
    sb, sem = g.sb, g.sem
    with ExitStack() as ctx:
        idx = sb(ctx, "agg_idx", [P, 2, 3], I32)
        ea_rows = sb(ctx, "ea_rows", [P, 2, D])
        x_rows = sb(ctx, "x_rows", [P, 2, D])
        scaled = sb(ctx, "scaled_rows", [P, 2, D])
        dinv_src = sb(ctx, "dinv_src", [P, 2, 1])
        ea_hi = sb(ctx, "ea_hi", [P, K, BE], F32R)
        ea_lo = sb(ctx, "ea_lo", [P, K, BE], F32R)
        run = sb(ctx, "run", [P, 2, K, P])
        sums = sb(ctx, "sums", [P, 2, D])
        part = sb(ctx, "part", [P, K, BE])
        ps = g.banks(ctx, "psa")
        ps_ea, ps_x, ps_back, ps_r = ps[0:2], ps[2:4], ps[4], ps[5:7]

        idx_ok = sem("agg_idx_staged")
        ea_in = [sem(f"ea_rows_in{s}") for s in range(2)]
        x_in = [sem(f"x_rows_in{s}") for s in range(2)]
        dinv_in = [sem(f"dinv_src_in{s}") for s in range(2)]
        scaled_ok, ea_t, x_t = sem("rows_scaled"), sem("ea_transposed"), sem("x_transposed")
        ea_hi_ok, ea_lo_ok, scan_ok, back_ok = (sem(n) for n in ("ea_high", "ea_low", "rows_summed", "sums_turned"))
        row_ok, row_out = sem("sum_rows_ready"), [sem(f"sum_rows_out{s}") for s in range(2)]
        r_mm, part_ok, part_out = sem("edge_part_in_psum"), sem("edge_part_ready"), sem("edge_part_out")

        with nc.Block() as block:

            @block.gpsimd
            def _(pool):
                def step(t, s, on):
                    wait(pool, ea_t, t - 1)
                    wait(pool, scaled_ok, t - 1)
                    nc.gpsimd.tensor_copy(idx[:, s, :], g.edge_idx[:, bass.ds(t, 1), 0:3].rearrange("p t c -> p (t c)")).then_inc(idx_ok, 1)
                    wait_alone(pool, idx_ok, t + 1, g.passed)
                    for i, (to, of, n) in enumerate(((ea_rows, g.ea, ea_in), (x_rows, g.x, x_in), (dinv_src, g.dinv_table, dinv_in))):
                        nc.gpsimd.indirect_dma_start(out=to[:, s, :], out_offset=None, in_=of, in_offset=bass.IndirectOffsetOnAxis(ap=idx[:, s, i:i + 1], axis=0)).then_inc(n[s], 16)
                sweep(pool, ET, 0, 2, 2, step)

            @block.scalar
            def _(act):
                def tile(b, s):
                    t = b * 2 + s
                    act.wait_ge(x_in[s], 16 * b + 16)
                    act.wait_ge(dinv_in[s], 16 * b + 16)
                    wait(act, x_t, t)
                    nc.scalar.activation(scaled[:, s, :], x_rows[:, s, :], ACT.Copy, scale=dinv_src[:, s, :]).then_inc(scaled_ok, 1)
                    act.wait_ge(ea_t, t + 1)
                    wait(act, r_mm, b)
                    nc.scalar.copy(ea_hi[:, :, s * P:(s + 1) * P], ps_ea[s][:].rearrange("p (k e) -> p k e", k=K)).then_inc(ea_hi_ok, 1)

                def back(b, s):
                    act.wait_ge(back_ok, b * 2 + s + 1)
                    wait(act, row_out[s], 16 * b)
                    nc.scalar.copy(sums[:, s, :], ps_back[:]).then_inc(row_ok, 1)

                def step(b):
                    tile(b, 0)
                    tile(b, 1)
                    back(b, 0)
                    act.wait_ge(r_mm, b + 1)
                    wait(act, part_out, 16 * b)
                    for m in range(K):
                        nc.scalar.activation(part[:, m, :], ps_r[m // 2][:, (m % 2) * BE:(m % 2 + 1) * BE], ACT.Identity, bias=g.br_col[:, m:m + 1]).then_inc(part_ok, 1)
                    back(b, 1)
                step(0)
                with act.Fori(1, NB) as b:
                    step(b)

            @block.vector
            def _(dve):
                v = nc.vector

                def step(b):
                    for s in range(2):
                        t = b * 2 + s
                        dve.wait_ge(ea_hi_ok, t + 1)
                        v.tensor_tensor(ea_lo[:, :, s * P:(s + 1) * P], ps_ea[s][:].rearrange("p (k e) -> p k e", k=K),
                                        ea_hi[:, :, s * P:(s + 1) * P].bitcast(F32), ALU.subtract).then_inc(ea_lo_ok, 1)
                        dve.wait_ge(x_t, t + 1)
                        wait(dve, scan_ok, K * t)
                        wait(dve, back_ok, t - 1)
                        for k in range(K):
                            before = run[:, 1 - s, k, P - 1:P]
                            if isinstance(t, int) and t == 0:
                                before = 0.0
                            v.tensor_tensor_scan(run[:, s, k, :], g.goes_on[:, bass.ds(t * P, P)], ps_x[s][:, k * P:(k + 1) * P],
                                                 before, ALU.mult, ALU.add).then_inc(scan_ok, 1)
                step(0)
                with dve.Fori(1, NB) as b:
                    step(b)

            @block.tensor
            def _(pe):
                def turn(b, s):
                    t = b * 2 + s
                    pe.wait_ge(ea_in[s], 16 * b + 16)
                    wait(pe, ea_lo_ok, t - 1)
                    for k in range(K):
                        tr = pe.transpose(ps_ea[s][:, k * P:(k + 1) * P], ea_rows[:, s, k * P:(k + 1) * P], g.ident[:])
                    tr.then_inc(ea_t, 1)
                    pe.wait_ge(scaled_ok, t + 1)
                    wait(pe, scan_ok, K * (t - 1))
                    for k in range(K):
                        tr = pe.transpose(ps_x[s][:, k * P:(k + 1) * P], scaled[:, s, k * P:(k + 1) * P], g.ident[:])
                    tr.then_inc(x_t, 1)

                def back(b, s):
                    t = b * 2 + s
                    pe.wait_ge(scan_ok, K * t + K)
                    wait(pe, row_ok, t)
                    for k in range(K):
                        tr = pe.transpose(ps_back[:, k * P:(k + 1) * P], run[:, s, k, :], g.ident[:])
                    tr.then_inc(back_ok, 1)

                def step(b):
                    turn(b, 0)
                    turn(b, 1)
                    back(b, 0)
                    pe.wait_ge(ea_lo_ok, 2 * b + 2)
                    wait(pe, part_ok, K * b)
                    for m in range(K):
                        to = ps_r[m // 2][:, (m % 2) * BE:(m % 2 + 1) * BE]
                        for k in range(K):
                            mm = g.product(pe, to, [g.w(h, WR_EDGE, k, m * P, P) for h in (g.w_hi, g.w_lo)],
                                           [h[:, k, :] for h in (ea_hi, ea_lo)], k == 0, k == K - 1)
                    mm.then_inc(r_mm, 1)
                    back(b, 1)
                step(0)
                with pe.Fori(1, NB) as b:
                    step(b)

            @block.sync
            def _(sp):
                def step(b):
                    for s in range(2):
                        sp.wait_ge(row_ok, 2 * b + s + 1)
                        sp.dma_start(g.sum_table[bass.ds((2 * b + s) * P, P), :], sums[:, s, :]).then_inc(row_out[s], 16)
                        if s == 0:
                            sp.wait_ge(part_ok, K * b + K)
                            sp.dma_start(g.edge_part[bass.ds(b, 1), :, :].rearrange("b p n -> (b p) n"), part[:].rearrange("p k e -> p (k e)")).then_inc(part_out, 16)
                with sp.Fori(0, NB) as b:
                    step(b)
                for s in range(2):
                    sp.wait_ge(row_out[s], 16 * NB)
                sp.wait_ge(part_out, 16 * NB)


def node_stage(nc, g):
    sb, sem = g.sb, g.sem
    with ExitStack() as ctx:
        RX = 4
        idx = sb(ctx, "node_idx", [P, 2, 1], I32)
        xr = sb(ctx, "node_x", [P, RX, D])
        rn = sb(ctx, "node_sum", [P, 2, D])
        gr = sb(ctx, "node_agg", [P, 2, D])
        g_hi = sb(ctx, "agg_hi", [P, 2, K, P], F32R)
        g_lo = sb(ctx, "agg_lo", [P, 2, K, P], F32R)
        z = sb(ctx, "node_z", [P, 2, D])
        y = sb(ctx, "node_y", [P, 2, D])
        x1 = sb(ctx, "node_x1", [P, 2, D])
        b_row = sb(ctx, "b_row", [P, D])
        stats = sb(ctx, "node_stats", [P, 2, 6])
        mv = sb(ctx, "node_mv", [P, 2, 4])
        root = sb(ctx, "node_root", [P, 2, 1])
        ps = g.banks(ctx, "psn")
        ps_t, ps_o = ps[0:2], ps[2:4]

        b_in, idx_ok = sem("b_row_in"), sem("node_idx_staged")
        x_in = [sem(f"node_x_in{s}") for s in range(RX)]
        rn_in = [sem(f"node_sum_in{s}") for s in range(2)]
        agg_ok, turned, hi_ok, lo_ok, mm_ok = (sem(n) for n in ("node_agg_ok", "node_turned", "node_high", "node_low", "node_product"))
        z_ok, leaky_ok, y_ok, stat_ok, root_ok, scale_ok, x1_ok, acc_ok = (sem(n) for n in (
            "node_z_ok", "node_leaky", "node_y_ok", "node_stat", "node_root_ok", "node_scale", "x1_ok", "x1_added"))
        x1_out = [sem(f"x1_out{s}") for s in range(2)]
        mine = sem("node_vector_step")

        with nc.Block() as block:

            @block.sync
            def _(sp):
                sp.dma_start(b_row[:], g.rows[0:1, :].to_broadcast([P, D])).then_inc(b_in, 16)

                def step(j, s, on):
                    if on(0):
                        wait(sp, y_ok, j - RX + 1)
                        sp.dma_start(xr[:, s, :], g.x[bass.ds(j * P, P), :]).then_inc(x_in[s], 16)
                    if on(4):
                        sp.wait_ge(x1_ok, j - 3)
                        sp.dma_start(g.x1_table[bass.ds((j - 4) * P, P), :], x1[:, s % 2, :]).then_inc(x1_out[s % 2], 16)
                sweep(sp, NT, 4, 4, 8, step)
                sp.wait_ge(b_in, 16)
                for s in range(2):
                    sp.wait_ge(x1_out[s], 16 * ((NT + 1 - s) // 2))

            @block.gpsimd
            def _(pool):
                def gather(j, s):
                    wait(pool, agg_ok, j - 1)
                    nc.gpsimd.tensor_copy(idx[:, s, :], g.last_edge[:, bass.ds(j, 1)]).then_inc(idx_ok, 1)
                    wait_alone(pool, idx_ok, j + 1, g.passed)
                    nc.gpsimd.indirect_dma_start(out=rn[:, s, :], out_offset=None, in_=g.sum_table, in_offset=bass.IndirectOffsetOnAxis(ap=idx[:, s, :], axis=0)).then_inc(rn_in[s], 16)

                def step(j, s, on):
                    if on(0):
                        gather(j, s % 2)
                    if on(3):
                        pool.wait_ge(leaky_ok, j - 2)
                        wait(pool, x1_ok, j - 4)
                        q = (s - 3) % 4
                        nc.gpsimd.tensor_tensor(y[:, q % 2, :], z[:, q % 2, :], xr[:, q, :], ALU.add).then_inc(y_ok, 1)
                    if on(5):
                        pool.wait_ge(x1_ok, j - 4)
                        wait(pool, acc_ok, j - 5)
                        r = slice(0, LAST) if isinstance(j, int) and j - 5 == NT - 1 else slice(0, P)
                        nc.gpsimd.tensor_tensor(g.acc_x[r, :], g.acc_x[r, :], x1[r, (s - 5) % 2, :], ALU.add).then_inc(acc_ok, 1)
                sweep(pool, NT, 5, 4, 8, step)

            @block.scalar
            def _(act):
                def step(j, s, on):
                    if on(0):
                        act.wait_ge(turned, j + 1)
                        wait(act, mm_ok, j - 1)
                        nc.scalar.copy(g_hi[:, s % 2, :, :], ps_t[s % 2][:].rearrange("p (k e) -> p k e", k=K)).then_inc(hi_ok, 1)
                    if on(4):
                        act.wait_ge(stat_ok, 2 * (j - 4) + 2)
                        nc.scalar.activation(root[:, s % 2, :], mv[:, s % 2, 1:2], ACT.Sqrt, bias=g.eps[:]).then_inc(root_ok, 1)
                        act.wait_ge(scale_ok, 2 * (j - 4) + 2)
                        wait(act, acc_ok, j - 5)
                        wait(act, x1_out[s % 2], 16 * (j // 2 - 2) if isinstance(j, int) else (j - s % 2) * 8 - 32)
                        nc.scalar.activation(x1[:, s % 2, :], y[:, s % 2, :], ACT.Identity, bias=mv[:, s % 2, 3:4], scale=mv[:, s % 2, 2:3]).then_inc(x1_ok, 1)

                sweep(act, NT, 4, 4, 8, step)

            @block.vector
            def _(dve):
                v = nc.vector
                dve.wait_ge(b_in, 16)

                def step(j, s, on):
                    if on(0):
                        if isinstance(j, int):
                            dve.wait_ge(x_in[s], 16 * (j // RX + 1))
                            dve.wait_ge(rn_in[s % 2], 16 * (j // 2 + 1))
                        else:
                            dve.wait_ge(x_in[s], (j - s) * 4 + 16)
                            dve.wait_ge(rn_in[s % 2], (j - s % 2) * 8 + 16)
                        wait(dve, turned, j - 1)
                        v.scalar_tensor_tensor(gr[:, s % 2, :], xr[:, s, :], g.dinv[:, bass.ds(j, 1)], rn[:, s % 2, :], ALU.mult, ALU.add).then_inc(agg_ok, 1)
                    if on(2):
                        dve.wait_ge(mm_ok, j - 1)
                        wait(dve, y_ok, j - 3)
                        v.scalar_tensor_tensor(z[:, s % 2, :], ps_o[s % 2][:], g.dinv[:, bass.ds(j - 2, 1)], b_row[:], ALU.mult, ALU.add).then_inc(z_ok, 1)
                        dve.wait_ge(z_ok, j - 1)
                        v.scalar_tensor_tensor(z[:, s % 2, :], z[:, s % 2, :], NEG_SLOPE, z[:, s % 2, :], ALU.mult, ALU.max).then_inc(leaky_ok, 1)
                    if on(4):
                        dve.wait_ge(y_ok, j - 3)
                        wait(dve, x1_ok, j - 5)
                        v.bn_stats(stats[:, s % 2, :], y[:, s % 2, :]).then_inc(stat_ok, 1)
                        wait_alone(dve, stat_ok, 2 * (j - 4) + 1, g.passed)
                        v.bn_aggr(mv[:, s % 2, 0:2], stats[:, s % 2, :]).then_inc(stat_ok, 1)
                    if on(0):
                        dve.wait_ge(hi_ok, j + 1)
                        v.tensor_tensor(g_lo[:, s % 2, :, :], ps_t[s % 2][:].rearrange("p (k e) -> p k e", k=K), g_hi[:, s % 2, :, :].bitcast(F32), ALU.subtract).then_inc(lo_ok, 1)
                    if on(4):
                        dve.wait_ge(root_ok, j - 3)
                        v.reciprocal(mv[:, s % 2, 2:3], root[:, s % 2, :]).then_inc(scale_ok, 1)
                        dve.wait_ge(scale_ok, 2 * (j - 4) + 1)
                        v.scalar_tensor_tensor(mv[:, s % 2, 3:4], mv[:, s % 2, 0:1], -1.0, mv[:, s % 2, 2:3], ALU.mult, ALU.mult).then_inc(scale_ok, 1)
                sweep(dve, NT, 4, 4, 8, step)

            @block.tensor
            def _(pe):
                def step(j, s, on):
                    if on(0):
                        pe.wait_ge(agg_ok, j + 1)
                        wait(pe, lo_ok, j - 1)
                        for k in range(K):
                            tr = pe.transpose(ps_t[s % 2][:, k * P:(k + 1) * P], gr[:, s % 2, k * P:(k + 1) * P], g.ident[:])
                        tr.then_inc(turned, 1)
                    if on(1):
                        q = (s - 1) % 2
                        pe.wait_ge(lo_ok, j)
                        wait(pe, z_ok, j - 2)
                        for k in range(K):
                            mm = g.product(pe, ps_o[q][:], [h[:, q, k, :] for h in (g_hi, g_lo)],
                                           [g.w(h, W0, k) for h in (g.w_hi, g.w_lo)], k == 0, k == K - 1)
                        mm.then_inc(mm_ok, 1)
                sweep(pe, NT, 1, 4, 8, step)


def edge_stage(nc, g):
    sb, sem = g.sb, g.sem
    SN = 4
    with ExitStack() as ctx:
        idx = sb(ctx, "edge_gather_idx", [P, 2, 2], I32)
        idx2 = sb(ctx, "edge_gather_idx2", [P, 2, 1], I32)
        rows = sb(ctx, "edge_rows", [P, 2, 2, D])
        again = sb(ctx, "dst_rows_again", [P, 2, D])
        part = sb(ctx, "part_in", [P, 2, K, BE])
        vt = sb(ctx, "v_turned", [P, 2, K, BE])
        coef = sb(ctx, "coef_all", [P, K, 2, BE])
        carry = sb(ctx, "carry", [P, K])
        q_rows = sb(ctx, "q_rows", [P, 2, D])
        k_rows = sb(ctx, "k_rows", [P, 2, D])
        score = sb(ctx, "score", [P, 2, H])
        goes_b = sb(ctx, "goes_b", [H, 2, BE], BF16)
        start_b = sb(ctx, "start_b", [H, BE])
        top = sb(ctx, "top", [H, 2, BE + 1])
        total = sb(ctx, "total", [H, 2, BE + 1])
        expo = sb(ctx, "expo", [H, 2, BE])
        inv = sb(ctx, "inv_total", [H, BE])
        cp = sb(ctx, "coef_small", [H, 2, BE])
        msg = sb(ctx, "msg_rows", [P, 2, D])
        node = sb(ctx, "node_rows", [P, 2, D])
        bq_row = sb(ctx, "bq_row", [P, D])
        bk_row = sb(ctx, "bk_row", [P, D])
        ps = g.banks(ctx, "pse")
        ps_r, ps_qk, ps_t, ps_o = ps[0:2], ps[2:4], ps[4:6], ps[6:8]
        ps_a = ps[7][0:H, 0:BE]

        xt = [h[:, W0, :].rearrange("p (o k e) -> p o k e", o=2, k=K) for h in (g.w_hi, g.w_lo)]
        rt = [h[:, WR_EDGE, 0:K * BE].rearrange("p (k e) -> p k e", k=K) for h in (g.w_hi, g.w_lo)]
        st = [h[:, WR_EDGE, K * BE:].rearrange("p (k e) -> p k e", k=K) for h in (g.w_hi, g.w_lo)]

        def two(banks):
            return [b[:].rearrange("p (m e) -> p m e", m=2) for b in banks]

        const_in, init_ok = sem("edge_rows_const"), sem("edge_init")
        idx_ok, again_idx = sem("edge_idx_ok"), sem("again_idx_ok")
        rows_in = [[sem(f"rows_in{s}{o}") for o in range(2)] for s in range(2)]
        again_in = [sem(f"again_in{s}") for s in range(2)]
        part_in = [sem(f"part_in{s}") for s in range(2)]
        start_in = [sem(f"start_in{s}") for s in range(2)]
        turned, x_hi, x_lo = sem("x_turned"), sem("x_high"), sem("x_low")
        r_mm, r_sum, r_hi, r_lo = sem("r_product"), sem("r_summed"), sem("r_high"), sem("r_low")
        q_mm, q_ok, k_mm, k_ok = sem("q_product"), sem("q_rows_ok"), sem("k_product"), sem("k_rows_ok")
        v_mm, v_ok = sem("v_product"), sem("v_ok")
        qk_ok, score_ok, a_t = sem("qk_multiplied"), sem("score_ok"), sem("score_turned")
        gap_ok, exp_ok, cp_ok = sem("gaps_ok"), sem("exp_ok"), sem("coef_ok")
        cp_out, coef_in = sem("coef_stored"), sem("coef_in")
        mul_ok, scan_ok, s_hi, s_lo = sem("v_weighted"), sem("v_summed"), sem("sum_high"), sem("sum_low")
        o_mm, msg_ok, cross_ok, cross2, added = (sem(n) for n in ("o_product", "msg_ok", "cross_ok", "cross_times_msg", "msg_added"))
        msg_out = [sem(f"msg_out{s}") for s in range(2)]
        node_in = [sem(f"node_in{s}") for s in range(2)]
        sq_ok, sq_added, x_added = sem("square_ok"), sem("square_added"), sem("node_added")
        mine = sem("edge_vector_step")
        MINE = 5

        def n_nodes(i):
            return LAST if isinstance(i, int) and i == NT - 1 else P

        with nc.Block() as block:

            @block.sync
            def _(sp):
                sp.dma_start(bq_row[:], g.rows[1:2, :].to_broadcast([P, D])).then_inc(const_in, 16)
                sp.dma_start(bk_row[:], g.rows[2:3, :].to_broadcast([P, D])).then_inc(const_in, 16)

                def step(j, s, on):
                    if on(0):
                        wait(sp, r_lo, j - 1)
                        wait(sp, gap_ok, j - 1)
                        sp.dma_start(part[:, s, :, :].rearrange("p k e -> p (k e)"), g.edge_part[bass.ds(j, 1), :, :].rearrange("b p n -> (b p) n")).then_inc(part_in[s], 16)
                        sp.dma_start(goes_b[:, s, :], g.goes_row[0:1, bass.ds(j * BE, BE)].to_broadcast([H, BE])).then_inc(start_in[s], 16)
                    if on(2):
                        wait(sp, scan_ok, K * (j - 2))
                        sp.wait_ge(cp_ok, j - 1)
                        c = g.coef_table[bass.ds(j - 2, 1), :, :].rearrange("b h n -> (b h) n")
                        sp.dma_start(c, cp[:].rearrange("h c e -> h (c e)")).then_inc(cp_out, 16)
                        sp.wait_ge(cp_out, 16 * (j - 2) + 16)
                        for half in range(2):
                            of = c.rearrange("(k two) n -> two k n", two=2)[half:half + 1, :, :]
                            sp.dma_start(coef[half * 64:(half + 1) * 64, :, :, :].rearrange("p k c e -> p k (c e)"),
                                         of.to_broadcast([64, K, 2 * BE])).then_inc(coef_in, 16)
                    if on(3):
                        for q in range(2):
                            sp.wait_ge(msg_ok, 2 * (j - 3) + q + 1)
                            sp.dma_start(g.msg_table[bass.ds((j - 3) * BE + q * P, P), :], msg[:, q, :]).then_inc(msg_out[q], 16)
                    if on(1):
                        for q in range(SN):
                            i = (j - 1) * SN + q
                            if isinstance(i, int) and i >= NT:
                                continue
                            wait(sp, sq_added, i - 1)
                            sp.dma_start(node[:, q % 2, :], g.x1_table[bass.ds(i * P, P), :]).then_inc(node_in[q % 2], 16)
                sweep(sp, NB, 3, 2, 4, step)
                sp.wait_ge(const_in, 32)
                for q in range(2):
                    sp.wait_ge(msg_out[q], 16 * NB)

            @block.gpsimd
            def _(pool):
                nc.gpsimd.memset(carry[:], 0.0).then_inc(init_ok, 1)
                nc.gpsimd.memset(top[:, :, 0:1], 0.0).then_inc(init_ok, 1)
                nc.gpsimd.memset(total[:, :, 0:1], 0.0).then_inc(init_ok, 1)

                def gather(j, q):
                    t = 2 * j + q
                    if not (isinstance(j, int) and j == 0):
                        pool.wait_ge(turned, 4 * (j - 1) + 3 + q)
                    nc.gpsimd.tensor_copy(idx[:, q, 0:1], g.edge_idx[:, bass.ds(t, 1), 1]).then_inc(idx_ok, 1)
                    nc.gpsimd.tensor_copy(idx[:, q, 1:2], g.edge_idx[:, bass.ds(t, 1), 3]).then_inc(idx_ok, 1)
                    wait_alone(pool, idx_ok, 2 * t + 2, g.passed)
                    for o in range(2):
                        nc.gpsimd.indirect_dma_start(out=rows[:, q, o, :], out_offset=None, in_=g.x1_table,
                                                     in_offset=bass.IndirectOffsetOnAxis(ap=idx[:, q, o:o + 1], axis=0)).then_inc(rows_in[q][o], 16)

                def step(j, s, on):
                    if on(0):
                        gather(j, 0)
                        gather(j, 1)
                    if on(3):
                        for q in range(2):
                            t = 2 * (j - 3) + q
                            wait(pool, added, 2 * (t - 2) + 2)
                            nc.gpsimd.tensor_copy(idx2[:, q, :], g.edge_idx[:, bass.ds(t, 1), 3]).then_inc(again_idx, 1)
                            wait_alone(pool, again_idx, t + 1, g.passed)
                            nc.gpsimd.indirect_dma_start(out=again[:, q, :], out_offset=None, in_=g.x1_table,
                                                         in_offset=bass.IndirectOffsetOnAxis(ap=idx2[:, q, :], axis=0)).then_inc(again_in[q], 16)
                    if on(2):
                        for q in range(2):
                            pool.wait_ge(k_ok, 2 * (j - 2) + q + 1)
                            nc.gpsimd.tensor_tensor(k_rows[:, q, :], k_rows[:, q, :], q_rows[:, q, :], ALU.mult).then_inc(qk_ok, 1)
                    if on(3):
                        for q in range(2):
                            t = 2 * (j - 3) + q
                            pool.wait_ge(cross_ok, t + 1)
                            nc.gpsimd.tensor_tensor(again[:, q, :], again[:, q, :], msg[:, q, :], ALU.mult).then_inc(cross2, 1)
                            wait(pool, added, 2 * t)
                            nc.gpsimd.tensor_tensor(g.sum_y[:], g.sum_y[:], msg[:, q, :], ALU.add).then_inc(added, 1)
                            pool.wait_ge(cross2, t + 1)
                            nc.gpsimd.tensor_tensor(g.sum_yy[:], g.sum_yy[:], again[:, q, :], ALU.add).then_inc(added, 1)
                sweep(pool, NB, 3, 2, 4, step)

            @block.scalar
            def _(act):
                def high(j, o):
                    if not (isinstance(j, int) and j == 0):
                        act.wait_ge(r_mm, j) if o == 0 else act.wait_ge(q_mm, 2 * j)
                    for q in range(2):
                        act.wait_ge(turned, 4 * j + 2 * o + q + 1)
                        nc.scalar.copy(xt[0][:, o, :, q * P:(q + 1) * P], ps_t[q][:].rearrange("p (k e) -> p k e", k=K)).then_inc(x_hi, 1)

                def step(j, s, on):
                    if on(3):
                        for q in range(2):
                            t = 2 * (j - 3) + q
                            act.wait_ge(o_mm, t + 1)
                            wait(act, msg_out[q], 16 * (j - 3))
                            wait(act, added, 2 * (t - 2) + 2)
                            nc.scalar.activation(msg[:, q, :], ps_o[q][:], ACT.Copy, scale=g.is_last[:, bass.ds(t, 1)]).then_inc(msg_ok, 1)
                    if on(2):
                        act.wait_ge(gap_ok, j - 1)
                        nc.scalar.activation(expo[:], expo[:], ACT.Exp, scale=float(D // H) ** -0.5).then_inc(exp_ok, 1)
                    if on(1):
                        act.wait_ge(r_sum, 2 * j)
                        nc.scalar.copy(rt[0], part[:, (s - 1) % 2, :, :]).then_inc(r_hi, 1)
                    if on(0):
                        high(j, 0)
                        high(j, 1)
                    if on(2):
                        act.wait_ge(scan_ok, K * (j - 2) + K)
                        wait(act, o_mm, 2 * (j - 2))
                        nc.scalar.copy(st[0], vt[:, s, :, :]).then_inc(s_hi, 1)
                    if on(1):
                        act.wait_ge(v_mm, j)
                        wait(act, s_lo, j - 2)
                        for m in range(K):
                            nc.scalar.activation(vt[:, (s - 1) % 2, m, :], two(ps_r)[m // 2][:, m % 2, :], ACT.Identity, bias=g.bv_col[:, m:m + 1]).then_inc(v_ok, 1)
                        for q in range(SN):
                            i = (j - 1) * SN + q
                            if isinstance(i, int) and i >= NT:
                                continue
                            act.wait_ge(node_in[q % 2], 32 * (j - 1) + 16 * (q // 2) + 16)
                            r = slice(0, n_nodes(i))
                            nc.scalar.activation(node[r, q % 2, :], node[r, q % 2, :], ACT.Square).then_inc(sq_ok, 1)
                sweep(act, NB, 3, 2, 4, step)

            @block.vector
            def _(dve):
                v = nc.vector
                dve.wait_ge(const_in, 32)
                dve.wait_ge(init_ok, 3)

                def low(j, o):
                    for q in range(2):
                        dve.wait_ge(x_hi, 4 * j + 2 * o + q + 1)
                        v.tensor_tensor(xt[1][:, o, :, q * P:(q + 1) * P], ps_t[q][:].rearrange("p (k e) -> p k e", k=K),
                                        xt[0][:, o, :, q * P:(q + 1) * P].bitcast(F32), ALU.subtract).then_inc(x_lo, 1)

                def softmax(b, s):
                    count = [0]

                    def then(ins):
                        count[0] += 1
                        ins.then_inc(mine, 1)
                        dve.wait_ge(mine, b * MINE + count[0])

                    dve.wait_ge(a_t, b + 1)
                    if isinstance(b, int):
                        dve.wait_ge(start_in[s], 16 * (b // 2) + 16)
                    else:
                        dve.wait_ge(start_in[s], (b - s) * 8 + 16)
                    m, z, st0 = top[:, s, :], total[:, s, :], start_b[:]
                    then(v.tensor_scalar(st0, goes_b[:, s, :], 1.0, -START, ALU.subtract, ALU.mult))
                    then(v.tensor_tensor_scan(m[:, 1:], st0, ps_a, m[:, 0:1], ALU.add, ALU.max))
                    v.tensor_copy(top[:, 1 - s, 0:1], m[:, BE:BE + 1])
                    then(v.tensor_tensor(expo[:, 0, :], m[:, 0:BE], st0, ALU.add))
                    v.tensor_tensor(expo[:, 0, :], expo[:, 0, :], m[:, 1:], ALU.subtract)
                    v.tensor_tensor(expo[:, 1, :], ps_a, m[:, 1:], ALU.subtract).then_inc(gap_ok, 1)
                    dve.wait_ge(exp_ok, b + 1)
                    then(v.tensor_tensor_scan(z[:, 1:], expo[:, 0, :], expo[:, 1, :], z[:, 0:1], ALU.mult, ALU.add))
                    v.tensor_copy(total[:, 1 - s, 0:1], z[:, BE:BE + 1])
                    wait(dve, cp_out, 16 * b)
                    v.tensor_tensor(cp[:, 0, :], expo[:, 0, :], z[:, 0:BE], ALU.mult)
                    then(v.reciprocal(inv[:], z[:, 1:]))
                    v.tensor_tensor(cp[:, 0, :], cp[:, 0, :], inv[:], ALU.mult)
                    v.tensor_tensor(cp[:, 1, :], expo[:, 1, :], inv[:], ALU.mult).then_inc(cp_ok, 1)

                def step(j, s, on):
                    if on(2):
                        for q in range(2):
                            t = 2 * (j - 2) + q
                            dve.wait_ge(k_mm, t + 1)
                            v.tensor_tensor(k_rows[:, q, :], ps_qk[q][:], bk_row[:], ALU.add).then_inc(k_ok, 1)
                        for q in range(2):
                            t = 2 * (j - 2) + q
                            dve.wait_ge(qk_ok, t + 1)
                            wait(dve, a_t, j - 2)
                            v.tensor_reduce(score[:, q, :], k_rows[:, q, :].rearrange("p (h d) -> p h d", h=H), AX.X, ALU.add).then_inc(score_ok, 1)
                    if on(3):
                        for q in range(2):
                            t = 2 * (j - 3) + q
                            dve.wait_ge(msg_ok, t + 1)
                            dve.wait_ge(again_in[q], 16 * (j - 3) + 16)
                            v.scalar_tensor_tensor(again[:, q, :], again[:, q, :], 2.0, msg[:, q, :], ALU.mult, ALU.add).then_inc(cross_ok, 1)
                    if on(2):
                        softmax(j - 2, s)
                    if on(1):
                        q = (s - 1) % 2
                        dve.wait_ge(r_mm, j)
                        if isinstance(j, int):
                            dve.wait_ge(part_in[q], 16 * ((j - 1) // 2) + 16)
                        else:
                            dve.wait_ge(part_in[q], (j - 1 - q) * 8 + 16)
                        for h in range(2):
                            v.tensor_tensor(part[:, q, 2 * h:2 * h + 2, :], two(ps_r)[h], part[:, q, 2 * h:2 * h + 2, :], ALU.add).then_inc(r_sum, 1)
                        dve.wait_ge(r_hi, j)
                        v.tensor_tensor(rt[1], part[:, q, :, :], rt[0].bitcast(F32), ALU.subtract).then_inc(r_lo, 1)
                    if on(0):
                        low(j, 0)
                    if on(1):
                        for q in range(2):
                            dve.wait_ge(q_mm, 2 * (j - 1) + q + 1)
                            wait(dve, qk_ok, 2 * (j - 2) + q + 1)
                            v.tensor_tensor(q_rows[:, q, :], ps_qk[q][:], bq_row[:], ALU.add).then_inc(q_ok, 1)
                    if on(0):
                        low(j, 1)
                    if on(2):
                        dve.wait_ge(coef_in, 32 * (j - 2) + 32)
                        dve.wait_ge(v_ok, K * (j - 2) + K)
                        v.tensor_tensor(vt[:, s, :, :], vt[:, s, :, :], coef[:, :, 1, :], ALU.mult).then_inc(mul_ok, 1)
                        dve.wait_ge(mul_ok, 2 * (j - 2) + 1)
                        for m in range(K):
                            v.tensor_tensor_scan(vt[:, s, m, :], coef[:, m, 0, :], vt[:, s, m, :], carry[:, m:m + 1], ALU.mult, ALU.add).then_inc(scan_ok, 1)
                        dve.wait_ge(scan_ok, K * (j - 2) + K)
                        v.tensor_copy(carry[:], vt[:, s, :, BE - 1]).then_inc(mul_ok, 1)
                        dve.wait_ge(s_hi, j - 1)
                        v.tensor_tensor(st[1], vt[:, s, :, :], st[0].bitcast(F32), ALU.subtract).then_inc(s_lo, 1)
                    if on(1):
                        for q in range(SN):
                            i = (j - 1) * SN + q
                            if isinstance(i, int) and i >= NT:
                                continue
                            dve.wait_ge(sq_ok, i + 1)
                            wait(dve, sq_added, i)
                            r = slice(0, n_nodes(i))
                            v.tensor_tensor(g.acc_xx[r, :], g.acc_xx[r, :], node[r, q % 2, :], ALU.add).then_inc(sq_added, 1)
                sweep(dve, NB, 3, 2, 4, step)

            @block.tensor
            def _(pe):
                def turn(j, o):
                    for q in range(2):
                        i = 4 * j + 2 * o + q
                        pe.wait_ge(rows_in[q][o], 16 * j + 16)
                        wait(pe, x_lo, i - 1)
                        for k in range(K):
                            tr = pe.transpose(ps_t[q][:, k * P:(k + 1) * P], rows[:, q, o, k * P:(k + 1) * P], g.ident[:])
                        tr.then_inc(turned, 1)

                def by_columns(slots, parts, ms):
                    n = len(slots) * K
                    for m in ms:
                        for i in range(n):
                            slot, k = slots[i // K], i % K
                            mm = g.product(pe, two(ps_r)[m // 2][:, m % 2, :], [g.w(h, slot, k, m * P, P) for h in (g.w_hi, g.w_lo)],
                                           parts(i // K, k), i == 0, i == n - 1)
                    return mm

                def by_rows(to, left, slot):
                    for k in range(K):
                        mm = g.product(pe, to, left(k), [g.w(h, slot, k) for h in (g.w_hi, g.w_lo)], k == 0, k == K - 1)
                    return mm

                def step(j, s, on):
                    if on(1):
                        b = j - 1
                        pe.wait_ge(x_lo, 4 * b + 4)
                        wait(pe, v_ok, K * b)
                        by_columns([WR_SRC, WR_DST], lambda o, k: [h[:, o, k, :] for h in xt], (0, 1))
                    if on(2):
                        pe.wait_ge(score_ok, 2 * (j - 2) + 2)
                        wait(pe, msg_ok, 2 * j - 4)
                        for q in range(2):
                            tr = pe.transpose(ps_a[:, q * P:(q + 1) * P], score[:, q, :], g.ident[:])
                        tr.then_inc(a_t, 1)
                    if on(1):
                        by_columns([WR_SRC, WR_DST], lambda o, k: [h[:, o, k, :] for h in xt], (2, 3)).then_inc(r_mm, 1)
                    if on(0):
                        turn(j, 0)
                    if on(1):
                        for q in range(2):
                            wait(pe, k_ok, 2 * (j - 2) + q + 1)
                            by_rows(ps_qk[q][:], lambda k: [h[:, 1, k, q * P:(q + 1) * P] for h in xt], WQ).then_inc(q_mm, 1)
                    if on(0):
                        turn(j, 1)
                    if on(1):
                        pe.wait_ge(r_lo, j)
                        by_columns([WV], lambda o, k: [h[:, k, :] for h in rt], range(K)).then_inc(v_mm, 1)
                        for q in range(2):
                            pe.wait_ge(q_ok, 2 * (j - 1) + q + 1)
                            by_rows(ps_qk[q][:], lambda k: [h[:, k, q * P:(q + 1) * P] for h in rt], WK).then_inc(k_mm, 1)
                    if on(2):
                        pe.wait_ge(s_lo, j - 1)
                        pe.wait_ge(gap_ok, j - 1)
                        for q in range(2):
                            wait(pe, msg_ok, 2 * (j - 3) + q + 1)
                            by_rows(ps_o[q][:], lambda k: [h[:, k, q * P:(q + 1) * P] for h in st], WO).then_inc(o_mm, 1)
                sweep(pe, NB, 2, 2, 4, step)


def finish_stage(nc, g):
    sb, sem = g.sb, g.sem
    with ExitStack() as ctx:
        idx = sb(ctx, "fin_idx", [P, 4, 1], I32)
        consts = sb(ctx, "fin_consts", [P, 3, D])
        mean = sb(ctx, "fin_mean", [P, D])
        scale = sb(ctx, "fin_scale", [P, D])
        scale1 = sb(ctx, "fin_scale1", [P, D])
        shift = sb(ctx, "fin_shift", [P, D])
        tmp = sb(ctx, "fin_tmp", [P, D])
        x1 = sb(ctx, "fin_x1", [P, 4, D])
        ms = sb(ctx, "fin_msg", [P, 4, D])
        y = sb(ctx, "fin_y", [P, 4, D])
        stats = sb(ctx, "fin_stats", [P, 2, 6])
        mv = sb(ctx, "fin_mv", [P, 2, 4])
        root = sb(ctx, "fin_root", [P, 2, 1])
        ps = g.banks(ctx, "psf")

        const_in, idx_ok, sums_ok, tot_ok, var_ok, std_ok, coef_ok = (sem(n) for n in (
            "fin_consts_in", "fin_idx_ok", "fin_sums", "fin_totals", "fin_var", "fin_std", "fin_coef"))
        x_in = [sem(f"fin_x_in{s}") for s in range(4)]
        m_in = [sem(f"fin_m_in{s}") for s in range(4)]
        ax_ok, am_ok, y_ok, stat_ok, root_ok, scale_ok, norm_ok = (sem(n) for n in (
            "fin_x_scaled", "fin_m_scaled", "fin_y_ok", "fin_stat", "fin_root_ok", "fin_scale_ok", "fin_norm"))
        y_out = [sem(f"fin_out{s}") for s in range(4)]
        mine = sem("fin_vector_step")
        R = 4

        def reuse(eng, sems, j, s):
            if isinstance(j, int):
                wait(eng, sems[s], 16 * (j // R))
            else:
                eng.wait_ge(sems[s], (j - s) * 4)

        def arrived(eng, sems, j, s):
            if isinstance(j, int):
                eng.wait_ge(sems[s], 16 * (j // R) + 16)
            else:
                eng.wait_ge(sems[s], (j - s) * 4 + 16)

        with nc.Block() as block:

            @block.sync
            def _(sp):
                for i in range(3):
                    sp.dma_start(consts[:, i, :], g.rows[3 + i:4 + i, :].to_broadcast([P, D])).then_inc(const_in, 16)

                def step(j, s, on):
                    if on(0):
                        wait(sp, ax_ok, j - R + 1)
                        sp.dma_start(x1[:, s, :], g.x1_table[bass.ds(j * P, P), :]).then_inc(x_in[s], 16)
                    if on(3):
                        q = (s - 3) % R
                        sp.wait_ge(norm_ok, j - 2)
                        r = LAST if isinstance(j, int) and j - 3 == NT - 1 else P
                        sp.dma_start(g.out[bass.ds((j - 3) * P, r), :], y[0:r, q, :]).then_inc(y_out[q], 16)
                sweep(sp, NT, 3, R, R, step)
                sp.wait_ge(const_in, 48)
                for s in range(R):
                    sp.wait_ge(y_out[s], 16 * ((NT - 1 - s) // R + 1))

            @block.gpsimd
            def _(pool):
                def step(j, s, on):
                    if on(0):
                        wait(pool, y_ok, j - R + 1)
                        nc.gpsimd.tensor_copy(idx[:, s, :], g.last_edge[:, bass.ds(j, 1)]).then_inc(idx_ok, 1)
                        wait_alone(pool, idx_ok, j + 1, g.passed)
                        nc.gpsimd.indirect_dma_start(out=ms[:, s, :], out_offset=None, in_=g.msg_table,
                                                     in_offset=bass.IndirectOffsetOnAxis(ap=idx[:, s, :], axis=0)).then_inc(m_in[s], 16)
                    if on(1):
                        q = (s - 1) % R
                        if isinstance(j, int) and j == 1:
                            pool.wait_ge(coef_ok, 1)
                        arrived(pool, x_in, j - 1, q)
                        reuse(pool, y_out, j - 1, q)
                        nc.gpsimd.tensor_tensor(y[:, q, :], x1[:, q, :], scale1[:], ALU.mult).then_inc(ax_ok, 1)
                sweep(pool, NT, 1, R, R, step)

            @block.tensor
            def _(pe):
                pe.wait_ge(sums_ok, 2)
                pe.matmul(ps[0][:], g.ones[:], g.sum_y[:], start=True, stop=True).then_inc(tot_ok, 1)
                pe.matmul(ps[1][:], g.ones[:], g.sum_yy[:], start=True, stop=True).then_inc(tot_ok, 1)

            @block.scalar
            def _(act):
                act.wait_ge(var_ok, 1)
                nc.scalar.activation(tmp[:], tmp[:], ACT.Sqrt, bias=g.eps[:]).then_inc(std_ok, 1)

                def step(j, s, on):
                    if on(2):
                        q = (s - 2) % R
                        h = s % 2
                        act.wait_ge(stat_ok, 2 * (j - 2) + 2)
                        nc.scalar.activation(root[:, h, :], mv[:, h, 1:2], ACT.Sqrt, bias=g.eps[:]).then_inc(root_ok, 1)
                        act.wait_ge(scale_ok, 2 * (j - 2) + 2)
                        nc.scalar.activation(y[:, q, :], y[:, q, :], ACT.Identity, bias=mv[:, h, 3:4], scale=mv[:, h, 2:3]).then_inc(norm_ok, 1)
                sweep(act, NT, 2, R, R, step)

            @block.vector
            def _(dve):
                v = nc.vector
                steps = [0]

                def then(ins):
                    steps[0] += 1
                    ins.then_inc(mine, 1)
                    dve.wait_ge(mine, steps[0])

                v.tensor_tensor(g.sum_y[:], g.sum_y[:], g.acc_x[:], ALU.add).then_inc(sums_ok, 1)
                v.tensor_tensor(g.sum_yy[:], g.sum_yy[:], g.acc_xx[:], ALU.add).then_inc(sums_ok, 1)
                dve.wait_ge(const_in, 48)
                dve.wait_ge(tot_ok, 2)
                then(v.tensor_scalar(mean[:], ps[0][:], 1.0 / N, None, ALU.mult))
                then(v.tensor_tensor(tmp[:], mean[:], mean[:], ALU.mult))
                then(v.scalar_tensor_tensor(tmp[:], ps[1][:], 1.0 / N, tmp[:], ALU.mult, ALU.subtract))
                v.tensor_scalar(tmp[:], tmp[:], 0.0, None, ALU.max).then_inc(var_ok, 1)
                then(v.tensor_tensor(mean[:], mean[:], consts[:, 0, :], ALU.add))
                then(v.tensor_tensor(mean[:], consts[:, 0, :], mean[:], ALU.subtract))
                dve.wait_ge(std_ok, 1)
                then(v.reciprocal(scale[:], tmp[:]))
                then(v.tensor_tensor(scale[:], scale[:], consts[:, 1, :], ALU.mult))
                v.tensor_scalar(scale1[:], scale[:], 1.0, None, ALU.add).then_inc(coef_ok, 1)
                then(v.tensor_tensor(shift[:], mean[:], scale[:], ALU.mult))
                then(v.tensor_tensor(shift[:], shift[:], consts[:, 2, :], ALU.add))

                def step(j, s, on):
                    if on(0):
                        arrived(dve, m_in, j, s)
                        v.tensor_tensor(ms[:, s, :], ms[:, s, :], scale[:], ALU.mult).then_inc(am_ok, 1)
                        dve.wait_ge(am_ok, 2 * j + 1)
                        v.tensor_tensor(ms[:, s, :], ms[:, s, :], shift[:], ALU.add).then_inc(am_ok, 1)
                        dve.wait_ge(ax_ok, j + 1)
                        dve.wait_ge(am_ok, 2 * j + 2)
                        v.tensor_tensor(y[:, s, :], y[:, s, :], ms[:, s, :], ALU.add).then_inc(y_ok, 1)
                    if on(0):
                        dve.wait_ge(y_ok, j + 1)
                        v.bn_stats(stats[:, s % 2, :], y[:, s, :]).then_inc(stat_ok, 1)
                    if on(1):
                        h = (s - 1) % 2
                        dve.wait_ge(root_ok, j)
                        v.reciprocal(mv[:, h, 2:3], root[:, h, :]).then_inc(scale_ok, 1)
                        dve.wait_ge(scale_ok, 2 * (j - 1) + 1)
                        v.scalar_tensor_tensor(mv[:, h, 3:4], mv[:, h, 0:1], -1.0, mv[:, h, 2:3], ALU.mult, ALU.mult).then_inc(scale_ok, 1)
                    if on(0):
                        wait(dve, norm_ok, j - 1)
                        wait_alone(dve, stat_ok, 2 * j + 1, g.passed)
                        v.bn_aggr(mv[:, s % 2, 0:2], stats[:, s % 2, :]).then_inc(stat_ok, 1)
                sweep(dve, NT, 1, R, R, step)


_OUTS = [((N, D), "float32")]


def kernel(**inputs):
    import numpy as np
    import concourse.bacc as bacc
    from concourse.bass_utils import run_bass_kernel_spmd

    a = {k: np.asarray(v) for k, v in inputs.items()}

    def padded(rows, n, fill=0):
        to = np.full((n,) + rows.shape[1:], fill, rows.dtype)
        to[:rows.shape[0]] = rows
        return to

    wr = a["L1_gnn_Wr"].T
    arrays = {
        "x": padded(a["x"], NP),
        "dst_in": padded(a["dst"].reshape(E, 1), EP + P, N),
        "src_in": padded(a["src"].reshape(E, 1), EP + P),
        "eid_in": np.arange(EP + P, dtype=np.int32).reshape(EP + P, 1),
        "ea": padded(a["edge_attr_512"], EP),
        "weights": np.concatenate([a["L0_gnn_W"], wr[2 * D:], wr[:D], wr[D:2 * D], a["L1_gnn_Wq"].T,
                                   a["L1_gnn_Wk"].T, a["L1_gnn_Wv"].T, a["L1_gnn_Wo"].T]),
        "br": a["L1_gnn_br"],
        "bv": a["L1_gnn_bv"],
        "rows": np.stack([a[n] for n in ("L0_gnn_b", "L1_gnn_bq", "L1_gnn_bk", "L1_gnn_bo", "L1_gnn_gamma", "L1_gnn_beta")]),
    }
    arrays = {f"in_{k}": np.ascontiguousarray(v) for k, v in arrays.items()}
    nc = bacc.Bacc("TRN2", target_bir_lowering=False, num_devices=1)
    args = [nc.dram_tensor(k, v.shape, mybir.dt.from_np(v.dtype), kind="ExternalInput").ap() for k, v in arrays.items()]
    out = nc.dram_tensor("out_0_dram", (N, D), F32, kind="ExternalOutput").ap()
    gnn_kernel(nc, *args, out)
    r = run_bass_kernel_spmd(nc, [arrays], core_ids=[0])
    return r.results[0]["out_0_dram"]
```

```python
from contextlib import ExitStack

import concourse.bass as bass
from concourse import mybir

F32 = mybir.dt.float32
F32R = mybir.dt.float32r
BF16 = mybir.dt.bfloat16
I32 = mybir.dt.int32
ALU = mybir.AluOpType
ACT = mybir.ActivationFunctionType
AX = mybir.AxisListType

P = 128
N = 10000
E = 5000
D = 512
H = 8
K = D // P
NT = -(-N // P)
NP = NT * P
ET = -(-E // P)
EP = ET * P
BE = 2 * P
NB = EP // BE
LAST = N - (NT - 1) * P
BITS = 7
EPS = 1e-5
NEG_SLOPE = 0.01
START = -1e30
W0, WR_EDGE, WR_SRC, WR_DST, WQ, WK, WV, WO = range(8)
NW = 8


def wait(eng, sem, count):
    if isinstance(count, int) and count <= 0:
        return
    eng.wait_ge(sem, count)


def wait_alone(eng, sem, count, passed):
    eng.wait_ge(sem, count)
    eng.sem_inc(passed, 1)


def landed(j, s, k, ring):
    if isinstance(j, int):
        return 16 * ((j - k) // ring + 1)
    return (j - s) * (16 // ring) + 16 * ((s - k) // ring + 1)


def sweep(eng, n, lag, unroll, head, step):
    rounds = (n - head) // unroll
    for j in range(head):
        step(j, j % unroll, lambda k, j=j: 0 <= j - k < n)
    with eng.Fori(0, rounds) as i:
        for s in range(unroll):
            step(i * unroll + (head + s), s, lambda k: True)
    for j in range(head + rounds * unroll, n + lag):
        step(j, j % unroll, lambda k, j=j: 0 <= j - k < n)


class Shared:
    pass


def gnn_kernel(nc, x, dst_in, src_in, eid_in, ea, weights, br, bv, rows, out):

    g = Shared()
    g.x, g.dst_in, g.src_in, g.eid_in, g.ea, g.weights = x, dst_in, src_in, eid_in, ea, weights
    g.br, g.bv, g.rows, g.out = br, bv, rows, out

    def dram(name, shape, dt):
        return nc.dram_tensor(name, shape, dt, kind="Internal").ap()

    g.sdst = dram("sorted_dst", [EP + P, 1], I32)
    g.ssrc = dram("sorted_src", [EP + P, 1], I32)
    g.seid = dram("sorted_edge", [EP + P, 1], I32)
    g.dinv_table = dram("dinv_table", [NP, 1], F32)
    g.goes_row = dram("goes_row", [1, EP], BF16)
    g.edge_part = dram("edge_part", [NB, P, K * BE], F32)
    g.sum_table = dram("sum_table", [EP + P, D], F32)
    g.x1_table = dram("x1_table", [NP, D], F32)
    g.coef_table = dram("coef_table", [NB, H, 2 * BE], F32)
    g.msg_table = dram("msg_table", [EP + P, D], F32)

    with ExitStack() as whole:

        def sem(name, ctx=whole):
            return ctx.enter_context(nc.semaphore(name))

        def sb(ctx, name, shape, dt=F32):
            return ctx.enter_context(nc.sbuf_tensor(name, shape, dt))

        def banks(ctx, name, n=8):
            return [ctx.enter_context(nc.psum_tensor(f"{name}{i}", [P, 512], F32)) for i in range(n)]

        g.passed = sem("wait_passed")
        g.const_in = sem("constants_loaded")
        g.step_v, g.steps = sem("vector_step"), [0]
        g.w_hi = sb(whole, "w_hi", [P, NW, K * D], F32R)
        g.w_lo = sb(whole, "w_lo", [P, NW, K * D], F32R)
        g.ident = sb(whole, "ident", [P, P])
        g.ones = sb(whole, "ones", [P, P])
        g.eps = sb(whole, "eps", [P, 1])
        g.dinv = sb(whole, "dinv", [P, NT])
        g.last_edge = sb(whole, "last_edge", [P, NT], I32)
        g.edge_idx = sb(whole, "edge_idx", [P, ET, 4], I32)
        g.is_last = sb(whole, "is_last", [P, ET])
        g.br_col = sb(whole, "br_col", [P, K])
        g.bv_col = sb(whole, "bv_col", [P, K])
        g.acc_x = sb(whole, "acc_x", [P, D])
        g.acc_xx = sb(whole, "acc_xx", [P, D])
        g.sum_y = sb(whole, "sum_y", [P, D])
        g.sum_yy = sb(whole, "sum_yy", [P, D])

        def w(half, slot, k, lo=0, n=D):
            return half[:, slot, k * D + lo:k * D + lo + n]

        def product(pe, to, left, right, first, last):
            pe.matmul(to, left[0], right[1], start=first, stop=False)
            pe.matmul(to, left[1], right[0], start=False, stop=False)
            return pe.matmul(to, left[0], right[0], start=False, stop=last)

        with ExitStack() as early:
            g.goes_on = sb(early, "goes_on", [P, EP], BF16)
            g.sb, g.sem, g.banks, g.w, g.product = sb, sem, banks, w, product
            index_stage(nc, g)
            aggregate_stage(nc, g)
        node_stage(nc, g)
        edge_stage(nc, g)
        finish_stage(nc, g)


def index_stage(nc, g):
    sb, sem = g.sb, g.sem
    with ExitStack() as ctx:
        flat = sb(ctx, "flat_check", [ET, 2, P], I32)
        worse = sb(ctx, "worse", [ET, P])
        worse_row = sb(ctx, "worse_row", [ET, 1])
        unsorted_i = sb(ctx, "unsorted", [1, 1], I32)
        w_stage = sb(ctx, "w_stage", [P, 2, K * D // 2])
        dst_row = sb(ctx, "dst_row", [P, 1 + EP], I32)
        iota_row = sb(ctx, "iota_row", [P, P], I32)
        upper = sb(ctx, "upper", [P, P])
        none_at = sb(ctx, "none_at", [P, NT])
        zero = sb(ctx, "zero_rows", [P, D])
        counting = ctx.enter_context(ExitStack())
        place_row = sb(counting, "place_row", [P, EP], mybir.dt.int16)
        one_row = g.goes_on
        cols = sb(counting, "cols", [P, 3, ET], I32)
        cols_f = sb(counting, "cols_f", [P, 3, ET])
        less = sb(counting, "less", [P, 2, ET])
        rank = sb(counting, "rank", [P, ET], I32)
        put = sb(counting, "put", [P, 4], I32)
        counting.close()
        flat_s = sb(ctx, "flat_sorted", [ET, 4, P], I32)
        flat_f = sb(ctx, "flat_float", [ET, 4, P])
        cols_s = sb(ctx, "cols_sorted", [P, 4, ET], I32)
        low = sb(ctx, "node_low", [P, 2, ET], I32)
        high = sb(ctx, "node_high", [P, 2, ET], I32)
        hot_low = sb(ctx, "hot_low", [P, ET, P], BF16)
        hot_high = sb(ctx, "hot_high", [P, ET, NT], BF16)
        cnt = sb(ctx, "cnt", [P, NT])
        small = sb(ctx, "small", [P, 8, NT])
        differs = sb(ctx, "differs", [P, ET])
        ps = g.banks(ctx, "psi")

        copied, checked_in = sem("tables_copied"), sem("check_loaded")
        worse_ok, flag_ps, flag_ok = sem("worse_summed"), sem("flag_in_psum"), sem("flag_ready")
        count_in, counted, rank_ok, put_ok, put_out = (sem(n) for n in ("count_loaded", "counted", "rank_ready", "put_staged", "put_written"))
        ordered, flat_in, row_in = sem("edges_ordered"), sem("flat_loaded"), sem("row_loaded")
        const_ok, const_in = sem("constants_made"), g.const_in
        flat_ok, cols_ok, hot_ok = sem("flat_as_float"), sem("columns_in_psum"), sem("one_hots_ready")
        hist_ok, cnt_ok, cum_ok, root_ok = (sem(n) for n in ("histogram_in_psum", "count_ready", "prefix_in_psum", "root_ready"))
        dinv_ok, start_ok, stored = sem("dinv_ready"), sem("start_ready"), sem("index_stored")
        w_in = [sem(f"weights_loaded{s}") for s in range(2)]
        w_hi_ok, w_lo_ok = sem("weights_high"), sem("weights_low")
        step_v, step_p = g.step_v, sem("pool_step")
        zero_ok = sem("zero_rows_made")

        def w_half(to, i):
            return to[:, i // 2, (i % 2) * K * D // 2:(i % 2 + 1) * K * D // 2]

        with nc.Block() as block:

            @block.sync
            def _(sp):
                for i in range(2):
                    sp.dma_start(flat[:, i, :], g.dst_in[i:i + EP, :].rearrange("(t p) c -> t (p c)", p=P)).then_inc(checked_in, 16)
                for to, of in ((g.sdst, g.dst_in), (g.ssrc, g.src_in), (g.seid, g.eid_in)):
                    sp.dma_start(to.rearrange("(a b) c -> a (b c)", a=16), of.rearrange("(a b) c -> a (b c)", a=16)).then_inc(copied, 16)
                sp.dma_start(g.br_col[:], g.br.rearrange("(k p) -> p k", p=P), allow_slow_non_contiguous=True).then_inc(const_in, 16)
                sp.dma_start(g.bv_col[:], g.bv.rearrange("(k p) -> p k", p=P), allow_slow_non_contiguous=True).then_inc(const_in, 16)
                sp.wait_ge(zero_ok, 1)
                sp.dma_start(g.sum_table[EP:EP + P, :], zero[:]).then_inc(stored, 16)
                sp.dma_start(g.msg_table[EP:EP + P, :], zero[:]).then_inc(stored, 16)
                sp.wait_ge(copied, 48)
                sp.wait_ge(ordered, 1)
                for i, (of, o) in enumerate(((g.sdst, 0), (g.ssrc, 0), (g.seid, 0), (g.sdst, 1))):
                    sp.dma_start(flat_s[:, i, :], of[o:o + EP, :].rearrange("(t p) c -> t (p c)", p=P)).then_inc(flat_in, 16)
                sp.dma_start(dst_row[:, 1:], g.sdst[0:EP, :].rearrange("e c -> (e c)").unsqueeze(0).to_broadcast([P, EP])).then_inc(row_in, 16)
                sp.wait_ge(dinv_ok, 1)
                sp.dma_start(g.dinv_table.rearrange("(p j) c -> p (j c)", p=P), g.dinv[:]).then_inc(stored, 16)
                sp.wait_ge(start_ok, 1)
                sp.dma_start(g.goes_row, g.goes_on[0:1, :]).then_inc(stored, 16)
                sp.wait_ge(const_in, 32)
                sp.wait_ge(stored, 64)

            @block.scalar
            def _(act):
                def load(i, s):
                    rows = g.weights[bass.ds(i * (D // 2), D // 2), :]
                    act.dma_start(w_stage[:, s, :].rearrange("p (k n) -> p k n", k=K // 2), rows.rearrange("(k p) n -> p k n", p=P)).then_inc(w_in[s], 16)

                load(0, 0)
                load(1, 1)
                for i in range(2 * NW):
                    s = i % 2
                    act.wait_ge(w_in[s], 16 * (i // 2 + 1))
                    nc.scalar.copy(w_half(g.w_hi, i), w_stage[:, s, :]).then_inc(w_hi_ok, 1)
                    if i + 2 < 2 * NW:
                        act.wait_ge(w_lo_ok, i + 1)
                        load(i + 2, s)
                    if i == 4:
                        act.wait_ge(cnt_ok, 1)
                        act.wait_ge(const_ok, 2)
                        nc.scalar.activation(small[:, 0, :], cnt[:], ACT.Sqrt, bias=g.ones[:, 0:1]).then_inc(root_ok, 1)

            @block.gpsimd
            def _(pool):
                steps = [0]

                def then(ins):
                    steps[0] += 1
                    ins.then_inc(step_p, 1)
                    pool.wait_ge(step_p, steps[0])

                then(nc.gpsimd.memset(g.ones[:], 1.0))
                nc.gpsimd.memset(g.eps[:], EPS).then_inc(const_ok, 1)
                nc.gpsimd.affine_select(out=g.ident[:], in_=g.ones[:], compare_op=ALU.is_equal, fill=0.0, base=0, pattern=[[-1, P]], channel_multiplier=1).then_inc(const_ok, 1)
                nc.gpsimd.affine_select(out=upper[:], in_=g.ones[:], compare_op=ALU.is_ge, fill=0.0, base=0, pattern=[[1, P]], channel_multiplier=-1).then_inc(const_ok, 1)
                nc.gpsimd.iota(iota_row[:], [[1, P]], base=0, channel_multiplier=0).then_inc(const_ok, 1)
                nc.gpsimd.iota(none_at[:], [[0, NT]], base=EP, channel_multiplier=1, allow_small_or_imprecise_dtypes=True).then_inc(const_ok, 1)
                nc.gpsimd.memset(zero[:], 0.0).then_inc(zero_ok, 1)
                nc.gpsimd.memset(g.acc_x[:], 0.0).then_inc(const_ok, 1)
                nc.gpsimd.memset(g.acc_xx[:], 0.0).then_inc(const_ok, 1)
                nc.gpsimd.memset(g.sum_y[:], 0.0).then_inc(const_ok, 1)
                nc.gpsimd.memset(g.sum_yy[:], 0.0).then_inc(const_ok, 1)
                pool.wait_ge(flag_ok, 1)
                flag = pool.value_load(unsorted_i[0:1, 0:1], min_val=0, max_val=EP)
                with pool.If(flag > 0):
                    pool.wait_ge(copied, 48)
                    nc.gpsimd.dma_start(dst_row[:, 1:], g.dst_in[0:EP, :].rearrange("e c -> (e c)").unsqueeze(0).to_broadcast([P, EP])).then_inc(count_in, 16)
                    for i, of in enumerate((g.dst_in, g.src_in, g.eid_in)):
                        nc.gpsimd.dma_start(cols[:, i, :], of[0:EP, :].rearrange("(t p) c -> p (t c)", p=P), allow_slow_non_contiguous=True).then_inc(count_in, 16)
                    nc.gpsimd.iota(place_row[:], [[1, EP]], base=0, channel_multiplier=0, allow_small_or_imprecise_dtypes=True).then_inc(counted, 1)
                    pool.wait_ge(rank_ok, 1)
                    with pool.Fori(0, ET) as t:
                        nc.gpsimd.tensor_copy(put[:, 0:3], cols[:, :, bass.ds(t, 1)].rearrange("p c t -> p (c t)")).then_inc(put_ok, 1)
                        nc.gpsimd.tensor_copy(put[:, 3:4], rank[:, bass.ds(t, 1)]).then_inc(put_ok, 1)
                        wait_alone(pool, put_ok, 2 * t + 2, g.passed)
                        for i, to in enumerate((g.sdst, g.ssrc, g.seid)):
                            nc.gpsimd.indirect_dma_start(out=to, out_offset=bass.IndirectOffsetOnAxis(ap=put[:, 3:4], axis=0), in_=put[:, i:i + 1], in_offset=None).then_inc(put_out, 16)
                        pool.wait_ge(put_out, 48 * t + 48)
                nc.gpsimd.engine_nop().then_inc(ordered, 1)
                for i in range(2 * NW):
                    pool.wait_ge(w_hi_ok, i + 1)
                    nc.gpsimd.tensor_tensor(w_half(g.w_lo, i), w_stage[:, i % 2, :], w_half(g.w_hi, i).bitcast(F32), ALU.subtract).then_inc(w_lo_ok, 1)

            @block.tensor
            def _(pe):
                pe.wait_ge(const_ok, 9)
                pe.wait_ge(worse_ok, 2)
                pe.matmul(ps[0][0:1, 0:1], worse_row[:], g.ones[0:ET, 0:1], start=True, stop=True).then_inc(flag_ps, 1)
                pe.wait_ge(flat_ok, 1)
                for i in range(4):
                    pe.transpose(ps[1][:, i * ET:(i + 1) * ET], flat_f[:, i, :], g.ident[0:ET, 0:ET]).then_inc(cols_ok, 1)
                pe.wait_ge(hot_ok, 2)
                for t in range(ET):
                    mm = pe.matmul(ps[2][:, 0:NT], hot_low[:, t, :], hot_high[:, t, :], start=t == 0, stop=t == ET - 1)
                mm.then_inc(hist_ok, 1)
                pe.wait_ge(cnt_ok, 1)
                pe.matmul(ps[3][:, 0:NT], upper[:], cnt[:], start=True, stop=True).then_inc(cum_ok, 1)
                pe.matmul(ps[4][:, 0:NT], g.ones[:], cnt[:], start=True, stop=True).then_inc(cum_ok, 1)

            @block.vector
            def _(dve):
                steps = g.steps

                def then(ins):
                    steps[0] += 1
                    ins.then_inc(step_v, 1)
                    dve.wait_ge(step_v, steps[0])

                v = nc.vector
                dve.wait_ge(checked_in, 32)
                v.tensor_tensor(worse[:], flat[:, 0, :], flat[:, 1, :], ALU.is_gt).then_inc(worse_ok, 1)
                dve.wait_ge(worse_ok, 1)
                v.tensor_reduce(worse_row[:], worse[:], AX.X, ALU.add).then_inc(worse_ok, 1)
                dve.wait_ge(flag_ps, 1)
                v.tensor_copy(unsorted_i[:], ps[0][0:1, 0:1]).then_inc(flag_ok, 1)
                dve.wait_ge(flag_ok, 1)
                flag = dve.value_load(unsorted_i[0:1, 0:1], min_val=0, max_val=EP)
                with dve.If(flag > 0):
                    dve.wait_ge(count_in, 64)
                    dve.wait_ge(counted, 1)
                    v.tensor_copy(cols_f[:], cols[:]).then_inc(counted, 1)
                    dve.wait_ge(counted, 2)
                    with dve.Fori(0, ET) as t:
                        v.tensor_scalar(one_row[:], dst_row[:, 1:], cols_f[:, 0, bass.ds(t, 1)], 0.0, ALU.is_lt, ALU.add,
                                        accum_out=less[:, 0, bass.ds(t, 1)]).then_inc(counted, 1)
                        dve.wait_ge(counted, 3 * t + 3)
                        v.tensor_scalar(one_row[:], dst_row[:, 1:], cols_f[:, 0, bass.ds(t, 1)], None, ALU.is_equal).then_inc(counted, 1)
                        dve.wait_ge(counted, 3 * t + 4)
                        v.scalar_tensor_tensor(one_row[:], place_row[:], cols_f[:, 2, bass.ds(t, 1)], one_row[:], ALU.is_lt, ALU.mult,
                                               accum_out=less[:, 1, bass.ds(t, 1)]).then_inc(counted, 1)
                        dve.wait_ge(counted, 3 * t + 5)
                    v.tensor_tensor(rank[:], less[:, 0, :], less[:, 1, :], ALU.add).then_inc(rank_ok, 1)
                dve.wait_ge(flat_in, 64)
                v.tensor_copy(flat_f[:], flat_s[:]).then_inc(flat_ok, 1)
                dve.wait_ge(cols_ok, 4)
                then(v.tensor_copy(cols_s[:], ps[1][:, 0:4 * ET].rearrange("p (c t) -> p c t", c=4)))
                v.tensor_tensor(differs[:], cols_s[:, 0, :], cols_s[:, 3, :], ALU.not_equal)
                v.tensor_scalar(high[:], cols_s[:, 0:2, :], BITS, None, ALU.logical_shift_right)
                then(v.tensor_scalar(low[:], cols_s[:, 0:2, :], P - 1, None, ALU.bitwise_and))
                dve.wait_ge(const_ok, 9)
                v.tensor_tensor(hot_low[:], iota_row[:].unsqueeze(1).to_broadcast([P, ET, P]),
                                low[:, 0, :].unsqueeze(2).to_broadcast([P, ET, P]), ALU.is_equal).then_inc(hot_ok, 1)
                v.tensor_tensor(hot_high[:], iota_row[:, 0:NT].unsqueeze(1).to_broadcast([P, ET, NT]),
                                high[:, 0, :].unsqueeze(2).to_broadcast([P, ET, NT]), ALU.is_equal).then_inc(hot_ok, 1)
                v.scalar_tensor_tensor(g.is_last[:], cols_s[:, 0, :], float(N), differs[:], ALU.is_lt, ALU.mult)
                v.tensor_copy(g.edge_idx[:, :, 0], cols_s[:, 2, :])
                v.tensor_copy(g.edge_idx[:, :, 1], cols_s[:, 1, :])
                v.scalar_tensor_tensor(g.edge_idx[:, :, 2], low[:, 1, :], float(NT), high[:, 1, :], ALU.mult, ALU.add)
                v.tensor_copy(g.edge_idx[:, :, 3], cols_s[:, 0, :])
                dve.wait_ge(hist_ok, 1)
                v.tensor_copy(cnt[:], ps[2][:, 0:NT]).then_inc(cnt_ok, 1)
                then(v.memset(dst_row[:, 0:1], -1))
                dve.wait_ge(row_in, 16)
                v.tensor_tensor(g.goes_on[:], dst_row[:, 1:], dst_row[:, 0:EP], ALU.is_equal).then_inc(start_ok, 1)
                deg, y, t = small[:, 1, :], small[:, 2, :], small[:, 3, :]
                v.tensor_scalar(deg, cnt[:], 1.0, None, ALU.add)
                dve.wait_ge(root_ok, 1)
                then(v.reciprocal(y, small[:, 0, :]))
                then(v.tensor_tensor(t, y, y, ALU.mult))
                then(v.tensor_tensor(t, t, deg, ALU.mult))
                then(v.tensor_scalar(t, t, -0.5, 1.5, ALU.mult, ALU.add))
                v.tensor_tensor(g.dinv[:], y, t, ALU.mult).then_inc(dinv_ok, 1)
                dve.wait_ge(cum_ok, 2)
                a, b, c, e = (small[:, i, :] for i in range(4, 8))
                then(v.tensor_tensor_scan(a, g.ones[:, 0:NT], ps[4][:, 0:NT], 0.0, ALU.mult, ALU.add))
                then(v.tensor_tensor(b, a, ps[4][:, 0:NT], ALU.subtract))
                then(v.scalar_tensor_tensor(c, ps[3][:, 0:NT], -1.0, b, ALU.add, ALU.add))
                then(v.tensor_tensor(e, none_at[:], c, ALU.subtract))
                then(v.scalar_tensor_tensor(e, cnt[:], 0.0, e, ALU.is_equal, ALU.mult))
                then(v.tensor_tensor(g.last_edge[:], c, e, ALU.add))


def aggregate_stage(nc, g):
    sb, sem = g.sb, g.sem
    R = 4
    with ExitStack() as ctx:
        idx = sb(ctx, "agg_idx", [P, R, 3], I32)
        ea_rows = sb(ctx, "ea_rows", [P, R, D])
        x_rows = sb(ctx, "x_rows", [P, R, D])
        scaled = sb(ctx, "scaled_rows", [P, 2, D])
        dinv_src = sb(ctx, "dinv_src", [P, R, 1])
        ea_hi = sb(ctx, "ea_hi", [P, 2, K, BE], F32R)
        ea_lo = sb(ctx, "ea_lo", [P, 2, K, BE], F32R)
        run = sb(ctx, "run", [P, R, K, P])
        sums = sb(ctx, "sums", [P, 2, D])
        part = sb(ctx, "part", [P, K, BE])
        ps = g.banks(ctx, "psa")
        ps_ea, ps_x, ps_back, ps_r = ps[0:2], ps[2:4], ps[4:6], ps[6:8]

        idx_ok = sem("agg_idx_staged")
        ea_in = [sem(f"ea_rows_in{s}") for s in range(R)]
        x_in = [sem(f"x_rows_and_dinv_in{s}") for s in range(R)]
        scaled_ok, ea_t, x_t = sem("rows_scaled"), sem("ea_transposed"), sem("x_transposed")
        ea_hi_ok, ea_lo_ok, scan_ok, back_ok = (sem(n) for n in ("ea_high", "ea_low", "rows_summed", "sums_turned"))
        row_ok, row_out = sem("sum_rows_ready"), [sem(f"sum_rows_out{s}") for s in range(2)]
        r_mm, part_ok, part_out = sem("edge_part_in_psum"), sem("edge_part_ready"), sem("edge_part_out")

        def by_k(row):
            return row.rearrange("p (k e) -> p k e", k=K)

        with nc.Block() as block:

            @block.gpsimd
            def _(pool):
                def step(t, s, on):
                    wait(pool, ea_t, t - R + 1)
                    wait(pool, scaled_ok, t - R + 1)
                    nc.gpsimd.tensor_copy(idx[:, s, :], g.edge_idx[:, bass.ds(t, 1), 0:3].rearrange("p t c -> p (t c)")).then_inc(idx_ok, 1)
                    wait_alone(pool, idx_ok, t + 1, g.passed)
                    for i, (to, of, n) in enumerate(((ea_rows, g.ea, ea_in), (x_rows, g.x, x_in), (dinv_src, g.dinv_table, x_in))):
                        nc.gpsimd.indirect_dma_start(out=to[:, s, :], out_offset=None, in_=of, in_offset=bass.IndirectOffsetOnAxis(ap=idx[:, s, i:i + 1], axis=0)).then_inc(n[s], 16)
                sweep(pool, ET, 0, R, R, step)

            @block.scalar
            def _(act):
                def step(j, s, on):
                    for q in range(2):
                        if on(0):
                            act.wait_ge(ea_t, 2 * j + q + 1)
                            wait(act, r_mm, j - 1)
                            nc.scalar.copy(ea_hi[:, s, :, q * P:(q + 1) * P], by_k(ps_ea[q][:])).then_inc(ea_hi_ok, 1)
                    for q in range(2):
                        if on(0):
                            act.wait_ge(x_in[2 * s + q], 2 * landed(j, s, 0, 2))
                            wait(act, x_t, 2 * (j - 1) + q + 1)
                            nc.scalar.activation(scaled[:, q, :], x_rows[:, 2 * s + q, :], ACT.Copy, scale=dinv_src[:, 2 * s + q, :]).then_inc(scaled_ok, 1)
                    if on(1):
                        act.wait_ge(r_mm, j)
                        wait(act, part_out, 16 * (j - 1))
                        for m in range(K):
                            nc.scalar.activation(part[:, m, :], ps_r[m // 2][:, (m % 2) * BE:(m % 2 + 1) * BE], ACT.Identity, bias=g.br_col[:, m:m + 1]).then_inc(part_ok, 1)
                        for q in range(2):
                            act.wait_ge(back_ok, 2 * (j - 1) + q + 1)
                            wait(act, row_out[q], 16 * (j - 1))
                            nc.scalar.copy(sums[:, q, :], ps_back[q][:]).then_inc(row_ok, 1)
                sweep(act, NB, 1, 2, 4, step)

            @block.vector
            def _(dve):
                v = nc.vector

                def step(j, s, on):
                    for q in range(2):
                        dve.wait_ge(ea_hi_ok, 2 * j + q + 1)
                        v.tensor_tensor(ea_lo[:, s, :, q * P:(q + 1) * P], by_k(ps_ea[q][:]),
                                        ea_hi[:, s, :, q * P:(q + 1) * P].bitcast(F32), ALU.subtract).then_inc(ea_lo_ok, 1)
                    for q in range(2):
                        t = 2 * j + q
                        dve.wait_ge(x_t, t + 1)
                        wait(dve, scan_ok, K * t)
                        wait(dve, back_ok, t - R + 1)
                        for k in range(K):
                            before = run[:, (2 * s + q - 1) % R, k, P - 1:P]
                            if isinstance(t, int) and t == 0:
                                before = 0.0
                            v.tensor_tensor_scan(run[:, 2 * s + q, k, :], g.goes_on[:, bass.ds(t * P, P)], ps_x[q][:, k * P:(k + 1) * P],
                                                 before, ALU.mult, ALU.add).then_inc(scan_ok, 1)
                sweep(dve, NB, 0, 2, 4, step)

            @block.tensor
            def _(pe):
                def step(j, s, on):
                    if on(0):
                        for q in range(2):
                            pe.wait_ge(ea_in[2 * s + q], landed(j, s, 0, 2))
                            wait(pe, ea_lo_ok, 2 * (j - 1) + q + 1)
                            for k in range(K):
                                tr = pe.transpose(ps_ea[q][:, k * P:(k + 1) * P], ea_rows[:, 2 * s + q, k * P:(k + 1) * P], g.ident[:])
                            tr.then_inc(ea_t, 1)
                    if on(1):
                        pe.wait_ge(ea_lo_ok, 2 * j)
                        wait(pe, part_ok, K * (j - 1))
                        for m in range(K):
                            to = ps_r[m // 2][:, (m % 2) * BE:(m % 2 + 1) * BE]
                            for k in range(K):
                                mm = g.product(pe, to, [g.w(h, WR_EDGE, k, m * P, P) for h in (g.w_hi, g.w_lo)],
                                               [h[:, 1 - s, k, :] for h in (ea_hi, ea_lo)], k == 0, k == K - 1)
                        mm.then_inc(r_mm, 1)
                    if on(0):
                        for q in range(2):
                            pe.wait_ge(scaled_ok, 2 * j + q + 1)
                            wait(pe, scan_ok, K * (2 * (j - 1) + q + 1))
                            for k in range(K):
                                tr = pe.transpose(ps_x[q][:, k * P:(k + 1) * P], scaled[:, q, k * P:(k + 1) * P], g.ident[:])
                            tr.then_inc(x_t, 1)
                    if on(1):
                        for q in range(2):
                            t = 2 * (j - 1) + q
                            pe.wait_ge(scan_ok, K * t + K)
                            wait(pe, row_ok, t - 1)
                            for k in range(K):
                                tr = pe.transpose(ps_back[q][:, k * P:(k + 1) * P], run[:, 2 * (1 - s) + q, k, :], g.ident[:])
                            tr.then_inc(back_ok, 1)
                sweep(pe, NB, 1, 2, 4, step)

            @block.sync
            def _(sp):
                def step(b):
                    sp.wait_ge(part_ok, K * b + K)
                    sp.dma_start(g.edge_part[bass.ds(b, 1), :, :].rearrange("b p n -> (b p) n"), part[:].rearrange("p k e -> p (k e)")).then_inc(part_out, 16)
                    for s in range(2):
                        sp.wait_ge(row_ok, 2 * b + s + 1)
                        sp.dma_start(g.sum_table[bass.ds((2 * b + s) * P, P), :], sums[:, s, :]).then_inc(row_out[s], 16)
                with sp.Fori(0, NB) as b:
                    step(b)
                for s in range(2):
                    sp.wait_ge(row_out[s], 16 * NB)
                sp.wait_ge(part_out, 16 * NB)


def node_stage(nc, g):
    sb, sem = g.sb, g.sem
    with ExitStack() as ctx:
        RX = 8
        RS = 4
        idx = sb(ctx, "node_idx", [P, RS, 1], I32)
        xr = sb(ctx, "node_x", [P, RX, D])
        rn = sb(ctx, "node_sum", [P, RS, D])
        gr = sb(ctx, "node_agg", [P, 2, D])
        g_hi = sb(ctx, "agg_hi", [P, 2, K, P], F32R)
        g_lo = sb(ctx, "agg_lo", [P, 2, K, P], F32R)
        z = sb(ctx, "node_z", [P, 2, D])
        y = sb(ctx, "node_y", [P, 2, D])
        x1 = sb(ctx, "node_x1", [P, 2, D])
        b_row = sb(ctx, "b_row", [P, D])
        stats = sb(ctx, "node_stats", [P, 2, 6])
        mv = sb(ctx, "node_mv", [P, 2, 4])
        root = sb(ctx, "node_root", [P, 2, 1])
        ps = g.banks(ctx, "psn")
        ps_t, ps_o = ps[0:2], ps[2:4]

        b_in, idx_ok = g.const_in, sem("node_idx_staged")
        x_in = [sem(f"node_x_in{s}") for s in range(RX)]
        rn_in = [sem(f"node_sum_in{s}") for s in range(RS)]
        agg_ok, turned, hi_ok, lo_ok, mm_ok = (sem(n) for n in ("node_agg_ok", "node_turned", "node_high", "node_low", "node_product"))
        z_ok, leaky_ok, y_ok, stat_ok, root_ok, scale_ok, x1_ok = (sem(n) for n in (
            "node_z_ok", "node_leaky", "node_y_ok", "node_stat", "node_root_ok", "node_scale", "x1_ok"))
        x1_out = [sem(f"x1_out{s}") for s in range(2)]

        def by_k(row):
            return row.rearrange("p (k e) -> p k e", k=K)

        with nc.Block() as block:

            @block.sync
            def _(sp):
                sp.dma_start(b_row[:], g.rows[0:1, :].to_broadcast([P, D])).then_inc(b_in, 16)

                def step(j, s, on):
                    if on(0):
                        wait(sp, y_ok, j - RX + 1)
                        sp.dma_start(xr[:, s, :], g.x[bass.ds(j * P, P), :]).then_inc(x_in[s], 16)
                    if on(6):
                        sp.wait_ge(x1_ok, j - 5)
                        sp.dma_start(g.x1_table[bass.ds((j - 6) * P, P), :], x1[:, s % 2, :]).then_inc(x1_out[s % 2], 16)
                sweep(sp, NT, 6, 8, 8, step)
                sp.wait_ge(b_in, 48)
                for s in range(2):
                    sp.wait_ge(x1_out[s], 16 * ((NT + 1 - s) // 2))

            @block.gpsimd
            def _(pool):
                def step(j, s, on):
                    if on(0):
                        wait(pool, agg_ok, j - RS + 1)
                        nc.gpsimd.tensor_copy(idx[:, s % RS, :], g.last_edge[:, bass.ds(j, 1)]).then_inc(idx_ok, 1)
                        wait_alone(pool, idx_ok, j + 1, g.passed)
                        nc.gpsimd.indirect_dma_start(out=rn[:, s % RS, :], out_offset=None, in_=g.sum_table,
                                                     in_offset=bass.IndirectOffsetOnAxis(ap=idx[:, s % RS, :], axis=0)).then_inc(rn_in[s % RS], 16)
                    if on(5):
                        pool.wait_ge(leaky_ok, j - 4)
                        wait(pool, x1_ok, j - 6)
                        nc.gpsimd.tensor_tensor(y[:, (s - 5) % 2, :], z[:, (s - 5) % 2, :], xr[:, (s - 5) % RX, :], ALU.add).then_inc(y_ok, 1)
                sweep(pool, NT, 5, 8, 8, step)

            @block.scalar
            def _(act):
                def step(j, s, on):
                    if on(2):
                        act.wait_ge(turned, j - 1)
                        wait(act, mm_ok, j - 3)
                        nc.scalar.copy(g_hi[:, s % 2, :, :], by_k(ps_t[s % 2][:])).then_inc(hi_ok, 1)
                    if on(6):
                        act.wait_ge(stat_ok, 2 * (j - 6) + 2)
                        nc.scalar.activation(root[:, s % 2, :], mv[:, s % 2, 1:2], ACT.Sqrt, bias=g.eps[:]).then_inc(root_ok, 1)
                        act.wait_ge(scale_ok, 2 * (j - 6) + 2)
                        wait(act, x1_out[s % 2], landed(j, s, 8, 2))
                        nc.scalar.activation(x1[:, s % 2, :], y[:, s % 2, :], ACT.Identity, bias=mv[:, s % 2, 3:4], scale=mv[:, s % 2, 2:3]).then_inc(x1_ok, 1)
                sweep(act, NT, 6, 8, 8, step)

            @block.vector
            def _(dve):
                v = nc.vector
                dve.wait_ge(b_in, 48)

                def step(j, s, on):
                    h = s % 2
                    if on(2):
                        dve.wait_ge(x_in[(s - 2) % RX], landed(j, s, 2, RX))
                        dve.wait_ge(rn_in[(s - 2) % RS], landed(j, s, 2, RS))
                        wait(dve, turned, j - 3)
                        v.scalar_tensor_tensor(gr[:, h, :], xr[:, (s - 2) % RX, :], g.dinv[:, bass.ds(j - 2, 1)], rn[:, (s - 2) % RS, :], ALU.mult, ALU.add).then_inc(agg_ok, 1)
                    if on(4):
                        dve.wait_ge(mm_ok, j - 3)
                        wait(dve, y_ok, j - 5)
                        v.scalar_tensor_tensor(z[:, h, :], ps_o[h][:], g.dinv[:, bass.ds(j - 4, 1)], b_row[:], ALU.mult, ALU.add).then_inc(z_ok, 1)
                    if on(6):
                        dve.wait_ge(y_ok, j - 5)
                        wait(dve, x1_ok, j - 7)
                        v.bn_stats(stats[:, h, :], y[:, h, :]).then_inc(stat_ok, 1)
                    if on(4):
                        dve.wait_ge(z_ok, j - 3)
                        v.scalar_tensor_tensor(z[:, h, :], z[:, h, :], NEG_SLOPE, z[:, h, :], ALU.mult, ALU.max).then_inc(leaky_ok, 1)
                    if on(6):
                        wait_alone(dve, stat_ok, 2 * (j - 6) + 1, g.passed)
                        v.bn_aggr(mv[:, h, 0:2], stats[:, h, :]).then_inc(stat_ok, 1)
                    if on(2):
                        dve.wait_ge(hi_ok, j - 1)
                        v.tensor_tensor(g_lo[:, h, :, :], by_k(ps_t[h][:]), g_hi[:, h, :, :].bitcast(F32), ALU.subtract).then_inc(lo_ok, 1)
                    if on(6):
                        dve.wait_ge(root_ok, j - 5)
                        v.reciprocal(mv[:, h, 2:3], root[:, h, :]).then_inc(scale_ok, 1)
                        dve.wait_ge(scale_ok, 2 * (j - 6) + 1)
                        v.scalar_tensor_tensor(mv[:, h, 3:4], mv[:, h, 0:1], -1.0, mv[:, h, 2:3], ALU.mult, ALU.mult).then_inc(scale_ok, 1)
                sweep(dve, NT, 6, 8, 8, step)

            @block.tensor
            def _(pe):
                def step(j, s, on):
                    if on(2):
                        pe.wait_ge(agg_ok, j - 1)
                        wait(pe, lo_ok, j - 3)
                        for k in range(K):
                            tr = pe.transpose(ps_t[s % 2][:, k * P:(k + 1) * P], gr[:, s % 2, k * P:(k + 1) * P], g.ident[:])
                        tr.then_inc(turned, 1)
                    if on(3):
                        q = (s - 3) % 2
                        pe.wait_ge(lo_ok, j - 2)
                        wait(pe, z_ok, j - 4)
                        for k in range(K):
                            mm = g.product(pe, ps_o[q][:], [h[:, q, k, :] for h in (g_hi, g_lo)],
                                           [g.w(h, W0, k) for h in (g.w_hi, g.w_lo)], k == 0, k == K - 1)
                        mm.then_inc(mm_ok, 1)
                sweep(pe, NT, 3, 8, 8, step)


def edge_stage(nc, g):
    sb, sem = g.sb, g.sem
    SN = 4
    with ExitStack() as ctx:
        idx = sb(ctx, "edge_gather_idx", [P, 2, 2], I32)
        idx2 = sb(ctx, "edge_gather_idx2", [P, 2, 1], I32)
        rows = sb(ctx, "edge_rows", [P, 2, 2, D])
        again = sb(ctx, "dst_rows_again", [P, 2, D])
        part = sb(ctx, "part_in", [P, 2, K, BE])
        vt = sb(ctx, "v_turned", [P, 2, K, BE])
        coef = sb(ctx, "coef_all", [P, K, 2, BE])
        carry = sb(ctx, "carry", [P, K])
        q_rows = sb(ctx, "q_rows", [P, 2, D])
        k_rows = sb(ctx, "k_rows", [P, 2, D])
        score = sb(ctx, "score", [P, 2, H])
        goes_b = sb(ctx, "goes_b", [H, 2, BE], BF16)
        start_b = sb(ctx, "start_b", [H, BE])
        top = sb(ctx, "top", [H, 2, BE + 1])
        total = sb(ctx, "total", [H, 2, BE + 1])
        expo = sb(ctx, "expo", [H, 2, BE])
        msg = sb(ctx, "msg_rows", [P, 2, D])
        node = sb(ctx, "node_rows", [P, SN, D])
        bq_row = sb(ctx, "bq_row", [P, D])
        bk_row = sb(ctx, "bk_row", [P, D])
        ps = g.banks(ctx, "pse")
        ps_r, ps_qk, ps_t, ps_o = ps[0:2], ps[2:4], ps[4:6], ps[6:8]
        ps_a = ps[7][0:H, 0:BE]

        xt = [h[:, W0, :].rearrange("p (o k e) -> p o k e", o=2, k=K) for h in (g.w_hi, g.w_lo)]
        rt = [h[:, WR_EDGE, 0:K * BE].rearrange("p (k e) -> p k e", k=K) for h in (g.w_hi, g.w_lo)]
        st = [h[:, WR_EDGE, K * BE:].rearrange("p (k e) -> p k e", k=K) for h in (g.w_hi, g.w_lo)]

        def two(banks):
            return [b[:].rearrange("p (m e) -> p m e", m=2) for b in banks]

        const_in, init_ok = g.const_in, sem("edge_init")
        idx_ok, again_idx = sem("edge_idx_ok"), sem("again_idx_ok")
        rows_in = [sem(f"rows_in{s}") for s in range(2)]
        again_in = [sem(f"again_in{s}") for s in range(2)]
        part_in = [sem(f"part_and_starts_in{s}") for s in range(2)]
        turned, x_hi, x_lo = sem("x_turned"), sem("x_high"), sem("x_low")
        r_mm, r_sum, r_hi, r_lo = sem("r_product"), sem("r_summed"), sem("r_high"), sem("r_low")
        q_mm, q_ok, k_mm, k_ok = sem("q_product"), sem("q_rows_ok"), sem("k_product"), sem("k_rows_ok")
        v_mm, v_ok = sem("v_product"), sem("v_ok")
        qk_ok, score_ok, a_t = sem("qk_multiplied"), sem("score_ok"), sem("score_turned")
        gap_ok, exp_ok, cp_ok = sem("gaps_ok"), sem("exp_ok"), sem("coef_ok")
        cp_out, coef_in = sem("coef_stored"), sem("coef_in")
        mul_ok, scan_ok, s_hi, s_lo = sem("v_weighted"), sem("v_summed"), sem("sum_high"), sem("sum_low")
        o_mm, msg_ok, cross_ok, cross2, added = (sem(n) for n in ("o_product", "msg_ok", "cross_ok", "cross_times_msg", "msg_added"))
        msg_out = [sem(f"msg_out{s}") for s in range(2)]
        node_in = sem("node_in")
        sq_ok, sq_added, x_added = sem("square_ok"), sem("square_added"), sem("node_added")
        mine = sem("edge_vector_step")
        MINE = 5

        def nodes_up_to(b):
            return min(SN * (b + 1), NT) if isinstance(b, int) else SN * (b + 1)

        def n_nodes(i):
            return LAST if isinstance(i, int) and i == NT - 1 else P

        with nc.Block() as block:

            @block.sync
            def _(sp):
                sp.dma_start(bq_row[:], g.rows[1:2, :].to_broadcast([P, D])).then_inc(const_in, 16)
                sp.dma_start(bk_row[:], g.rows[2:3, :].to_broadcast([P, D])).then_inc(const_in, 16)

                def step(j, s, on):
                    if on(0):
                        wait(sp, r_lo, j - 1)
                        wait(sp, gap_ok, j - 1)
                        sp.dma_start(part[:, s, :, :].rearrange("p k e -> p (k e)"), g.edge_part[bass.ds(j, 1), :, :].rearrange("b p n -> (b p) n")).then_inc(part_in[s], 16)
                        sp.dma_start(goes_b[:, s, :], g.goes_row[0:1, bass.ds(j * BE, BE)].to_broadcast([H, BE])).then_inc(part_in[s], 16)
                    if on(2):
                        wait(sp, scan_ok, K * (j - 2))
                        sp.wait_ge(cp_ok, j - 1)
                        c = g.coef_table[bass.ds(j - 2, 1), :, :].rearrange("b h n -> (b h) n")
                        sp.dma_start(c, expo[:].rearrange("h c e -> h (c e)")).then_inc(cp_out, 16)
                        sp.wait_ge(cp_out, 16 * (j - 2) + 16)
                        for half in range(2):
                            of = c.rearrange("(k two) n -> two k n", two=2)[half:half + 1, :, :]
                            sp.dma_start(coef[half * 64:(half + 1) * 64, :, :, :].rearrange("p k c e -> p k (c e)"),
                                         of.to_broadcast([64, K, 2 * BE])).then_inc(coef_in, 16)
                    if on(3):
                        for q in range(2):
                            sp.wait_ge(msg_ok, 2 * (j - 3) + q + 1)
                            sp.dma_start(g.msg_table[bass.ds((j - 3) * BE + q * P, P), :], msg[:, q, :]).then_inc(msg_out[q], 16)
                    if on(1):
                        wait(sp, sq_added, SN * (j - 1))
                        for q in range(SN):
                            i = (j - 1) * SN + q
                            if isinstance(i, int) and i >= NT:
                                continue
                            sp.dma_start(node[:, q, :], g.x1_table[bass.ds(i * P, P), :]).then_inc(node_in, 16)
                sweep(sp, NB, 3, 2, 6, step)
                sp.wait_ge(const_in, 80)
                for q in range(2):
                    sp.wait_ge(msg_out[q], 16 * NB)

            @block.gpsimd
            def _(pool):
                nc.gpsimd.memset(carry[:], 0.0).then_inc(init_ok, 1)
                nc.gpsimd.memset(top[:, :, 0:1], 0.0).then_inc(init_ok, 1)
                nc.gpsimd.memset(total[:, :, 0:1], 0.0).then_inc(init_ok, 1)

                def gather(j, q):
                    t = 2 * j + q
                    if not (isinstance(j, int) and j == 0):
                        pool.wait_ge(turned, 4 * (j - 1) + 3 + q)
                    nc.gpsimd.tensor_copy(idx[:, q, 0:1], g.edge_idx[:, bass.ds(t, 1), 1]).then_inc(idx_ok, 1)
                    nc.gpsimd.tensor_copy(idx[:, q, 1:2], g.edge_idx[:, bass.ds(t, 1), 3]).then_inc(idx_ok, 1)
                    wait_alone(pool, idx_ok, 2 * t + 2, g.passed)
                    for o in range(2):
                        nc.gpsimd.indirect_dma_start(out=rows[:, q, o, :], out_offset=None, in_=g.x1_table,
                                                     in_offset=bass.IndirectOffsetOnAxis(ap=idx[:, q, o:o + 1], axis=0)).then_inc(rows_in[q], 16)

                def step(j, s, on):
                    if on(0):
                        gather(j, 0)
                        gather(j, 1)
                    if on(2):
                        for q in range(2):
                            pool.wait_ge(k_ok, 2 * (j - 2) + q + 1)
                            nc.gpsimd.tensor_tensor(k_rows[:, q, :], k_rows[:, q, :], q_rows[:, q, :], ALU.mult).then_inc(qk_ok, 1)
                    if on(4):
                        for q in range(2):
                            t = 2 * (j - 4) + q
                            pool.wait_ge(cross_ok, t + 1)
                            nc.gpsimd.tensor_tensor(again[:, q, :], again[:, q, :], msg[:, q, :], ALU.mult).then_inc(cross2, 1)
                            wait(pool, added, 2 * t)
                            nc.gpsimd.tensor_tensor(g.sum_y[:], g.sum_y[:], msg[:, q, :], ALU.add).then_inc(added, 1)
                            pool.wait_ge(cross2, t + 1)
                            nc.gpsimd.tensor_tensor(g.sum_yy[:], g.sum_yy[:], again[:, q, :], ALU.add).then_inc(added, 1)
                    if on(3):
                        for q in range(2):
                            t = 2 * (j - 3) + q
                            wait(pool, added, 2 * (t - 2) + 2)
                            nc.gpsimd.tensor_copy(idx2[:, q, :], g.edge_idx[:, bass.ds(t, 1), 3]).then_inc(again_idx, 1)
                            wait_alone(pool, again_idx, t + 1, g.passed)
                            nc.gpsimd.indirect_dma_start(out=again[:, q, :], out_offset=None, in_=g.x1_table,
                                                         in_offset=bass.IndirectOffsetOnAxis(ap=idx2[:, q, :], axis=0)).then_inc(again_in[q], 16)
                    if on(2):
                        pool.wait_ge(node_in, 16 * nodes_up_to(j - 2))
                        for q in range(SN):
                            i = (j - 2) * SN + q
                            if isinstance(i, int) and i >= NT:
                                continue
                            wait(pool, x_added, i)
                            r = slice(0, n_nodes(i))
                            nc.gpsimd.tensor_tensor(g.acc_x[r, :], g.acc_x[r, :], node[r, q, :], ALU.add).then_inc(x_added, 1)
                sweep(pool, NB, 4, 2, 6, step)

            @block.scalar
            def _(act):
                def high(j, o):
                    if not (isinstance(j, int) and j == 0):
                        act.wait_ge(r_mm, j) if o == 0 else act.wait_ge(q_mm, 2 * j)
                    for q in range(2):
                        act.wait_ge(turned, 4 * j + 2 * o + q + 1)
                        nc.scalar.copy(xt[0][:, o, :, q * P:(q + 1) * P], ps_t[q][:].rearrange("p (k e) -> p k e", k=K)).then_inc(x_hi, 1)

                def step(j, s, on):
                    if on(0):
                        high(j, 0)
                    if on(2):
                        act.wait_ge(gap_ok, j - 1)
                        nc.scalar.activation(expo[:], expo[:], ACT.Exp, scale=float(D // H) ** -0.5).then_inc(exp_ok, 1)
                    if on(1):
                        act.wait_ge(r_sum, 2 * j)
                        nc.scalar.copy(rt[0], part[:, (s - 1) % 2, :, :]).then_inc(r_hi, 1)
                    if on(2):
                        for q in range(SN):
                            i = (j - 2) * SN + q
                            if isinstance(i, int) and i >= NT:
                                continue
                            act.wait_ge(x_added, i + 1)
                            r = slice(0, n_nodes(i))
                            nc.scalar.activation(node[r, q, :], node[r, q, :], ACT.Square).then_inc(sq_ok, 1)
                    if on(3):
                        for q in range(2):
                            t = 2 * (j - 3) + q
                            act.wait_ge(o_mm, t + 1)
                            wait(act, msg_out[q], 16 * (j - 3))
                            wait(act, added, 2 * (t - 2) + 2)
                            nc.scalar.activation(msg[:, q, :], ps_o[q][:], ACT.Copy, scale=g.is_last[:, bass.ds(t, 1)]).then_inc(msg_ok, 1)
                    if on(0):
                        high(j, 1)
                    if on(2):
                        act.wait_ge(scan_ok, K * (j - 2) + K)
                        wait(act, o_mm, 2 * (j - 2))
                        nc.scalar.copy(st[0], vt[:, s, :, :]).then_inc(s_hi, 1)
                    if on(1):
                        act.wait_ge(v_mm, j)
                        wait(act, s_lo, j - 2)
                        for m in range(K):
                            nc.scalar.activation(vt[:, (s - 1) % 2, m, :], two(ps_r)[m // 2][:, m % 2, :], ACT.Identity, bias=g.bv_col[:, m:m + 1]).then_inc(v_ok, 1)
                sweep(act, NB, 3, 2, 6, step)

            @block.vector
            def _(dve):
                v = nc.vector
                dve.wait_ge(const_in, 80)
                dve.wait_ge(init_ok, 3)

                def low(j, o):
                    for q in range(2):
                        dve.wait_ge(x_hi, 4 * j + 2 * o + q + 1)
                        v.tensor_tensor(xt[1][:, o, :, q * P:(q + 1) * P], ps_t[q][:].rearrange("p (k e) -> p k e", k=K),
                                        xt[0][:, o, :, q * P:(q + 1) * P].bitcast(F32), ALU.subtract).then_inc(x_lo, 1)

                def maxima(b, s):
                    dve.wait_ge(a_t, b + 1)
                    dve.wait_ge(part_in[s], 2 * landed(b, s, 0, 2))
                    m, st0 = top[:, s, :], start_b[:]
                    v.tensor_scalar(st0, goes_b[:, s, :], 1.0, -START, ALU.subtract, ALU.mult).then_inc(mine, 1)
                    dve.wait_ge(mine, MINE * b + 1)
                    v.tensor_tensor_scan(m[:, 1:], st0, ps_a, m[:, 0:1], ALU.add, ALU.max).then_inc(mine, 1)
                    dve.wait_ge(mine, MINE * b + 2)
                    wait(dve, cp_out, 16 * b)
                    v.tensor_copy(top[:, 1 - s, 0:1], m[:, BE:BE + 1])
                    v.tensor_tensor(expo[:, 0, :], m[:, 0:BE], st0, ALU.add).then_inc(mine, 1)
                    dve.wait_ge(mine, MINE * b + 3)
                    v.tensor_tensor(expo[:, 0, :], expo[:, 0, :], m[:, 1:], ALU.subtract)
                    v.tensor_tensor(expo[:, 1, :], ps_a, m[:, 1:], ALU.subtract).then_inc(gap_ok, 1)

                def coefficients(b, s):
                    z = total[:, s, :]
                    dve.wait_ge(exp_ok, b + 1)
                    v.tensor_tensor_scan(z[:, 1:], expo[:, 0, :], expo[:, 1, :], z[:, 0:1], ALU.mult, ALU.add).then_inc(mine, 1)
                    dve.wait_ge(mine, MINE * b + 4)
                    v.tensor_copy(total[:, 1 - s, 0:1], z[:, BE:BE + 1])
                    v.tensor_tensor(expo[:, 0, :], expo[:, 0, :], z[:, 0:BE], ALU.mult)
                    v.reciprocal(start_b[:], z[:, 1:]).then_inc(mine, 1)
                    dve.wait_ge(mine, MINE * b + 5)
                    v.tensor_tensor(expo[:], expo[:], start_b[:].unsqueeze(1).to_broadcast([H, 2, BE]), ALU.mult).then_inc(cp_ok, 1)

                def step(j, s, on):
                    if on(2):
                        for q in range(2):
                            t = 2 * (j - 2) + q
                            dve.wait_ge(k_mm, t + 1)
                            v.tensor_tensor(k_rows[:, q, :], ps_qk[q][:], bk_row[:], ALU.add).then_inc(k_ok, 1)
                    if on(4):
                        for q in range(2):
                            t = 2 * (j - 4) + q
                            dve.wait_ge(msg_ok, t + 1)
                            dve.wait_ge(again_in[q], 16 * (j - 4) + 16)
                            v.scalar_tensor_tensor(again[:, q, :], again[:, q, :], 2.0, msg[:, q, :], ALU.mult, ALU.add).then_inc(cross_ok, 1)
                    if on(2):
                        for q in range(2):
                            t = 2 * (j - 2) + q
                            dve.wait_ge(qk_ok, t + 1)
                            wait(dve, a_t, j - 2)
                            v.tensor_reduce(score[:, q, :], k_rows[:, q, :].rearrange("p (h d) -> p h d", h=H), AX.X, ALU.add).then_inc(score_ok, 1)
                        maxima(j - 2, s)
                    if on(1):
                        dve.wait_ge(r_mm, j)
                        dve.wait_ge(part_in[(s - 1) % 2], 2 * landed(j, s, 1, 2))
                        r = part[:, (s - 1) % 2, :, :]
                        for h in range(2):
                            v.tensor_tensor(r[:, 2 * h:2 * h + 2, :], two(ps_r)[h], r[:, 2 * h:2 * h + 2, :], ALU.add).then_inc(r_sum, 1)
                    if on(0):
                        low(j, 0)
                    if on(2):
                        coefficients(j - 2, s)
                    if on(1):
                        dve.wait_ge(r_hi, j)
                        v.tensor_tensor(rt[1], r, rt[0].bitcast(F32), ALU.subtract).then_inc(r_lo, 1)
                        for q in range(2):
                            dve.wait_ge(q_mm, 2 * (j - 1) + q + 1)
                            wait(dve, qk_ok, 2 * (j - 2) + q + 1)
                            v.tensor_tensor(q_rows[:, q, :], ps_qk[q][:], bq_row[:], ALU.add).then_inc(q_ok, 1)
                    if on(0):
                        low(j, 1)
                    if on(2):
                        dve.wait_ge(coef_in, 32 * (j - 2) + 32)
                        dve.wait_ge(v_ok, K * (j - 2) + K)
                        v.tensor_tensor(vt[:, s, :, :], vt[:, s, :, :], coef[:, :, 1, :], ALU.mult).then_inc(mul_ok, 1)
                        dve.wait_ge(mul_ok, 2 * (j - 2) + 1)
                        for m in range(K):
                            v.tensor_tensor_scan(vt[:, s, m, :], coef[:, m, 0, :], vt[:, s, m, :], carry[:, m:m + 1], ALU.mult, ALU.add).then_inc(scan_ok, 1)
                        dve.wait_ge(scan_ok, K * (j - 2) + K)
                        v.tensor_copy(carry[:], vt[:, s, :, BE - 1]).then_inc(mul_ok, 1)
                        for q in range(SN):
                            i = (j - 2) * SN + q
                            if isinstance(i, int) and i >= NT:
                                continue
                            dve.wait_ge(sq_ok, i + 1)
                            wait(dve, sq_added, i)
                            r = slice(0, n_nodes(i))
                            v.tensor_tensor(g.acc_xx[r, :], g.acc_xx[r, :], node[r, q, :], ALU.add).then_inc(sq_added, 1)
                        dve.wait_ge(s_hi, j - 1)
                        v.tensor_tensor(st[1], vt[:, s, :, :], st[0].bitcast(F32), ALU.subtract).then_inc(s_lo, 1)
                sweep(dve, NB, 4, 2, 6, step)

            @block.tensor
            def _(pe):
                def turn(j, o):
                    for q in range(2):
                        i = 4 * j + 2 * o + q
                        pe.wait_ge(rows_in[q], 32 * j + 32)
                        wait(pe, x_lo, i - 1)
                        for k in range(K):
                            tr = pe.transpose(ps_t[q][:, k * P:(k + 1) * P], rows[:, q, o, k * P:(k + 1) * P], g.ident[:])
                        tr.then_inc(turned, 1)

                def by_columns(slots, parts, ms):
                    n = len(slots) * K
                    for m in ms:
                        for i in range(n):
                            slot, k = slots[i // K], i % K
                            mm = g.product(pe, two(ps_r)[m // 2][:, m % 2, :], [g.w(h, slot, k, m * P, P) for h in (g.w_hi, g.w_lo)],
                                           parts(i // K, k), i == 0, i == n - 1)
                    return mm

                def by_rows(to, left, slot):
                    for k in range(K):
                        mm = g.product(pe, to, left(k), [g.w(h, slot, k) for h in (g.w_hi, g.w_lo)], k == 0, k == K - 1)
                    return mm

                def step(j, s, on):
                    if on(1):
                        pe.wait_ge(x_lo, 4 * j)
                        wait(pe, v_ok, K * (j - 1))
                        by_columns([WR_SRC, WR_DST], lambda o, k: [h[:, o, k, :] for h in xt], range(K)).then_inc(r_mm, 1)
                    if on(2):
                        pe.wait_ge(score_ok, 2 * (j - 2) + 2)
                        wait(pe, msg_ok, 2 * j - 6)
                        for q in range(2):
                            tr = pe.transpose(ps_a[:, q * P:(q + 1) * P], score[:, q, :], g.ident[:])
                        tr.then_inc(a_t, 1)
                    if on(0):
                        turn(j, 0)
                    if on(1):
                        for q in range(2):
                            wait(pe, k_ok, 2 * (j - 2) + q + 1)
                            by_rows(ps_qk[q][:], lambda k: [h[:, 1, k, q * P:(q + 1) * P] for h in xt], WQ).then_inc(q_mm, 1)
                    if on(3):
                        pe.wait_ge(s_lo, j - 2)
                        pe.wait_ge(gap_ok, min(j - 1, NB) if isinstance(j, int) else j - 1)
                        for q in range(2):
                            wait(pe, msg_ok, 2 * (j - 4) + q + 1)
                            by_rows(ps_o[q][:], lambda k: [h[:, k, q * P:(q + 1) * P] for h in st], WO).then_inc(o_mm, 1)
                    if on(0):
                        turn(j, 1)
                    if on(1):
                        pe.wait_ge(r_lo, j)
                        by_columns([WV], lambda o, k: [h[:, k, :] for h in rt], range(K)).then_inc(v_mm, 1)
                        for q in range(2):
                            pe.wait_ge(q_ok, 2 * (j - 1) + q + 1)
                            by_rows(ps_qk[q][:], lambda k: [h[:, k, q * P:(q + 1) * P] for h in rt], WK).then_inc(k_mm, 1)
                sweep(pe, NB, 3, 2, 6, step)


def finish_stage(nc, g):
    sb, sem = g.sb, g.sem
    with ExitStack() as ctx:
        idx = sb(ctx, "fin_idx", [P, 4, 1], I32)
        consts = sb(ctx, "fin_consts", [P, 3, D])
        mean = sb(ctx, "fin_mean", [P, D])
        scale = sb(ctx, "fin_scale", [P, D])
        scale1 = sb(ctx, "fin_scale1", [P, D])
        shift = sb(ctx, "fin_shift", [P, D])
        tmp = sb(ctx, "fin_tmp", [P, D])
        x1 = sb(ctx, "fin_x1", [P, 4, D])
        ms = sb(ctx, "fin_msg", [P, 4, D])
        y = sb(ctx, "fin_y", [P, 4, D])
        stats = sb(ctx, "fin_stats", [P, 2, 6])
        mv = sb(ctx, "fin_mv", [P, 2, 4])
        root = sb(ctx, "fin_root", [P, 2, 1])
        ps = g.banks(ctx, "psf")

        const_in = g.const_in
        idx_ok, sums_ok, tot_ok, var_ok, std_ok, coef_ok = (sem(n) for n in (
            "fin_idx_ok", "fin_sums", "fin_totals", "fin_var", "fin_std", "fin_coef"))
        x_in = [sem(f"fin_x_in{s}") for s in range(4)]
        m_in = [sem(f"fin_m_in{s}") for s in range(4)]
        ax_ok, am_ok, y_ok, stat_ok, root_ok, scale_ok, norm_ok = (sem(n) for n in (
            "fin_x_scaled", "fin_m_scaled", "fin_y_ok", "fin_stat", "fin_root_ok", "fin_scale_ok", "fin_norm"))
        y_out = [sem(f"fin_out{s}") for s in range(4)]
        mine = g.step_v
        R = 4

        def reuse(eng, sems, j, s):
            if isinstance(j, int):
                wait(eng, sems[s], 16 * (j // R))
            else:
                eng.wait_ge(sems[s], (j - s) * 4)

        def arrived(eng, sems, j, s):
            if isinstance(j, int):
                eng.wait_ge(sems[s], 16 * (j // R) + 16)
            else:
                eng.wait_ge(sems[s], (j - s) * 4 + 16)

        with nc.Block() as block:

            @block.sync
            def _(sp):
                for i in range(3):
                    sp.dma_start(consts[:, i, :], g.rows[3 + i:4 + i, :].to_broadcast([P, D])).then_inc(const_in, 16)

                def step(j, s, on):
                    if on(0):
                        wait(sp, ax_ok, j - R + 1)
                        sp.dma_start(x1[:, s, :], g.x1_table[bass.ds(j * P, P), :]).then_inc(x_in[s], 16)
                    if on(3):
                        q = (s - 3) % R
                        sp.wait_ge(norm_ok, j - 2)
                        r = LAST if isinstance(j, int) and j - 3 == NT - 1 else P
                        sp.dma_start(g.out[bass.ds((j - 3) * P, r), :], y[0:r, q, :]).then_inc(y_out[q], 16)
                sweep(sp, NT, 3, R, R, step)
                sp.wait_ge(const_in, 128)
                for s in range(R):
                    sp.wait_ge(y_out[s], 16 * ((NT - 1 - s) // R + 1))

            @block.gpsimd
            def _(pool):
                def step(j, s, on):
                    if on(0):
                        wait(pool, y_ok, j - R + 1)
                        nc.gpsimd.tensor_copy(idx[:, s, :], g.last_edge[:, bass.ds(j, 1)]).then_inc(idx_ok, 1)
                        wait_alone(pool, idx_ok, j + 1, g.passed)
                        nc.gpsimd.indirect_dma_start(out=ms[:, s, :], out_offset=None, in_=g.msg_table,
                                                     in_offset=bass.IndirectOffsetOnAxis(ap=idx[:, s, :], axis=0)).then_inc(m_in[s], 16)
                    if on(1):
                        q = (s - 1) % R
                        if isinstance(j, int) and j == 1:
                            pool.wait_ge(coef_ok, 1)
                        arrived(pool, x_in, j - 1, q)
                        reuse(pool, y_out, j - 1, q)
                        nc.gpsimd.tensor_tensor(y[:, q, :], x1[:, q, :], scale1[:], ALU.mult).then_inc(ax_ok, 1)
                sweep(pool, NT, 1, R, R, step)

            @block.tensor
            def _(pe):
                pe.wait_ge(sums_ok, 2)
                pe.matmul(ps[0][:], g.ones[:], g.sum_y[:], start=True, stop=True).then_inc(tot_ok, 1)
                pe.matmul(ps[1][:], g.ones[:], g.sum_yy[:], start=True, stop=True).then_inc(tot_ok, 1)

            @block.scalar
            def _(act):
                act.wait_ge(var_ok, 1)
                nc.scalar.activation(tmp[:], tmp[:], ACT.Sqrt, bias=g.eps[:]).then_inc(std_ok, 1)

                def step(j, s, on):
                    if on(2):
                        q = (s - 2) % R
                        h = s % 2
                        act.wait_ge(stat_ok, 2 * (j - 2) + 2)
                        nc.scalar.activation(root[:, h, :], mv[:, h, 1:2], ACT.Sqrt, bias=g.eps[:]).then_inc(root_ok, 1)
                        act.wait_ge(scale_ok, 2 * (j - 2) + 2)
                        nc.scalar.activation(y[:, q, :], y[:, q, :], ACT.Identity, bias=mv[:, h, 3:4], scale=mv[:, h, 2:3]).then_inc(norm_ok, 1)
                sweep(act, NT, 2, R, R, step)

            @block.vector
            def _(dve):
                v = nc.vector
                steps = g.steps

                def then(ins):
                    steps[0] += 1
                    ins.then_inc(mine, 1)
                    dve.wait_ge(mine, steps[0])

                v.tensor_tensor(g.sum_y[:], g.sum_y[:], g.acc_x[:], ALU.add).then_inc(sums_ok, 1)
                v.tensor_tensor(g.sum_yy[:], g.sum_yy[:], g.acc_xx[:], ALU.add).then_inc(sums_ok, 1)
                dve.wait_ge(const_in, 128)
                dve.wait_ge(tot_ok, 2)
                then(v.tensor_scalar(mean[:], ps[0][:], 1.0 / N, None, ALU.mult))
                then(v.tensor_tensor(tmp[:], mean[:], mean[:], ALU.mult))
                then(v.scalar_tensor_tensor(tmp[:], ps[1][:], 1.0 / N, tmp[:], ALU.mult, ALU.subtract))
                v.tensor_scalar(tmp[:], tmp[:], 0.0, None, ALU.max).then_inc(var_ok, 1)
                then(v.tensor_tensor(mean[:], mean[:], consts[:, 0, :], ALU.add))
                then(v.tensor_tensor(mean[:], consts[:, 0, :], mean[:], ALU.subtract))
                dve.wait_ge(std_ok, 1)
                then(v.reciprocal(scale[:], tmp[:]))
                then(v.tensor_tensor(scale[:], scale[:], consts[:, 1, :], ALU.mult))
                v.tensor_scalar(scale1[:], scale[:], 1.0, None, ALU.add).then_inc(coef_ok, 1)
                then(v.tensor_tensor(shift[:], mean[:], scale[:], ALU.mult))
                then(v.tensor_tensor(shift[:], shift[:], consts[:, 2, :], ALU.add))

                def step(j, s, on):
                    if on(0):
                        arrived(dve, m_in, j, s)
                        v.tensor_tensor(ms[:, s, :], ms[:, s, :], scale[:], ALU.mult).then_inc(am_ok, 1)
                        dve.wait_ge(am_ok, 2 * j + 1)
                        v.tensor_tensor(ms[:, s, :], ms[:, s, :], shift[:], ALU.add).then_inc(am_ok, 1)
                        dve.wait_ge(ax_ok, j + 1)
                        dve.wait_ge(am_ok, 2 * j + 2)
                        v.tensor_tensor(y[:, s, :], y[:, s, :], ms[:, s, :], ALU.add).then_inc(y_ok, 1)
                    if on(0):
                        dve.wait_ge(y_ok, j + 1)
                        v.bn_stats(stats[:, s % 2, :], y[:, s, :]).then_inc(stat_ok, 1)
                    if on(1):
                        h = (s - 1) % 2
                        dve.wait_ge(root_ok, j)
                        v.reciprocal(mv[:, h, 2:3], root[:, h, :]).then_inc(scale_ok, 1)
                        dve.wait_ge(scale_ok, 2 * (j - 1) + 1)
                        v.scalar_tensor_tensor(mv[:, h, 3:4], mv[:, h, 0:1], -1.0, mv[:, h, 2:3], ALU.mult, ALU.mult).then_inc(scale_ok, 1)
                    if on(0):
                        wait(dve, norm_ok, j - 1)
                        wait_alone(dve, stat_ok, 2 * j + 1, g.passed)
                        v.bn_aggr(mv[:, s % 2, 0:2], stats[:, s % 2, :]).then_inc(stat_ok, 1)
                sweep(dve, NT, 1, R, R, step)


_OUTS = [((N, D), "float32")]


def kernel(**inputs):
    import numpy as np
    import concourse.bacc as bacc
    from concourse.bass_utils import run_bass_kernel_spmd

    a = {k: np.asarray(v) for k, v in inputs.items()}

    def padded(rows, n, fill=0):
        to = np.full((n,) + rows.shape[1:], fill, rows.dtype)
        to[:rows.shape[0]] = rows
        return to

    wr = a["L1_gnn_Wr"].T
    arrays = {
        "x": padded(a["x"], NP),
        "dst_in": padded(a["dst"].reshape(E, 1), EP + P, N),
        "src_in": padded(a["src"].reshape(E, 1), EP + P),
        "eid_in": np.arange(EP + P, dtype=np.int32).reshape(EP + P, 1),
        "ea": padded(a["edge_attr_512"], EP),
        "weights": np.concatenate([a["L0_gnn_W"], wr[2 * D:], wr[:D], wr[D:2 * D], a["L1_gnn_Wq"].T,
                                   a["L1_gnn_Wk"].T, a["L1_gnn_Wv"].T, a["L1_gnn_Wo"].T]),
        "br": a["L1_gnn_br"],
        "bv": a["L1_gnn_bv"],
        "rows": np.stack([a[n] for n in ("L0_gnn_b", "L1_gnn_bq", "L1_gnn_bk", "L1_gnn_bo", "L1_gnn_gamma", "L1_gnn_beta")]),
    }
    arrays = {f"in_{k}": np.ascontiguousarray(v) for k, v in arrays.items()}
    nc = bacc.Bacc("TRN2", target_bir_lowering=False, num_devices=1)
    args = [nc.dram_tensor(k, v.shape, mybir.dt.from_np(v.dtype), kind="ExternalInput").ap() for k, v in arrays.items()]
    out = nc.dram_tensor("out_0_dram", (N, D), F32, kind="ExternalOutput").ap()
    gnn_kernel(nc, *args, out)
    r = run_bass_kernel_spmd(nc, [arrays], core_ids=[0])
    return r.results[0]["out_0_dram"]
```

```python
from contextlib import ExitStack

import concourse.bass as bass
from concourse import mybir

F32 = mybir.dt.float32
F32R = mybir.dt.float32r
BF16 = mybir.dt.bfloat16
I32 = mybir.dt.int32
ALU = mybir.AluOpType
ACT = mybir.ActivationFunctionType
AX = mybir.AxisListType

P = 128
N = 10000
E = 5000
D = 512
H = 8
K = D // P
NT = -(-N // P)
NP = NT * P
ET = -(-E // P)
EP = ET * P
BE = 2 * P
NB = EP // BE
LAST = N - (NT - 1) * P
BITS = 7
EPS = 1e-5
NEG_SLOPE = 0.01
START = -1e30
WR_EDGE, W0, WR_SRC, WR_DST, WQ, WK, WV, WO = range(8)
NW = 8
WH = K * D // 2
LATER = 2 * (NW - 1)


def wait(eng, sem, count):
    if isinstance(count, int) and count <= 0:
        return
    eng.wait_ge(sem, count)


def wait_alone(eng, sem, count, passed):
    eng.wait_ge(sem, count)
    eng.sem_inc(passed, 1)


def landed(j, s, k, ring):
    if isinstance(j, int):
        return 16 * ((j - k) // ring + 1)
    return (j - s) * (16 // ring) + 16 * ((s - k) // ring + 1)


def sweep(eng, n, lag, unroll, head, step, split=None):
    end = head + (n - head) // unroll * unroll
    for j in range(head):
        step(j, j % unroll, lambda k, of=n, j=j: 0 <= j - k < of)
    bounds = [head, end] if split is None else [head, split, end]
    for first, last in zip(bounds, bounds[1:]):
        with eng.Fori(0, (last - first) // unroll) as i:
            for s in range(unroll):
                step(i * unroll + (first + s), s, lambda k, of=n, first=first: first < of)
    for j in range(end, n + lag):
        step(j, j % unroll, lambda k, of=n, j=j: 0 <= j - k < of)


class Shared:
    pass


def gnn_kernel(nc, x, dst_in, src_in, eid_in, ea, weights, br, bv, rows, out):

    g = Shared()
    g.x, g.dst_in, g.src_in, g.eid_in, g.ea, g.weights = x, dst_in, src_in, eid_in, ea, weights
    g.br, g.bv, g.rows, g.out = br, bv, rows, out

    def dram(name, shape, dt):
        return nc.dram_tensor(name, shape, dt, kind="Internal").ap()

    g.sdst = dram("sorted_dst", [EP + P, 1], I32)
    g.ssrc = dram("sorted_src", [EP + P, 1], I32)
    g.seid = dram("sorted_edge", [EP + P, 1], I32)
    g.dinv_table = dram("dinv_table", [NP, 1], F32)
    g.goes_row = dram("goes_row", [1, EP + 1], BF16)
    g.edge_part = dram("edge_part", [NB, P, K * BE], F32)
    g.sum_table = dram("sum_table", [EP + P, D], F32)
    g.x1_table = dram("x1_table", [NP, D], F32)
    g.coef_table = dram("coef_table", [NB, H, 2 * BE], F32)
    g.msg_table = dram("msg_table", [EP + P, D], F32)

    with ExitStack() as whole:

        def sem(name, ctx=whole):
            return ctx.enter_context(nc.semaphore(name))

        def sb(ctx, name, shape, dt=F32):
            return ctx.enter_context(nc.sbuf_tensor(name, shape, dt))

        def banks(ctx, name, n=8):
            return [ctx.enter_context(nc.psum_tensor(f"{name}{i}", [P, 512], F32)) for i in range(n)]

        g.passed = sem("wait_passed")
        g.const_in = sem("constants_loaded")
        g.step_v, g.steps = sem("vector_step"), [0]
        g.node_in = [sem(f"node_rows_in{s}") for s in range(8)]
        g.sum_in = [sem(f"sum_rows_in{s}") for s in range(4)]
        g.ea_in = [sem(f"ea_rows_in{s}") for s in range(4)]
        g.w_hi = sb(whole, "w_hi", [P, NW, K * D], F32R)
        g.w_lo = sb(whole, "w_lo", [P, NW, K * D], F32R)
        g.ident = sb(whole, "ident", [P, P])
        g.ones = sb(whole, "ones", [P, P])
        g.eps = sb(whole, "eps", [P, 1])
        g.dinv = sb(whole, "dinv", [P, NT])
        g.last_edge = sb(whole, "last_edge", [P, NT], I32)
        g.edge_idx = sb(whole, "edge_idx", [P, ET, 4], I32)
        g.is_last = sb(whole, "is_last", [P, ET])
        g.br_col = sb(whole, "br_col", [P, K])
        g.bv_col = sb(whole, "bv_col", [P, K])

        def w_half(to, i):
            return to[:].rearrange("p w n -> p (w n)")[:, bass.ds(i * WH, WH)]

        def load_half(eng, to, i):
            return eng.dma_start(to.rearrange("p (k n) -> p k n", k=K // 2),
                                 weights[bass.ds(i * (D // 2), D // 2), :].rearrange("(k p) n -> p k n", p=P))

        def w(half, slot, k, lo=0, n=D):
            return half[:, slot, k * D + lo:k * D + lo + n]

        def product(pe, to, left, right, first, last):
            pe.matmul(to, left[0], right[1], start=first, stop=False)
            pe.matmul(to, left[1], right[0], start=False, stop=False)
            return pe.matmul(to, left[0], right[0], start=False, stop=last)

        with ExitStack() as early:
            g.goes_on = sb(early, "goes_on", [P, EP], BF16)
            g.sb, g.sem, g.banks, g.w, g.product = sb, sem, banks, w, product
            g.w_half, g.load_half = w_half, load_half
            index_stage(nc, g)
            aggregate_stage(nc, g)
        g.acc_x = sb(whole, "acc_x", [P, D])
        g.acc_xx = sb(whole, "acc_xx", [P, D])
        g.sum_y = sb(whole, "sum_y", [P, D])
        g.sum_yy = sb(whole, "sum_yy", [P, D])
        node_stage(nc, g)
        edge_stage(nc, g)
        finish_stage(nc, g)


def index_stage(nc, g):
    sb, sem = g.sb, g.sem
    with ExitStack() as ctx:
        flat = sb(ctx, "flat_check", [ET, 2, P], I32)
        worse = sb(ctx, "worse", [ET, P])
        worse_row = sb(ctx, "worse_row", [ET, 1])
        unsorted_i = sb(ctx, "unsorted", [1, 1], I32)
        w_stage = sb(ctx, "w_stage", [P, 2, WH])
        dst_row = sb(ctx, "dst_row", [P, EP], I32)
        iota_row = sb(ctx, "iota_row", [P, P], BF16)
        upper = sb(ctx, "upper", [P, P])
        none_at = sb(ctx, "none_at", [P, NT])
        zero = sb(ctx, "zero_rows", [P, D])
        counting = ctx.enter_context(ExitStack())
        place_row = sb(counting, "place_row", [P, EP], mybir.dt.int16)
        one_row = g.goes_on
        cols = sb(counting, "cols", [P, 3, ET], I32)
        cols_f = sb(counting, "cols_f", [P, 3, ET])
        less = sb(counting, "less", [P, 2, ET])
        rank = sb(counting, "rank", [P, ET], I32)
        put = sb(counting, "put", [P, 4], I32)
        counting.close()
        flat_s = sb(ctx, "flat_sorted", [ET, 4, P], I32)
        flat_f = sb(ctx, "flat_float", [ET, 4, P])
        same = sb(ctx, "same_as_next", [ET, P + 1], BF16)
        cols_s = sb(ctx, "cols_sorted", [P, 4, ET], I32)
        low = sb(ctx, "node_low", [P, 2, ET], I32)
        high = sb(ctx, "node_high", [P, 2, ET], I32)
        parts = sb(ctx, "node_parts", [P, 2, ET], BF16)
        hot_low = sb(ctx, "hot_low", [P, ET, P], BF16)
        hot_high = sb(ctx, "hot_high", [P, ET, NT], BF16)
        cnt = sb(ctx, "cnt", [P, NT])
        small = sb(ctx, "small", [P, 8, NT])
        differs = sb(ctx, "differs", [P, ET])
        ps = g.banks(ctx, "psi")

        copied, checked_in = sem("tables_copied"), sem("check_loaded")
        worse_ok, flag_ps, flag_ok = sem("worse_summed"), sem("flag_in_psum"), sem("flag_ready")
        count_in, counted, rank_ok, put_ok, put_out = (sem(n) for n in ("count_loaded", "counted", "rank_ready", "put_staged", "put_written"))
        ordered, flat_in, row_in = sem("edges_ordered"), sem("flat_loaded"), sem("row_loaded")
        const_ok, const_in = sem("constants_made"), g.const_in
        flat_ok, cols_ok, hot_ok = sem("flat_as_float"), sem("columns_in_psum"), sem("one_hots_ready")
        hist_ok, cnt_ok, cum_ok, root_ok = (sem(n) for n in ("histogram_in_psum", "count_ready", "prefix_in_psum", "root_ready"))
        dinv_ok, start_ok, stored = sem("dinv_ready"), sem("start_ready"), sem("index_stored")
        w_in = [sem(f"weights_loaded{s}") for s in range(2)]
        w_hi_ok = sem("weights_high")
        step_v, step_p = g.step_v, sem("pool_step")
        zero_ok = sem("zero_rows_made")

        with nc.Block() as block:

            @block.sync
            def _(sp):
                for i in range(2):
                    sp.dma_start(flat[:, i, :], g.dst_in[i:i + EP, :].rearrange("(t p) c -> t (p c)", p=P)).then_inc(checked_in, 16)
                for to, of in ((g.sdst, g.dst_in), (g.ssrc, g.src_in), (g.seid, g.eid_in)):
                    sp.dma_start(to.rearrange("(a b) c -> a (b c)", a=16), of.rearrange("(a b) c -> a (b c)", a=16)).then_inc(copied, 16)
                sp.dma_start(g.br_col[:], g.br.rearrange("(k p) -> p k", p=P), allow_slow_non_contiguous=True).then_inc(const_in, 16)
                sp.dma_start(g.bv_col[:], g.bv.rearrange("(k p) -> p k", p=P), allow_slow_non_contiguous=True).then_inc(const_in, 16)
                sp.wait_ge(zero_ok, 1)
                sp.dma_start(g.sum_table[EP:EP + P, :], zero[:]).then_inc(stored, 16)
                sp.dma_start(g.msg_table[EP:EP + P, :], zero[:]).then_inc(stored, 16)
                sp.wait_ge(copied, 48)
                sp.wait_ge(ordered, 1)
                for i, (of, o) in enumerate(((g.sdst, 0), (g.ssrc, 0), (g.seid, 0), (g.sdst, 1))):
                    sp.dma_start(flat_s[:, i, :], of[o:o + EP, :].rearrange("(t p) c -> t (p c)", p=P)).then_inc(flat_in, 16)
                sp.wait_ge(start_ok, 2)
                sp.dma_start(g.goes_row[0:1, 0:1], same[0:1, P:P + 1]).then_inc(row_in, 16)
                sp.dma_start(g.goes_row[0:1, 1:EP + 1].rearrange("a (t p) -> (a t) p", p=P), same[:, 0:P]).then_inc(row_in, 16)
                sp.wait_ge(row_in, 32)
                sp.dma_start(g.goes_on[:], g.goes_row[0:1, 0:EP].to_broadcast([P, EP])).then_inc(stored, 16)
                sp.wait_ge(dinv_ok, 1)
                sp.dma_start(g.dinv_table.rearrange("(p j) c -> p (j c)", p=P), g.dinv[:]).then_inc(stored, 16)
                sp.wait_ge(const_in, 32)
                sp.wait_ge(stored, 64)

            @block.scalar
            def _(act):
                for i in range(2):
                    g.load_half(act, w_stage[:, i, :], i).then_inc(w_in[i], 16)
                for i in range(2):
                    act.wait_ge(w_in[i], 16)
                    nc.scalar.copy(g.w_half(g.w_hi, i), w_stage[:, i, :]).then_inc(w_hi_ok, 1)
                act.wait_ge(const_ok, 2)
                act.wait_ge(cnt_ok, 1)
                nc.scalar.activation(small[:, 0, :], cnt[:], ACT.Sqrt, bias=g.ones[:, 0:1]).then_inc(root_ok, 1)

            @block.gpsimd
            def _(pool):
                steps = [0]

                def then(ins):
                    steps[0] += 1
                    ins.then_inc(step_p, 1)
                    pool.wait_ge(step_p, steps[0])

                then(nc.gpsimd.memset(g.ones[:], 1.0))
                nc.gpsimd.memset(g.eps[:], EPS).then_inc(const_ok, 1)
                nc.gpsimd.affine_select(out=g.ident[:], in_=g.ones[:], compare_op=ALU.is_equal, fill=0.0, base=0, pattern=[[-1, P]], channel_multiplier=1).then_inc(const_ok, 1)
                nc.gpsimd.affine_select(out=upper[:], in_=g.ones[:], compare_op=ALU.is_ge, fill=0.0, base=0, pattern=[[1, P]], channel_multiplier=-1).then_inc(const_ok, 1)
                nc.gpsimd.iota(iota_row[:], [[1, P]], base=0, channel_multiplier=0, allow_small_or_imprecise_dtypes=True).then_inc(const_ok, 1)
                nc.gpsimd.iota(none_at[:], [[0, NT]], base=EP, channel_multiplier=1, allow_small_or_imprecise_dtypes=True).then_inc(const_ok, 1)
                nc.gpsimd.memset(zero[:], 0.0).then_inc(zero_ok, 1)
                pool.wait_ge(flag_ok, 1)
                flag = pool.value_load(unsorted_i[0:1, 0:1], min_val=0, max_val=EP)
                with pool.If(flag > 0):
                    pool.wait_ge(copied, 48)
                    nc.gpsimd.dma_start(dst_row[:], g.dst_in[0:EP, :].rearrange("e c -> (e c)").unsqueeze(0).to_broadcast([P, EP])).then_inc(count_in, 16)
                    for i, of in enumerate((g.dst_in, g.src_in, g.eid_in)):
                        nc.gpsimd.dma_start(cols[:, i, :], of[0:EP, :].rearrange("(t p) c -> p (t c)", p=P), allow_slow_non_contiguous=True).then_inc(count_in, 16)
                    nc.gpsimd.iota(place_row[:], [[1, EP]], base=0, channel_multiplier=0, allow_small_or_imprecise_dtypes=True).then_inc(counted, 1)
                    pool.wait_ge(rank_ok, 1)
                    with pool.Fori(0, ET) as t:
                        nc.gpsimd.tensor_copy(put[:, 0:3], cols[:, :, bass.ds(t, 1)].rearrange("p c t -> p (c t)")).then_inc(put_ok, 1)
                        nc.gpsimd.tensor_copy(put[:, 3:4], rank[:, bass.ds(t, 1)]).then_inc(put_ok, 1)
                        wait_alone(pool, put_ok, 2 * t + 2, g.passed)
                        for i, to in enumerate((g.sdst, g.ssrc, g.seid)):
                            nc.gpsimd.indirect_dma_start(out=to, out_offset=bass.IndirectOffsetOnAxis(ap=put[:, 3:4], axis=0), in_=put[:, i:i + 1], in_offset=None).then_inc(put_out, 16)
                        pool.wait_ge(put_out, 48 * t + 48)
                nc.gpsimd.engine_nop().then_inc(ordered, 1)
                for i in range(2):
                    pool.wait_ge(w_hi_ok, i + 1)
                    nc.gpsimd.tensor_tensor(g.w_half(g.w_lo, i), w_stage[:, i, :], g.w_half(g.w_hi, i).bitcast(F32), ALU.subtract)

            @block.tensor
            def _(pe):
                pe.wait_ge(const_ok, 5)
                pe.wait_ge(worse_ok, 2)
                pe.matmul(ps[0][0:1, 0:1], worse_row[:], g.ones[0:ET, 0:1], start=True, stop=True).then_inc(flag_ps, 1)
                pe.wait_ge(flat_ok, 1)
                for i in range(4):
                    pe.transpose(ps[1][:, i * ET:(i + 1) * ET], flat_f[:, i, :], g.ident[0:ET, 0:ET]).then_inc(cols_ok, 1)
                pe.wait_ge(hot_ok, 2)
                for t in range(ET):
                    mm = pe.matmul(ps[2][:, 0:NT], hot_low[:, t, :], hot_high[:, t, :], start=t == 0, stop=t == ET - 1)
                mm.then_inc(hist_ok, 1)
                pe.wait_ge(cnt_ok, 1)
                pe.matmul(ps[3][:, 0:NT], upper[:], cnt[:], start=True, stop=True).then_inc(cum_ok, 1)
                pe.matmul(ps[4][:, 0:NT], g.ones[:], cnt[:], start=True, stop=True).then_inc(cum_ok, 1)

            @block.vector
            def _(dve):
                steps = g.steps

                def then(ins):
                    steps[0] += 1
                    ins.then_inc(step_v, 1)
                    dve.wait_ge(step_v, steps[0])

                v = nc.vector
                dve.wait_ge(checked_in, 32)
                v.tensor_tensor(worse[:], flat[:, 0, :], flat[:, 1, :], ALU.is_gt).then_inc(worse_ok, 1)
                dve.wait_ge(worse_ok, 1)
                v.tensor_reduce(worse_row[:], worse[:], AX.X, ALU.add).then_inc(worse_ok, 1)
                dve.wait_ge(flag_ps, 1)
                v.tensor_copy(unsorted_i[:], ps[0][0:1, 0:1]).then_inc(flag_ok, 1)
                dve.wait_ge(flag_ok, 1)
                flag = dve.value_load(unsorted_i[0:1, 0:1], min_val=0, max_val=EP)
                with dve.If(flag > 0):
                    dve.wait_ge(count_in, 64)
                    dve.wait_ge(counted, 1)
                    v.tensor_copy(cols_f[:], cols[:]).then_inc(counted, 1)
                    dve.wait_ge(counted, 2)
                    with dve.Fori(0, ET) as t:
                        v.tensor_scalar(one_row[:], dst_row[:], cols_f[:, 0, bass.ds(t, 1)], 0.0, ALU.is_lt, ALU.add,
                                        accum_out=less[:, 0, bass.ds(t, 1)]).then_inc(counted, 1)
                        dve.wait_ge(counted, 3 * t + 3)
                        v.tensor_scalar(one_row[:], dst_row[:], cols_f[:, 0, bass.ds(t, 1)], None, ALU.is_equal).then_inc(counted, 1)
                        dve.wait_ge(counted, 3 * t + 4)
                        v.scalar_tensor_tensor(one_row[:], place_row[:], cols_f[:, 2, bass.ds(t, 1)], one_row[:], ALU.is_lt, ALU.mult,
                                               accum_out=less[:, 1, bass.ds(t, 1)]).then_inc(counted, 1)
                        dve.wait_ge(counted, 3 * t + 5)
                    v.tensor_tensor(rank[:], less[:, 0, :], less[:, 1, :], ALU.add).then_inc(rank_ok, 1)
                dve.wait_ge(flat_in, 64)
                v.tensor_copy(flat_f[:], flat_s[:]).then_inc(flat_ok, 1)
                v.memset(same[:, P:P + 1], 0.0).then_inc(start_ok, 1)
                v.tensor_tensor(same[:, 0:P], flat_s[:, 0, :], flat_s[:, 3, :], ALU.is_equal).then_inc(start_ok, 1)
                dve.wait_ge(cols_ok, 4)
                then(v.tensor_copy(cols_s[:], ps[1][:, 0:4 * ET].rearrange("p (c t) -> p c t", c=4)))
                v.tensor_tensor(differs[:], cols_s[:, 0, :], cols_s[:, 3, :], ALU.not_equal)
                v.tensor_scalar(high[:], cols_s[:, 0:2, :], BITS, None, ALU.logical_shift_right)
                then(v.tensor_scalar(low[:], cols_s[:, 0:2, :], P - 1, None, ALU.bitwise_and))
                v.tensor_copy(parts[:, 0, :], low[:, 0, :])
                then(v.tensor_copy(parts[:, 1, :], high[:, 0, :]))
                dve.wait_ge(const_ok, 5)
                v.tensor_tensor(hot_low[:], iota_row[:].unsqueeze(1).to_broadcast([P, ET, P]),
                                parts[:, 0, :].unsqueeze(2).to_broadcast([P, ET, P]), ALU.is_equal).then_inc(hot_ok, 1)
                v.tensor_tensor(hot_high[:], iota_row[:, 0:NT].unsqueeze(1).to_broadcast([P, ET, NT]),
                                parts[:, 1, :].unsqueeze(2).to_broadcast([P, ET, NT]), ALU.is_equal).then_inc(hot_ok, 1)
                v.scalar_tensor_tensor(g.is_last[:], cols_s[:, 0, :], float(N), differs[:], ALU.is_lt, ALU.mult)
                v.tensor_copy(g.edge_idx[:, :, 0], cols_s[:, 2, :])
                v.tensor_copy(g.edge_idx[:, :, 1], cols_s[:, 1, :])
                v.scalar_tensor_tensor(g.edge_idx[:, :, 2], low[:, 1, :], float(NT), high[:, 1, :], ALU.mult, ALU.add)
                v.tensor_copy(g.edge_idx[:, :, 3], cols_s[:, 0, :])
                dve.wait_ge(hist_ok, 1)
                v.tensor_copy(cnt[:], ps[2][:, 0:NT]).then_inc(cnt_ok, 1)
                deg, y, t = small[:, 1, :], small[:, 2, :], small[:, 3, :]
                dve.wait_ge(cnt_ok, 1)
                v.tensor_scalar(deg, cnt[:], 1.0, None, ALU.add)
                dve.wait_ge(root_ok, 1)
                then(v.reciprocal(y, small[:, 0, :]))
                then(v.tensor_tensor(t, y, y, ALU.mult))
                then(v.tensor_tensor(t, t, deg, ALU.mult))
                then(v.tensor_scalar(t, t, -0.5, 1.5, ALU.mult, ALU.add))
                v.tensor_tensor(g.dinv[:], y, t, ALU.mult).then_inc(dinv_ok, 1)
                dve.wait_ge(cum_ok, 2)
                a, b, c, e = (small[:, i, :] for i in range(4, 8))
                then(v.tensor_tensor_scan(a, g.ones[:, 0:NT], ps[4][:, 0:NT], 0.0, ALU.mult, ALU.add))
                then(v.tensor_tensor(b, a, ps[4][:, 0:NT], ALU.subtract))
                then(v.scalar_tensor_tensor(c, ps[3][:, 0:NT], -1.0, b, ALU.add, ALU.add))
                then(v.tensor_tensor(e, none_at[:], c, ALU.subtract))
                then(v.scalar_tensor_tensor(e, cnt[:], 0.0, e, ALU.is_equal, ALU.mult))
                then(v.tensor_tensor(g.last_edge[:], c, e, ALU.add))


def aggregate_stage(nc, g):
    sb, sem = g.sb, g.sem
    R = 4
    with ExitStack() as ctx:
        idx = sb(ctx, "agg_idx", [P, R, 3], I32)
        ea_rows = sb(ctx, "ea_rows", [P, R, D])
        x_rows = sb(ctx, "x_rows", [P, R, D])
        scaled = sb(ctx, "scaled_rows", [P, 2, D])
        dinv_src = sb(ctx, "dinv_src", [P, R, 1])
        ea_hi = sb(ctx, "ea_hi", [P, 2, K, BE], F32R)
        ea_lo = sb(ctx, "ea_lo", [P, 2, K, BE], F32R)
        run = sb(ctx, "run", [P, R, K, P])
        sums = sb(ctx, "sums", [P, 2, D])
        part = sb(ctx, "part", [P, K, BE])
        w_stage = sb(ctx, "w_stage_later", [P, 2, WH])
        ps = g.banks(ctx, "psa")
        ps_ea, ps_x, ps_back, ps_r = ps[0:2], ps[2:4], ps[4:6], ps[6:8]

        idx_ok = sem("agg_idx_staged")
        ea_in = g.ea_in
        x_in = [sem(f"x_rows_and_dinv_in{s}") for s in range(R)]
        scaled_ok, ea_t, x_t = sem("rows_scaled"), sem("ea_transposed"), sem("x_transposed")
        ea_hi_ok, ea_lo_ok, scan_ok, back_ok = (sem(n) for n in ("ea_high", "ea_low", "rows_summed", "sums_turned"))
        row_ok, row_out = sem("sum_rows_ready"), [sem(f"sum_rows_out{s}") for s in range(2)]
        r_mm, part_ok, part_out = sem("edge_part_in_psum"), sem("edge_part_ready"), sem("edge_part_out")

        w_in = [sem(f"weights_in{s}") for s in range(2)]
        w_hi_ok, w_lo_ok = sem("later_weights_high"), sem("later_weights_low")

        def by_k(row):
            return row.rearrange("p (k e) -> p k e", k=K)

        with nc.Block() as block:

            @block.gpsimd
            def _(pool):
                def step(t, s, on):
                    wait(pool, ea_t, t - R + 1)
                    wait(pool, scaled_ok, t - R + 1)
                    nc.gpsimd.tensor_copy(idx[:, s, :], g.edge_idx[:, bass.ds(t, 1), 0:3].rearrange("p t c -> p (t c)")).then_inc(idx_ok, 1)
                    wait_alone(pool, idx_ok, t + 1, g.passed)
                    for i, (to, of, n) in enumerate(((ea_rows, g.ea, ea_in), (x_rows, g.x, x_in), (dinv_src, g.dinv_table, x_in))):
                        nc.gpsimd.indirect_dma_start(out=to[:, s, :], out_offset=None, in_=of, in_offset=bass.IndirectOffsetOnAxis(ap=idx[:, s, i:i + 1], axis=0)).then_inc(n[s], 16)
                sweep(pool, ET, 0, R, R, step)

            @block.scalar
            def _(act):
                def step(j, s, on):
                    for q in range(2):
                        if on(0):
                            act.wait_ge(ea_t, 2 * j + q + 1)
                            wait(act, r_mm, j - 1)
                            nc.scalar.copy(ea_hi[:, s, :, q * P:(q + 1) * P], by_k(ps_ea[q][:])).then_inc(ea_hi_ok, 1)
                    for q in range(2):
                        if on(0):
                            act.wait_ge(x_in[2 * s + q], 2 * landed(j, s, 0, 2))
                            wait(act, x_t, 2 * (j - 1) + q + 1)
                            nc.scalar.activation(scaled[:, q, :], x_rows[:, 2 * s + q, :], ACT.Copy, scale=dinv_src[:, 2 * s + q, :]).then_inc(scaled_ok, 1)
                    if on(1):
                        act.wait_ge(r_mm, j)
                        wait(act, part_out, 16 * (j - 1))
                        for m in range(K):
                            nc.scalar.activation(part[:, m, :], ps_r[m // 2][:, (m % 2) * BE:(m % 2 + 1) * BE], ACT.Identity, bias=g.br_col[:, m:m + 1]).then_inc(part_ok, 1)
                        for q in range(2):
                            act.wait_ge(back_ok, 2 * (j - 1) + q + 1)
                            wait(act, row_out[q], 16 * (j - 1))
                            nc.scalar.copy(sums[:, q, :], ps_back[q][:]).then_inc(row_ok, 1)
                    if on(0, LATER):
                        wait_alone(act, w_in[s], landed(j, s, 0, 2), g.passed)
                        nc.scalar.copy(g.w_half(g.w_hi, j + 2), w_stage[:, s, :]).then_inc(w_hi_ok, 1)
                sweep(act, NB, 1, 2, 2, step, LATER)

            @block.vector
            def _(dve):
                v = nc.vector

                def step(j, s, on):
                    for q in range(2):
                        dve.wait_ge(ea_hi_ok, 2 * j + q + 1)
                        v.tensor_tensor(ea_lo[:, s, :, q * P:(q + 1) * P], by_k(ps_ea[q][:]),
                                        ea_hi[:, s, :, q * P:(q + 1) * P].bitcast(F32), ALU.subtract).then_inc(ea_lo_ok, 1)
                    for q in range(2):
                        t = 2 * j + q
                        dve.wait_ge(x_t, t + 1)
                        wait(dve, scan_ok, K * t)
                        wait(dve, back_ok, t - R + 1)
                        for k in range(K):
                            before = run[:, (2 * s + q - 1) % R, k, P - 1:P]
                            if isinstance(t, int) and t == 0:
                                before = 0.0
                            v.tensor_tensor_scan(run[:, 2 * s + q, k, :], g.goes_on[:, bass.ds(t * P, P)], ps_x[q][:, k * P:(k + 1) * P],
                                                 before, ALU.mult, ALU.add).then_inc(scan_ok, 1)
                    if on(0, LATER):
                        wait_alone(dve, w_hi_ok, j + 1, g.passed)
                        v.tensor_tensor(g.w_half(g.w_lo, j + 2), w_stage[:, s, :], g.w_half(g.w_hi, j + 2).bitcast(F32), ALU.subtract).then_inc(w_lo_ok, 1)
                sweep(dve, NB, 0, 2, 2, step, LATER)

            @block.tensor
            def _(pe):
                def step(j, s, on):
                    if on(0):
                        for q in range(2):
                            pe.wait_ge(ea_in[2 * s + q], landed(j, s, 0, 2))
                            wait(pe, ea_lo_ok, 2 * (j - 1) + q + 1)
                            for k in range(K):
                                tr = pe.transpose(ps_ea[q][:, k * P:(k + 1) * P], ea_rows[:, 2 * s + q, k * P:(k + 1) * P], g.ident[:])
                            tr.then_inc(ea_t, 1)
                    if on(1):
                        pe.wait_ge(ea_lo_ok, 2 * j)
                        wait(pe, part_ok, K * (j - 1))
                        for m in range(K):
                            to = ps_r[m // 2][:, (m % 2) * BE:(m % 2 + 1) * BE]
                            for k in range(K):
                                mm = g.product(pe, to, [g.w(h, WR_EDGE, k, m * P, P) for h in (g.w_hi, g.w_lo)],
                                               [h[:, 1 - s, k, :] for h in (ea_hi, ea_lo)], k == 0, k == K - 1)
                        mm.then_inc(r_mm, 1)
                    if on(0):
                        for q in range(2):
                            pe.wait_ge(scaled_ok, 2 * j + q + 1)
                            wait(pe, scan_ok, K * (2 * (j - 1) + q + 1))
                            for k in range(K):
                                tr = pe.transpose(ps_x[q][:, k * P:(k + 1) * P], scaled[:, q, k * P:(k + 1) * P], g.ident[:])
                            tr.then_inc(x_t, 1)
                    if on(1):
                        for q in range(2):
                            t = 2 * (j - 1) + q
                            pe.wait_ge(scan_ok, K * t + K)
                            wait(pe, row_ok, t - 1)
                            for k in range(K):
                                tr = pe.transpose(ps_back[q][:, k * P:(k + 1) * P], run[:, 2 * (1 - s) + q, k, :], g.ident[:])
                            tr.then_inc(back_ok, 1)
                sweep(pe, NB, 1, 2, 4, step)

            @block.sync
            def _(sp):
                for i in range(2):
                    g.load_half(sp, w_stage[:, i, :], i + 2).then_inc(w_in[i], 16)

                def step(b, s, on):
                    if on(0, LATER - 2):
                        sp.wait_ge(w_lo_ok, b + 1)
                        g.load_half(sp, w_stage[:, s, :], b + 4).then_inc(w_in[s], 16)
                    sp.wait_ge(part_ok, K * b + K)
                    sp.dma_start(g.edge_part[bass.ds(b, 1), :, :].rearrange("b p n -> (b p) n"), part[:].rearrange("p k e -> p (k e)")).then_inc(part_out, 16)
                    for q in range(2):
                        sp.wait_ge(row_ok, 2 * b + q + 1)
                        sp.dma_start(g.sum_table[bass.ds((2 * b + q) * P, P), :], sums[:, q, :]).then_inc(row_out[q], 16)
                sweep(sp, NB, 0, 2, 2, step, LATER - 2)
                for s in range(2):
                    sp.wait_ge(row_out[s], 16 * NB)
                sp.wait_ge(part_out, 16 * NB)


def node_stage(nc, g):
    sb, sem = g.sb, g.sem
    with ExitStack() as ctx:
        RX = 8
        RS = 4
        idx = sb(ctx, "node_idx", [P, RS, 1], I32)
        xr = sb(ctx, "node_x", [P, RX, D])
        rn = sb(ctx, "node_sum", [P, RS, D])
        gr = sb(ctx, "node_agg", [P, 2, D])
        g_hi = sb(ctx, "agg_hi", [P, 2, K, P], F32R)
        g_lo = sb(ctx, "agg_lo", [P, 2, K, P], F32R)
        z = sb(ctx, "node_z", [P, 2, D])
        y = sb(ctx, "node_y", [P, 2, D])
        x1 = sb(ctx, "node_x1", [P, 2, D])
        b_row = sb(ctx, "b_row", [P, D])
        stats = sb(ctx, "node_stats", [P, 2, 6])
        mv = sb(ctx, "node_mv", [P, 2, 4])
        root = sb(ctx, "node_root", [P, 2, 1])
        ps = g.banks(ctx, "psn")
        ps_t, ps_o = ps[0:2], ps[4:8]

        b_in, idx_ok = g.const_in, sem("node_idx_staged")
        x_in, rn_in = g.node_in, g.sum_in
        agg_even, agg_scaled, agg_odd = sem("node_agg_even"), sem("node_agg_odd_scaled"), sem("node_agg_odd")
        turned, hi_ok, lo_ok, mm_ok = (sem(n) for n in ("node_turned", "node_high", "node_low", "node_product"))
        z_ok, leaky_ok, y_ok, stat_ok, root_ok, scale_ok, x1_ok = (sem(n) for n in (
            "node_z_ok", "node_leaky", "node_y_ok", "node_stat", "node_root_ok", "node_scale", "x1_ok"))
        x1_out = [sem(f"x1_out{s}") for s in range(2)]

        def by_k(row):
            return row.rearrange("p (k e) -> p k e", k=K)

        def wait_agg(eng, i, s):
            if s % 2 == 0:
                wait(eng, agg_even, i + 2)
            else:
                wait(eng, agg_odd, i + 1)

        with nc.Block() as block:

            @block.sync
            def _(sp):
                sp.dma_start(b_row[:], g.rows[0:1, :].to_broadcast([P, D])).then_inc(b_in, 16)

                def step(j, s, on):
                    if on(0):
                        wait(sp, y_ok, j - RX + 1)
                        sp.dma_start(xr[:, s, :], g.x[bass.ds(j * P, P), :]).then_inc(x_in[s], 16)
                    if on(7):
                        sp.wait_ge(x1_ok, j - 6)
                        sp.dma_start(g.x1_table[bass.ds((j - 7) * P, P), :], x1[:, (s - 7) % 2, :]).then_inc(x1_out[(s - 7) % 2], 16)
                sweep(sp, NT, 7, 8, 8, step)
                sp.wait_ge(b_in, 48)
                for s in range(2):
                    sp.wait_ge(x1_out[s], 16 * ((NT + 1 - s) // 2))

            @block.gpsimd
            def _(pool):
                def step(j, s, on):
                    if on(2) and s % 2:
                        pool.wait_ge(agg_scaled, j - 1)
                        pool.wait_ge(rn_in[(s - 2) % RS], landed(j, s, 2, RS))
                        nc.gpsimd.tensor_tensor(gr[:, 1, :], gr[:, 1, :], rn[:, (s - 2) % RS, :], ALU.add).then_inc(agg_odd, 2)
                    if on(0):
                        wait_agg(pool, j - RS, s)
                        nc.gpsimd.tensor_copy(idx[:, s % RS, :], g.last_edge[:, bass.ds(j, 1)]).then_inc(idx_ok, 1)
                        wait_alone(pool, idx_ok, j + 1, g.passed)
                        nc.gpsimd.indirect_dma_start(out=rn[:, s % RS, :], out_offset=None, in_=g.sum_table,
                                                     in_offset=bass.IndirectOffsetOnAxis(ap=idx[:, s % RS, :], axis=0)).then_inc(rn_in[s % RS], 16)
                    if on(6):
                        pool.wait_ge(leaky_ok, j - 5)
                        wait(pool, x1_ok, j - 7)
                        nc.gpsimd.tensor_tensor(y[:, s % 2, :], z[:, s % 2, :], xr[:, (s - 6) % RX, :], ALU.add).then_inc(y_ok, 1)
                sweep(pool, NT, 6, 8, 8, step)
                for acc in (g.acc_x, g.acc_xx, g.sum_y, g.sum_yy):
                    nc.gpsimd.memset(acc[:], 0.0)

            @block.scalar
            def _(act):
                def step(j, s, on):
                    if on(2):
                        act.wait_ge(turned, j - 1)
                        wait(act, mm_ok, j - 3)
                        nc.scalar.copy(g_hi[:, s % 2, :, :], by_k(ps_t[s % 2][:])).then_inc(hi_ok, 1)
                    if on(1) and s % 2 == 0:
                        act.wait_ge(x_in[(s - 1) % RX], landed(j, s, 1, RX))
                        wait(act, turned, j - 2)
                        nc.scalar.activation(gr[:, 1, :], xr[:, (s - 1) % RX, :], ACT.Copy, scale=g.dinv[:, bass.ds(j - 1, 1)]).then_inc(agg_scaled, 2)
                    if on(7):
                        h = (s - 7) % 2
                        act.wait_ge(stat_ok, 2 * (j - 7) + 2)
                        nc.scalar.activation(root[:, h, :], mv[:, h, 1:2], ACT.Sqrt, bias=g.eps[:]).then_inc(root_ok, 1)
                        act.wait_ge(scale_ok, 2 * (j - 7) + 2)
                        wait(act, x1_out[h], landed(j, s, 9, 2))
                        nc.scalar.activation(x1[:, h, :], y[:, h, :], ACT.Identity, bias=mv[:, h, 3:4], scale=mv[:, h, 2:3]).then_inc(x1_ok, 1)
                sweep(act, NT, 7, 8, 16, step)

            @block.vector
            def _(dve):
                v = nc.vector
                dve.wait_ge(b_in, 48)

                def step(j, s, on):
                    h = s % 2
                    if on(2) and h == 0:
                        dve.wait_ge(x_in[(s - 2) % RX], landed(j, s, 2, RX))
                        dve.wait_ge(rn_in[(s - 2) % RS], landed(j, s, 2, RS))
                        wait(dve, turned, j - 3)
                        v.scalar_tensor_tensor(gr[:, h, :], xr[:, (s - 2) % RX, :], g.dinv[:, bass.ds(j - 2, 1)], rn[:, (s - 2) % RS, :], ALU.mult, ALU.add).then_inc(agg_even, 2)
                    if on(5):
                        q = (s - 5) % 2
                        dve.wait_ge(mm_ok, j - 4)
                        wait(dve, y_ok, j - 6)
                        v.scalar_tensor_tensor(z[:, q, :], ps_o[(s - 5) % 4][:], g.dinv[:, bass.ds(j - 5, 1)], b_row[:], ALU.mult, ALU.add).then_inc(z_ok, 1)
                    if on(7):
                        m = (s - 7) % 2
                        dve.wait_ge(y_ok, j - 6)
                        wait(dve, x1_ok, j - 8)
                        v.bn_stats(stats[:, m, :], y[:, m, :]).then_inc(stat_ok, 1)
                    if on(5):
                        dve.wait_ge(z_ok, j - 4)
                        v.scalar_tensor_tensor(z[:, q, :], z[:, q, :], NEG_SLOPE, z[:, q, :], ALU.mult, ALU.max).then_inc(leaky_ok, 1)
                    if on(7):
                        wait_alone(dve, stat_ok, 2 * (j - 7) + 1, g.passed)
                        v.bn_aggr(mv[:, m, 0:2], stats[:, m, :]).then_inc(stat_ok, 1)
                    if on(2):
                        dve.wait_ge(hi_ok, j - 1)
                        v.tensor_tensor(g_lo[:, h, :, :], by_k(ps_t[h][:]), g_hi[:, h, :, :].bitcast(F32), ALU.subtract).then_inc(lo_ok, 1)
                    if on(7):
                        dve.wait_ge(root_ok, j - 6)
                        v.reciprocal(mv[:, m, 2:3], root[:, m, :]).then_inc(scale_ok, 1)
                        dve.wait_ge(scale_ok, 2 * (j - 7) + 1)
                        v.scalar_tensor_tensor(mv[:, m, 3:4], mv[:, m, 0:1], -1.0, mv[:, m, 2:3], ALU.mult, ALU.mult).then_inc(scale_ok, 1)
                sweep(dve, NT, 7, 8, 16, step)

            @block.tensor
            def _(pe):
                def step(j, s, on):
                    if on(2):
                        wait_agg(pe, j - 2, s)
                        wait(pe, lo_ok, j - 3)
                        for k in range(K):
                            tr = pe.transpose(ps_t[s % 2][:, k * P:(k + 1) * P], gr[:, s % 2, k * P:(k + 1) * P], g.ident[:])
                        tr.then_inc(turned, 1)
                    if on(3):
                        q = (s - 3) % 2
                        pe.wait_ge(lo_ok, j - 2)
                        wait(pe, z_ok, j - 6)
                        for k in range(K):
                            mm = g.product(pe, ps_o[(s - 3) % 4][:], [h[:, q, k, :] for h in (g_hi, g_lo)],
                                           [g.w(h, W0, k) for h in (g.w_hi, g.w_lo)], k == 0, k == K - 1)
                        mm.then_inc(mm_ok, 1)
                sweep(pe, NT, 3, 8, 8, step)


def edge_stage(nc, g):
    sb, sem = g.sb, g.sem
    SN = 4
    with ExitStack() as ctx:
        idx = sb(ctx, "edge_gather_idx", [P, 2, 2], I32)
        idx2 = sb(ctx, "edge_gather_idx2", [P, 2, 1], I32)
        rows = sb(ctx, "edge_rows", [P, 2, 2, D])
        again = sb(ctx, "dst_rows_again", [P, 2, D])
        part = sb(ctx, "part_in", [P, 2, K, BE])
        vt = sb(ctx, "v_turned", [P, 2, K, BE])
        coef = sb(ctx, "coef_all", [P, K, 2, BE])
        carry = sb(ctx, "carry", [P, K])
        q_rows = sb(ctx, "q_rows", [P, 2, D])
        k_rows = sb(ctx, "k_rows", [P, 2, D])
        score = sb(ctx, "score", [P, 2, H])
        goes_b = sb(ctx, "goes_b", [H, 2, BE], BF16)
        start_b = sb(ctx, "start_b", [H, BE])
        top = sb(ctx, "top", [H, 2, BE + 1])
        total = sb(ctx, "total", [H, 2, BE + 1])
        expo = sb(ctx, "expo", [H, 2, BE])
        msg = sb(ctx, "msg_rows", [P, 2, D])
        node = sb(ctx, "node_rows", [P, SN, D])
        bq_row = sb(ctx, "bq_row", [P, D])
        bk_row = sb(ctx, "bk_row", [P, D])
        ps = g.banks(ctx, "pse")
        ps_r, ps_qk, ps_t, ps_o = ps[0:2], ps[2:4], ps[4:6], ps[6:8]

        def scores(b):
            bank = ps_t[1] if isinstance(b, int) and b == NB - 1 else ps_o[1]
            return bank[0:H, 0:BE]

        xt = [h[:, W0, :].rearrange("p (o k e) -> p o k e", o=2, k=K) for h in (g.w_hi, g.w_lo)]
        rt = [h[:, WR_EDGE, 0:K * BE].rearrange("p (k e) -> p k e", k=K) for h in (g.w_hi, g.w_lo)]
        st = [h[:, WR_EDGE, K * BE:].rearrange("p (k e) -> p k e", k=K) for h in (g.w_hi, g.w_lo)]

        def two(banks):
            return [b[:].rearrange("p (m e) -> p m e", m=2) for b in banks]

        const_in, init_ok = g.const_in, sem("edge_init")
        idx_ok, again_idx = sem("edge_idx_ok"), sem("again_idx_ok")
        rows_in = [sem(f"rows_in{s}") for s in range(2)]
        again_in = [sem(f"again_in{s}") for s in range(2)]
        part_in = [sem(f"part_and_starts_in{s}") for s in range(2)]
        turned, x_hi, x_lo = sem("x_turned"), sem("x_high"), sem("x_low")
        r_mm, r_sum, r_hi, r_lo = sem("r_product"), sem("r_summed"), sem("r_high"), sem("r_low")
        q_mm, q_ok, k_mm, k_ok = sem("q_product"), sem("q_rows_ok"), sem("k_product"), sem("k_rows_ok")
        v_mm, v_ok = sem("v_product"), sem("v_ok")
        qk_ok, score_ok, a_t = sem("qk_multiplied"), sem("score_ok"), sem("score_turned")
        gap_ok, exp_ok, cp_ok = sem("gaps_ok"), sem("exp_ok"), sem("coef_ok")
        cp_out, coef_in = sem("coef_stored"), sem("coef_in")
        mul_ok, scan_ok, s_hi, s_lo = sem("v_weighted"), sem("v_summed"), sem("sum_high"), sem("sum_low")
        o_mm, msg_ok, cross_ok, cross2, added = (sem(n) for n in ("o_product", "msg_ok", "cross_ok", "cross_times_msg", "msg_added"))
        msg_out = [sem(f"msg_out{s}") for s in range(2)]
        node_in = sem("node_in")
        sq_ok, sq_added, x_added = sem("square_ok"), sem("square_added"), sem("node_added")
        mine = sem("edge_vector_step")
        MINE = 5

        def nodes_up_to(b):
            return min(SN * (b + 1), NT) if isinstance(b, int) else SN * (b + 1)

        def n_nodes(i):
            return LAST if isinstance(i, int) and i == NT - 1 else P

        with nc.Block() as block:

            @block.sync
            def _(sp):
                sp.dma_start(bq_row[:], g.rows[1:2, :].to_broadcast([P, D])).then_inc(const_in, 16)
                sp.dma_start(bk_row[:], g.rows[2:3, :].to_broadcast([P, D])).then_inc(const_in, 16)

                def step(j, s, on):
                    if on(0):
                        wait(sp, r_lo, j - 1)
                        wait(sp, gap_ok, j - 1)
                        sp.dma_start(part[:, s, :, :].rearrange("p k e -> p (k e)"), g.edge_part[bass.ds(j, 1), :, :].rearrange("b p n -> (b p) n")).then_inc(part_in[s], 16)
                        sp.dma_start(goes_b[:, s, :], g.goes_row[0:1, bass.ds(j * BE, BE)].to_broadcast([H, BE])).then_inc(part_in[s], 16)
                    if on(2):
                        wait(sp, scan_ok, K * (j - 2))
                        sp.wait_ge(cp_ok, j - 1)
                        c = g.coef_table[bass.ds(j - 2, 1), :, :].rearrange("b h n -> (b h) n")
                        sp.dma_start(c, expo[:].rearrange("h c e -> h (c e)")).then_inc(cp_out, 16)
                        sp.wait_ge(cp_out, 16 * (j - 2) + 16)
                        for half in range(2):
                            of = c.rearrange("(k two) n -> two k n", two=2)[half:half + 1, :, :]
                            sp.dma_start(coef[half * 64:(half + 1) * 64, :, :, :].rearrange("p k c e -> p k (c e)"),
                                         of.to_broadcast([64, K, 2 * BE])).then_inc(coef_in, 16)
                    if on(3):
                        for q in range(2):
                            sp.wait_ge(msg_ok, 2 * (j - 3) + q + 1)
                            sp.dma_start(g.msg_table[bass.ds((j - 3) * BE + q * P, P), :], msg[:, q, :]).then_inc(msg_out[q], 16)
                    if on(1):
                        wait(sp, sq_added, SN * (j - 1))
                        for q in range(SN):
                            i = (j - 1) * SN + q
                            if isinstance(i, int) and i >= NT:
                                continue
                            sp.dma_start(node[:, q, :], g.x1_table[bass.ds(i * P, P), :]).then_inc(node_in, 16)
                sweep(sp, NB, 3, 2, 6, step)
                sp.wait_ge(const_in, 80)
                for q in range(2):
                    sp.wait_ge(msg_out[q], 16 * NB)

            @block.gpsimd
            def _(pool):
                nc.gpsimd.memset(carry[:], 0.0).then_inc(init_ok, 1)
                nc.gpsimd.memset(top[:, :, 0:1], 0.0).then_inc(init_ok, 1)
                nc.gpsimd.memset(total[:, :, 0:1], 0.0).then_inc(init_ok, 1)

                def gather(j, q):
                    t = 2 * j + q
                    if not (isinstance(j, int) and j == 0):
                        pool.wait_ge(turned, 4 * (j - 1) + 3 + q)
                    nc.gpsimd.tensor_copy(idx[:, q, 0:1], g.edge_idx[:, bass.ds(t, 1), 1]).then_inc(idx_ok, 1)
                    nc.gpsimd.tensor_copy(idx[:, q, 1:2], g.edge_idx[:, bass.ds(t, 1), 3]).then_inc(idx_ok, 1)
                    wait_alone(pool, idx_ok, 2 * t + 2, g.passed)
                    for o in range(2):
                        nc.gpsimd.indirect_dma_start(out=rows[:, q, o, :], out_offset=None, in_=g.x1_table,
                                                     in_offset=bass.IndirectOffsetOnAxis(ap=idx[:, q, o:o + 1], axis=0)).then_inc(rows_in[q], 16)

                def step(j, s, on):
                    if on(0):
                        gather(j, 0)
                        gather(j, 1)
                    if on(2):
                        for q in range(2):
                            pool.wait_ge(k_ok, 2 * (j - 2) + q + 1)
                            nc.gpsimd.tensor_tensor(k_rows[:, q, :], k_rows[:, q, :], q_rows[:, q, :], ALU.mult).then_inc(qk_ok, 1)
                    if on(4):
                        for q in range(2):
                            t = 2 * (j - 4) + q
                            pool.wait_ge(cross_ok, t + 1)
                            nc.gpsimd.tensor_tensor(again[:, q, :], again[:, q, :], msg[:, q, :], ALU.mult).then_inc(cross2, 1)
                            wait(pool, added, 2 * t)
                            if not (isinstance(j, int) and j >= NB + 2):
                                nc.gpsimd.tensor_tensor(g.sum_y[:], g.sum_y[:], msg[:, q, :], ALU.add).then_inc(added, 1)
                            pool.wait_ge(cross2, t + 1)
                            nc.gpsimd.tensor_tensor(g.sum_yy[:], g.sum_yy[:], again[:, q, :], ALU.add).then_inc(added, 1)
                    if on(3):
                        for q in range(2):
                            t = 2 * (j - 3) + q
                            wait(pool, added, 2 * (t - 2) + 2)
                            nc.gpsimd.tensor_copy(idx2[:, q, :], g.edge_idx[:, bass.ds(t, 1), 3]).then_inc(again_idx, 1)
                            wait_alone(pool, again_idx, t + 1, g.passed)
                            nc.gpsimd.indirect_dma_start(out=again[:, q, :], out_offset=None, in_=g.x1_table,
                                                         in_offset=bass.IndirectOffsetOnAxis(ap=idx2[:, q, :], axis=0)).then_inc(again_in[q], 16)
                    if on(2):
                        pool.wait_ge(node_in, 16 * nodes_up_to(j - 2))
                        for q in range(SN):
                            i = (j - 2) * SN + q
                            if isinstance(i, int) and i >= NT:
                                continue
                            wait(pool, x_added, i)
                            r = slice(0, n_nodes(i))
                            nc.gpsimd.tensor_tensor(g.acc_x[r, :], g.acc_x[r, :], node[r, q, :], ALU.add).then_inc(x_added, 1)
                sweep(pool, NB, 4, 2, 6, step)

            @block.scalar
            def _(act):
                def high(j, o):
                    if not (isinstance(j, int) and j == 0):
                        act.wait_ge(r_mm, j) if o == 0 else act.wait_ge(q_mm, 2 * j)
                    for q in range(2):
                        act.wait_ge(turned, 4 * j + 2 * o + q + 1)
                        nc.scalar.copy(xt[0][:, o, :, q * P:(q + 1) * P], ps_t[q][:].rearrange("p (k e) -> p k e", k=K)).then_inc(x_hi, 1)

                def step(j, s, on):
                    if on(0):
                        high(j, 0)
                    if on(2):
                        act.wait_ge(gap_ok, j - 1)
                        nc.scalar.activation(expo[:], expo[:], ACT.Exp, scale=float(D // H) ** -0.5).then_inc(exp_ok, 1)
                    if on(1):
                        act.wait_ge(r_sum, 2 * j)
                        nc.scalar.copy(rt[0], part[:, (s - 1) % 2, :, :]).then_inc(r_hi, 1)
                    if on(2):
                        for q in range(SN):
                            i = (j - 2) * SN + q
                            if isinstance(i, int) and i >= NT:
                                continue
                            act.wait_ge(x_added, i + 1)
                            r = slice(0, n_nodes(i))
                            nc.scalar.activation(node[r, q, :], node[r, q, :], ACT.Square).then_inc(sq_ok, 1)
                    if on(3):
                        for q in range(2):
                            t = 2 * (j - 3) + q
                            act.wait_ge(o_mm, t + 1)
                            wait(act, msg_out[q], 16 * (j - 3))
                            wait(act, added, 2 * (t - 2) + 2)
                            nc.scalar.activation(msg[:, q, :], ps_o[q][:], ACT.Copy, scale=g.is_last[:, bass.ds(t, 1)]).then_inc(msg_ok, 1)
                    if on(0):
                        high(j, 1)
                    if on(2):
                        act.wait_ge(scan_ok, K * (j - 2) + K)
                        wait(act, o_mm, 2 * (j - 2))
                        nc.scalar.copy(st[0], vt[:, s, :, :]).then_inc(s_hi, 1)
                    if on(1):
                        act.wait_ge(v_mm, j)
                        wait(act, s_lo, j - 2)
                        for m in range(K):
                            nc.scalar.activation(vt[:, (s - 1) % 2, m, :], two(ps_r)[m // 2][:, m % 2, :], ACT.Identity, bias=g.bv_col[:, m:m + 1]).then_inc(v_ok, 1)
                sweep(act, NB, 3, 2, 6, step)

            @block.vector
            def _(dve):
                v = nc.vector
                dve.wait_ge(const_in, 80)
                dve.wait_ge(init_ok, 3)

                def low(j, o):
                    for q in range(2):
                        dve.wait_ge(x_hi, 4 * j + 2 * o + q + 1)
                        v.tensor_tensor(xt[1][:, o, :, q * P:(q + 1) * P], ps_t[q][:].rearrange("p (k e) -> p k e", k=K),
                                        xt[0][:, o, :, q * P:(q + 1) * P].bitcast(F32), ALU.subtract).then_inc(x_lo, 1)

                def maxima(b, s):
                    dve.wait_ge(a_t, b + 1)
                    dve.wait_ge(part_in[s], 2 * landed(b, s, 0, 2))
                    m, st0 = top[:, s, :], start_b[:]
                    v.tensor_scalar(st0, goes_b[:, s, :], 1.0, -START, ALU.subtract, ALU.mult).then_inc(mine, 1)
                    dve.wait_ge(mine, MINE * b + 1)
                    v.tensor_tensor_scan(m[:, 1:], st0, scores(b), m[:, 0:1], ALU.add, ALU.max).then_inc(mine, 1)
                    dve.wait_ge(mine, MINE * b + 2)
                    wait(dve, cp_out, 16 * b)
                    v.tensor_copy(top[:, 1 - s, 0:1], m[:, BE:BE + 1])
                    v.tensor_tensor(expo[:, 0, :], m[:, 0:BE], st0, ALU.add).then_inc(mine, 1)
                    dve.wait_ge(mine, MINE * b + 3)
                    v.tensor_tensor(expo[:, 0, :], expo[:, 0, :], m[:, 1:], ALU.subtract)
                    v.tensor_tensor(expo[:, 1, :], scores(b), m[:, 1:], ALU.subtract).then_inc(gap_ok, 1)

                def coefficients(b, s):
                    z = total[:, s, :]
                    dve.wait_ge(exp_ok, b + 1)
                    v.tensor_tensor_scan(z[:, 1:], expo[:, 0, :], expo[:, 1, :], z[:, 0:1], ALU.mult, ALU.add).then_inc(mine, 1)
                    dve.wait_ge(mine, MINE * b + 4)
                    v.tensor_copy(total[:, 1 - s, 0:1], z[:, BE:BE + 1])
                    v.tensor_tensor(expo[:, 0, :], expo[:, 0, :], z[:, 0:BE], ALU.mult)
                    v.reciprocal(start_b[:], z[:, 1:]).then_inc(mine, 1)
                    dve.wait_ge(mine, MINE * b + 5)
                    v.tensor_tensor(expo[:], expo[:], start_b[:].unsqueeze(1).to_broadcast([H, 2, BE]), ALU.mult).then_inc(cp_ok, 1)

                def sum_low(j, s):
                    dve.wait_ge(s_hi, j - 1)
                    v.tensor_tensor(st[1], vt[:, s, :, :], st[0].bitcast(F32), ALU.subtract).then_inc(s_lo, 1)

                def step(j, s, on):
                    at_end = isinstance(j, int) and j == NB + 1
                    if on(2):
                        for q in range(2):
                            t = 2 * (j - 2) + q
                            dve.wait_ge(k_mm, t + 1)
                            v.tensor_tensor(k_rows[:, q, :], ps_qk[q][:], bk_row[:], ALU.add).then_inc(k_ok, 1)
                    if on(4):
                        for q in range(2):
                            t = 2 * (j - 4) + q
                            dve.wait_ge(msg_ok, t + 1)
                            dve.wait_ge(again_in[q], 16 * (j - 4) + 16)
                            v.scalar_tensor_tensor(again[:, q, :], again[:, q, :], 2.0, msg[:, q, :], ALU.mult, ALU.add).then_inc(cross_ok, 1)
                            if isinstance(j, int) and j >= NB + 2:
                                dve.wait_ge(added, 2 * t)
                                v.tensor_tensor(g.sum_y[:], g.sum_y[:], msg[:, q, :], ALU.add).then_inc(added, 1)
                    if on(2):
                        for q in range(2):
                            t = 2 * (j - 2) + q
                            dve.wait_ge(qk_ok, t + 1)
                            wait(dve, a_t, j - 2)
                            v.tensor_reduce(score[:, q, :], k_rows[:, q, :].rearrange("p (h d) -> p h d", h=H), AX.X, ALU.add).then_inc(score_ok, 1)
                        maxima(j - 2, s)
                    if on(1):
                        dve.wait_ge(r_mm, j)
                        dve.wait_ge(part_in[(s - 1) % 2], 2 * landed(j, s, 1, 2))
                        r = part[:, (s - 1) % 2, :, :]
                        for h in range(2):
                            v.tensor_tensor(r[:, 2 * h:2 * h + 2, :], two(ps_r)[h], r[:, 2 * h:2 * h + 2, :], ALU.add).then_inc(r_sum, 1)
                    if on(0):
                        low(j, 0)
                    if on(2):
                        coefficients(j - 2, s)
                    if on(1):
                        dve.wait_ge(r_hi, j)
                        v.tensor_tensor(rt[1], r, rt[0].bitcast(F32), ALU.subtract).then_inc(r_lo, 1)
                        for q in range(2):
                            dve.wait_ge(q_mm, 2 * (j - 1) + q + 1)
                            wait(dve, qk_ok, 2 * (j - 2) + q + 1)
                            v.tensor_tensor(q_rows[:, q, :], ps_qk[q][:], bq_row[:], ALU.add).then_inc(q_ok, 1)
                    if on(0):
                        low(j, 1)
                    if on(2):
                        dve.wait_ge(coef_in, 32 * (j - 2) + 32)
                        dve.wait_ge(v_ok, K * (j - 2) + K)
                        v.tensor_tensor(vt[:, s, :, :], vt[:, s, :, :], coef[:, :, 1, :], ALU.mult).then_inc(mul_ok, 1)
                        dve.wait_ge(mul_ok, 2 * (j - 2) + 1)
                        for m in range(K):
                            v.tensor_tensor_scan(vt[:, s, m, :], coef[:, m, 0, :], vt[:, s, m, :], carry[:, m:m + 1], ALU.mult, ALU.add).then_inc(scan_ok, 1)
                        dve.wait_ge(scan_ok, K * (j - 2) + K)
                        v.tensor_copy(carry[:], vt[:, s, :, BE - 1]).then_inc(mul_ok, 1)
                        if at_end:
                            sum_low(j, s)
                        for q in range(SN):
                            i = (j - 2) * SN + q
                            if isinstance(i, int) and i >= NT:
                                continue
                            dve.wait_ge(sq_ok, i + 1)
                            wait(dve, sq_added, i)
                            r = slice(0, n_nodes(i))
                            v.tensor_tensor(g.acc_xx[r, :], g.acc_xx[r, :], node[r, q, :], ALU.add).then_inc(sq_added, 1)
                        if not at_end:
                            sum_low(j, s)
                sweep(dve, NB, 4, 2, 6, step)

            @block.tensor
            def _(pe):
                def turn(j, o):
                    for q in range(2):
                        i = 4 * j + 2 * o + q
                        pe.wait_ge(rows_in[q], 32 * j + 32)
                        wait(pe, x_lo, i - 1)
                        for k in range(K):
                            tr = pe.transpose(ps_t[q][:, k * P:(k + 1) * P], rows[:, q, o, k * P:(k + 1) * P], g.ident[:])
                        tr.then_inc(turned, 1)

                def by_columns(slots, parts, ms):
                    n = len(slots) * K
                    for m in ms:
                        for i in range(n):
                            slot, k = slots[i // K], i % K
                            mm = g.product(pe, two(ps_r)[m // 2][:, m % 2, :], [g.w(h, slot, k, m * P, P) for h in (g.w_hi, g.w_lo)],
                                           parts(i // K, k), i == 0, i == n - 1)
                    return mm

                def by_rows(to, left, slot):
                    for k in range(K):
                        mm = g.product(pe, to, left(k), [g.w(h, slot, k) for h in (g.w_hi, g.w_lo)], k == 0, k == K - 1)
                    return mm

                def turn_scores(j):
                    pe.wait_ge(score_ok, 2 * (j - 2) + 2)
                    wait(pe, msg_ok, 2 * j - 6)
                    for q in range(2):
                        tr = pe.transpose(scores(j - 2)[:, q * P:(q + 1) * P], score[:, q, :], g.ident[:])
                    tr.then_inc(a_t, 1)

                def messages(j, q):
                    wait(pe, msg_ok, 2 * (j - 4) + q + 1)
                    if q == 0:
                        pe.wait_ge(s_lo, j - 2)
                    elif isinstance(j, int) and j > NB:
                        pe.wait_ge(gap_ok, NB - 1)
                    else:
                        pe.wait_ge(gap_ok, j - 1)
                    by_rows(ps_o[q][:], lambda k: [h[:, k, q * P:(q + 1) * P] for h in st], WO).then_inc(o_mm, 1)

                def step(j, s, on):
                    at_end = isinstance(j, int) and j == NB + 1
                    if on(1):
                        pe.wait_ge(x_lo, 4 * j)
                        wait(pe, v_ok, K * (j - 1))
                        by_columns([WR_SRC, WR_DST], lambda o, k: [h[:, o, k, :] for h in xt], range(K)).then_inc(r_mm, 1)
                    if on(2) and not at_end:
                        turn_scores(j)
                    if on(0):
                        turn(j, 0)
                    if on(1):
                        for q in range(2):
                            wait(pe, k_ok, 2 * (j - 2) + q + 1)
                            by_rows(ps_qk[q][:], lambda k: [h[:, 1, k, q * P:(q + 1) * P] for h in xt], WQ).then_inc(q_mm, 1)
                    if on(3):
                        messages(j, 0)
                        if at_end:
                            turn_scores(j)
                        messages(j, 1)
                    if on(0):
                        turn(j, 1)
                    if on(1):
                        pe.wait_ge(r_lo, j)
                        by_columns([WV], lambda o, k: [h[:, k, :] for h in rt], range(K)).then_inc(v_mm, 1)
                        for q in range(2):
                            pe.wait_ge(q_ok, 2 * (j - 1) + q + 1)
                            by_rows(ps_qk[q][:], lambda k: [h[:, k, q * P:(q + 1) * P] for h in rt], WK).then_inc(k_mm, 1)
                sweep(pe, NB, 3, 2, 6, step)


def finish_stage(nc, g):
    sb, sem = g.sb, g.sem
    R = 8
    RY = 4
    SHARE = 4
    with ExitStack() as ctx:
        idx = sb(ctx, "fin_idx", [P, R, 1], I32)
        consts = sb(ctx, "fin_consts", [P, 3, K])
        mean = sb(ctx, "fin_mean", [P, K])
        var = sb(ctx, "fin_var", [P, K])
        factor = sb(ctx, "fin_factor", [P, 2, K])
        spread = sb(ctx, "fin_spread", [P, 2, K, P])
        scale = sb(ctx, "fin_scale", [P, D])
        scale1 = sb(ctx, "fin_scale1", [P, D])
        shift_hi = sb(ctx, "fin_shift_hi", [P, D], F32R)
        shift_lo = sb(ctx, "fin_shift_lo", [P, D], F32R)
        ident_r = sb(ctx, "fin_ident", [P, P], F32R)
        x1 = sb(ctx, "fin_x1", [P, R, D])
        ms = sb(ctx, "fin_msg", [P, R, D])
        y = sb(ctx, "fin_y", [P, RY, D])
        stats = sb(ctx, "fin_stats", [P, 2, 6])
        mv = sb(ctx, "fin_mv", [P, 2, 4])
        root = sb(ctx, "fin_root", [P, 2, 1])
        ps = g.banks(ctx, "psf")
        ps_y = ps[4:8]

        const_in = g.const_in
        idx_ok, sums_ok, tot_ok, var_ok, std_ok, spread_ok, wide_ok, coef_ok = (sem(n) for n in (
            "fin_idx_ok", "fin_sums", "fin_totals", "fin_var_ok", "fin_std", "fin_spread_ok", "fin_wide", "fin_coef"))
        x_in, m_in = g.node_in, g.sum_in + g.ea_in
        x_before = [landed(NT - 1 - s, 0, 0, R) for s in range(R)]
        m_before = [landed(NT - 1 - s, 0, 0, 4) for s in range(4)] + [landed(ET - 1 - s, 0, 0, 4) for s in range(4)]
        xs_pool, xs_dve, m_ok, sum_ok, stat_ok, root_ok, scale_ok, norm_ok = (sem(n) for n in (
            "fin_x_scaled_pool", "fin_x_scaled_dve", "fin_m_scaled", "fin_y_summed", "fin_stat", "fin_root_ok", "fin_scale_ok", "fin_norm"))
        y_out = [sem(f"fin_out{s}") for s in range(RY)]
        mine = g.step_v

        with nc.Block() as block:

            @block.sync
            def _(sp):
                for i in range(3):
                    sp.dma_start(consts[:, i, :], g.rows[3 + i:4 + i, :].rearrange("a (k p) -> p (a k)", p=P), allow_slow_non_contiguous=True).then_inc(const_in, 16)

                def step(j, s, on):
                    if on(0):
                        wait(sp, sum_ok, j - R + 1)
                        sp.dma_start(x1[:, s, :], g.x1_table[bass.ds(j * P, P), :]).then_inc(x_in[s], 16)
                    if on(5):
                        q = (s - 5) % RY
                        sp.wait_ge(norm_ok, j - 4)
                        r = LAST if isinstance(j, int) and j - 5 == NT - 1 else P
                        sp.dma_start(g.out[bass.ds((j - 5) * P, r), :], y[0:r, q, :]).then_inc(y_out[q], 16)
                sweep(sp, NT, 5, 8, 8, step)
                sp.wait_ge(const_in, 128)
                for s in range(RY):
                    sp.wait_ge(y_out[s], 16 * ((NT - 1 - s) // RY + 1))

            @block.gpsimd
            def _(pool):
                def step(j, s, on):
                    if on(0):
                        wait(pool, sum_ok, j - R + 1)
                        nc.gpsimd.tensor_copy(idx[:, s, :], g.last_edge[:, bass.ds(j, 1)]).then_inc(idx_ok, 1)
                        wait_alone(pool, idx_ok, j + 1, g.passed)
                        nc.gpsimd.indirect_dma_start(out=ms[:, s, :], out_offset=None, in_=g.msg_table,
                                                     in_offset=bass.IndirectOffsetOnAxis(ap=idx[:, s, :], axis=0)).then_inc(m_in[s], 16)
                    if on(3):
                        q = (s - 3) % R
                        if isinstance(j, int) and j == 3:
                            pool.wait_ge(coef_ok, 1)
                        if q % SHARE:
                            pool.wait_ge(x_in[q], x_before[q] + landed(j, s, 3, R))
                            nc.gpsimd.tensor_tensor(x1[:, q, :], x1[:, q, :], scale1[:], ALU.mult).then_inc(xs_pool, SHARE)
                sweep(pool, NT, 3, 8, 8, step)

            @block.tensor
            def _(pe):
                pe.wait_ge(sums_ok, 2)
                for i, acc in enumerate((g.sum_y, g.sum_yy)):
                    for k in range(K):
                        mm = pe.matmul(ps[0][:, i * K + k:i * K + k + 1], acc[:, k * P:(k + 1) * P], g.ones[:, 0:1], start=True, stop=True)
                mm.then_inc(tot_ok, 1)
                for i in range(2):
                    pe.wait_ge(spread_ok, i + 1)
                    pe.matmul(ps[1 + i][:], g.ones[:], spread[:, i, :, :].rearrange("p k n -> p (k n)"), start=True, stop=True).then_inc(wide_ok, 1)
                pe.wait_ge(coef_ok, 2)

                def step(j, s, on):
                    if on(3):
                        q = (s - 3) % R
                        to = ps_y[q % 4][:]
                        wait(pe, norm_ok, j - 6)
                        pe.matmul(to, ident_r[:], shift_hi[:], start=True, stop=False)
                        pe.matmul(to, ident_r[:], shift_lo[:], start=False, stop=False)
                        if q % SHARE:
                            pe.wait_ge(xs_pool, (j - 3) * (SHARE - 1) + q % SHARE)
                        else:
                            pe.wait_ge(xs_dve, j - 3 + SHARE)
                        pe.matmul(to, g.ident[:], x1[:, q, :], start=False, stop=False)
                        pe.wait_ge(m_ok, j - 2)
                        pe.matmul(to, g.ident[:], ms[:, q, :], start=False, stop=True).then_inc(sum_ok, 1)
                sweep(pe, NT, 3, 8, 8, step)

            @block.scalar
            def _(act):
                act.wait_ge(var_ok, 1)
                nc.scalar.activation(var[:], var[:], ACT.Sqrt, bias=g.eps[:]).then_inc(std_ok, 1)
                act.wait_ge(wide_ok, 1)
                nc.scalar.copy(scale[:], ps[1][:]).then_inc(std_ok, 1)

                def step(j, s, on):
                    if on(4):
                        h = s % 2
                        act.wait_ge(stat_ok, 2 * (j - 4) + 2)
                        nc.scalar.activation(root[:, h, :], mv[:, h, 1:2], ACT.Sqrt, bias=g.eps[:]).then_inc(root_ok, 1)
                    if on(5):
                        h, q = (s - 5) % 2, (s - 5) % RY
                        act.wait_ge(scale_ok, 2 * (j - 5) + 2)
                        wait(act, y_out[q], landed(j, s, 9, RY))
                        nc.scalar.activation(y[:, q, :], ps_y[q][:], ACT.Identity, bias=mv[:, h, 3:4], scale=mv[:, h, 2:3]).then_inc(norm_ok, 1)
                sweep(act, NT, 5, 8, 16, step)

            @block.vector
            def _(dve):
                v = nc.vector
                steps = g.steps

                def then(ins):
                    steps[0] += 1
                    ins.then_inc(mine, 1)
                    dve.wait_ge(mine, steps[0])

                v.tensor_tensor(g.sum_y[:], g.sum_y[:], g.acc_x[:], ALU.add).then_inc(sums_ok, 1)
                v.tensor_tensor(g.sum_yy[:], g.sum_yy[:], g.acc_xx[:], ALU.add).then_inc(sums_ok, 1)
                v.tensor_copy(ident_r[:], g.ident[:])
                dve.wait_ge(const_in, 128)
                dve.wait_ge(tot_ok, 1)
                then(v.tensor_scalar(mean[:], ps[0][:, 0:K], 1.0 / N, None, ALU.mult))
                then(v.tensor_tensor(var[:], mean[:], mean[:], ALU.mult))
                then(v.scalar_tensor_tensor(var[:], ps[0][:, K:2 * K], 1.0 / N, var[:], ALU.mult, ALU.subtract))
                v.tensor_scalar(var[:], var[:], 0.0, None, ALU.max).then_inc(var_ok, 1)
                then(v.tensor_tensor(mean[:], mean[:], consts[:, 0, :], ALU.add))
                then(v.tensor_tensor(mean[:], consts[:, 0, :], mean[:], ALU.subtract))
                dve.wait_ge(std_ok, 1)
                then(v.reciprocal(var[:], var[:]))
                then(v.tensor_tensor(factor[:, 0, :], var[:], consts[:, 1, :], ALU.mult))
                diagonal = g.ident[:].unsqueeze(1).to_broadcast([P, K, P])
                v.tensor_tensor(spread[:, 0, :, :], diagonal, factor[:, 0, :].unsqueeze(2).to_broadcast([P, K, P]), ALU.mult).then_inc(spread_ok, 1)
                then(v.tensor_tensor(mean[:], mean[:], factor[:, 0, :], ALU.mult))
                then(v.tensor_tensor(factor[:, 1, :], mean[:], consts[:, 2, :], ALU.add))
                v.tensor_tensor(spread[:, 1, :, :], diagonal, factor[:, 1, :].unsqueeze(2).to_broadcast([P, K, P]), ALU.mult).then_inc(spread_ok, 1)
                dve.wait_ge(std_ok, 2)
                v.tensor_scalar(scale1[:], scale[:], 1.0, None, ALU.add).then_inc(coef_ok, 1)
                dve.wait_ge(wide_ok, 2)
                then(v.tensor_copy(shift_hi[:], ps[2][:]))
                v.tensor_tensor(shift_lo[:], ps[2][:], shift_hi[:].bitcast(F32), ALU.subtract).then_inc(coef_ok, 1)
                dve.wait_ge(coef_ok, 1)

                def step(j, s, on):
                    if on(3):
                        q = (s - 3) % R
                        dve.wait_ge(m_in[q], m_before[q] + landed(j, s, 3, R))
                        v.tensor_tensor(ms[:, q, :], ms[:, q, :], scale[:], ALU.mult).then_inc(m_ok, 1)
                        if q % SHARE == 0:
                            dve.wait_ge(x_in[q], x_before[q] + landed(j, s, 3, R))
                            v.tensor_tensor(x1[:, q, :], x1[:, q, :], scale1[:], ALU.mult).then_inc(xs_dve, SHARE)
                    if on(4):
                        dve.wait_ge(sum_ok, j - 3)
                        v.bn_stats(stats[:, s % 2, :], ps_y[(s - 4) % 4][:]).then_inc(stat_ok, 1)
                    if on(5):
                        h = (s - 5) % 2
                        dve.wait_ge(root_ok, j - 4)
                        v.reciprocal(mv[:, h, 2:3], root[:, h, :]).then_inc(scale_ok, 1)
                    if on(4):
                        wait(dve, norm_ok, j - 5)
                        wait_alone(dve, stat_ok, 2 * (j - 4) + 1, g.passed)
                        v.bn_aggr(mv[:, s % 2, 0:2], stats[:, s % 2, :]).then_inc(stat_ok, 1)
                    if on(5):
                        dve.wait_ge(scale_ok, 2 * (j - 5) + 1)
                        v.scalar_tensor_tensor(mv[:, h, 3:4], mv[:, h, 0:1], -1.0, mv[:, h, 2:3], ALU.mult, ALU.mult).then_inc(scale_ok, 1)
                sweep(dve, NT, 5, 8, 8, step)


_OUTS = [((N, D), "float32")]


def kernel(**inputs):
    import numpy as np
    import concourse.bacc as bacc
    from concourse.bass_utils import run_bass_kernel_spmd

    a = {k: np.asarray(v) for k, v in inputs.items()}

    def padded(rows, n, fill=0):
        to = np.full((n,) + rows.shape[1:], fill, rows.dtype)
        to[:rows.shape[0]] = rows
        return to

    wr = a["L1_gnn_Wr"].T
    arrays = {
        "x": padded(a["x"], NP),
        "dst_in": padded(a["dst"].reshape(E, 1), EP + P, N),
        "src_in": padded(a["src"].reshape(E, 1), EP + P),
        "eid_in": np.arange(EP + P, dtype=np.int32).reshape(EP + P, 1),
        "ea": padded(a["edge_attr_512"], EP),
        "weights": np.concatenate([wr[2 * D:], a["L0_gnn_W"], wr[:D], wr[D:2 * D], a["L1_gnn_Wq"].T,
                                   a["L1_gnn_Wk"].T, a["L1_gnn_Wv"].T, a["L1_gnn_Wo"].T]),
        "br": a["L1_gnn_br"],
        "bv": a["L1_gnn_bv"],
        "rows": np.stack([a[n] for n in ("L0_gnn_b", "L1_gnn_bq", "L1_gnn_bk", "L1_gnn_bo", "L1_gnn_gamma", "L1_gnn_beta")]),
    }
    arrays = {f"in_{k}": np.ascontiguousarray(v) for k, v in arrays.items()}
    nc = bacc.Bacc("TRN2", target_bir_lowering=False, num_devices=1)
    args = [nc.dram_tensor(k, v.shape, mybir.dt.from_np(v.dtype), kind="ExternalInput").ap() for k, v in arrays.items()]
    out = nc.dram_tensor("out_0_dram", (N, D), F32, kind="ExternalOutput").ap()
    gnn_kernel(nc, *args, out)
    r = run_bass_kernel_spmd(nc, [arrays], core_ids=[0])
    return r.results[0]["out_0_dram"]
```
